# Optimizing a Trainium2 kernel written in Bass

```python
import numpy as np
import jax
import jax.numpy as jnp

def _softmax(x, axis=-1):
    return jax.nn.softmax(x, axis=axis)

def _gelu(x):
    return jax.nn.gelu(x, approximate=True)

def _silu(x):
    return jax.nn.silu(x)

def _sigmoid(x):
    return jax.nn.sigmoid(x)

def _layernorm(x, axis=-1, eps=1e-05):
    m = jnp.mean(x, axis=axis, keepdims=True)
    v = jnp.var(x, axis=axis, keepdims=True)
    return (x - m) / jnp.sqrt(v + eps)

def _scatter_add(tgt, idx, src, axis=0):
    return tgt.at[idx].add(src)

def _segment_sum(src, seg, n):
    return jax.ops.segment_sum(src, seg, n)
kernel_name = 'mk_sandwich_d1_jaxref_r4_570d59'

def setup_inputs(seed: int=0):
    np.random.seed(seed)
    _w = jnp.asarray

    def _L0_attn_setup():
        import jax, jax.numpy as jnp
        import numpy as np
        B, N, DE, H, DH = (2, 256, 256, 16, 64)
        DK = H * DH
        MIN_EXP = -30.0
        EPS = 0.0001
        key = jax.random.key(seed)
        ks = jax.random.split(key, 8)

        def g(i, shape, sc=1.0):
            return jax.random.normal(ks[i], shape, jnp.float32) * sc
        freqs = 10000.0 ** (-np.arange(DH // 2, dtype=np.float64) / (DH // 2))
        omega = jnp.asarray(np.tile(freqs[None, :], (H, 1)), jnp.float32)
        return {'x': g(0, (B, N, DE)), 'Wq': g(1, (DE, 2 * DK), 1.0 / np.sqrt(DE)), 'Wk': g(2, (DE, 2 * DK), 1.0 / np.sqrt(DE)), 'Wv': g(3, (DE, 2 * DK), 1.0 / np.sqrt(DE)), 'Wo': g(4, (2 * DK, DE), 1.0 / np.sqrt(2 * DK)), 'omega': omega, 'mu_raw': g(5, (H,)) - 2.0, 'sigma_raw': g(6, (H,)), 'eta_raw': jnp.ones((H,), jnp.float32), 'gamma_raw': jnp.ones((H,), jnp.float32), 'tau': jnp.ones((H,), jnp.float32), 'nu_raw': jnp.ones((H,), jnp.float32) * 4.0}
    _L0_attn_in = _L0_attn_setup()

    def _L0_ffn_setup():
        import jax, jax.numpy as jnp
        import numpy as np
        DIM = 256
        HIDDEN = 768
        SCALE = 1.0 / 127.0

        def _dequant(w_int, dtype):
            return w_int.astype(dtype) * jnp.asarray(SCALE, dtype)
        key = jax.random.key(seed)
        k_x, k_g, k_u, k_d = jax.random.split(key, 4)
        x = jax.random.normal(k_x, (4, 512, DIM), dtype=jnp.float32)
        w_gate = jax.random.randint(k_g, (HIDDEN, DIM), -127, 128, dtype=jnp.int32)
        w_up = jax.random.randint(k_u, (HIDDEN, DIM), -127, 128, dtype=jnp.int32)
        w_down = jax.random.randint(k_d, (DIM, HIDDEN), -127, 128, dtype=jnp.int32)
        return {'x': x, 'w_gate': w_gate, 'w_up': w_up, 'w_down': w_down}
    _L0_ffn_in = _L0_ffn_setup()
    _d = {'L0_attn_x': _L0_attn_in['x'], 'L0_attn_Wq': _L0_attn_in['Wq'], 'L0_attn_Wk': _L0_attn_in['Wk'], 'L0_attn_Wv': _L0_attn_in['Wv'], 'L0_attn_Wo': _L0_attn_in['Wo'], 'L0_attn_omega': _L0_attn_in['omega'], 'L0_attn_mu_raw': _L0_attn_in['mu_raw'], 'L0_attn_sigma_raw': _L0_attn_in['sigma_raw'], 'L0_attn_eta_raw': _L0_attn_in['eta_raw'], 'L0_attn_gamma_raw': _L0_attn_in['gamma_raw'], 'L0_attn_tau': _L0_attn_in['tau'], 'L0_attn_nu_raw': _L0_attn_in['nu_raw'], 'L0_ffn_w_gate': _L0_ffn_in['w_gate'], 'L0_ffn_w_up': _L0_ffn_in['w_up'], 'L0_ffn_w_down': _L0_ffn_in['w_down']}
    _x0 = _d['L0_attn_x']
    _d['L0_attn_x'] = jax.random.normal(jax.random.fold_in(jax.random.key(seed), 1), (8, 512, 256), dtype=_x0.dtype)
    del _x0
    return _d

def reference(L0_attn_x, L0_attn_Wq, L0_attn_Wk, L0_attn_Wv, L0_attn_Wo, L0_attn_omega, L0_attn_mu_raw, L0_attn_sigma_raw, L0_attn_eta_raw, L0_attn_gamma_raw, L0_attn_tau, L0_attn_nu_raw, L0_ffn_w_gate, L0_ffn_w_up, L0_ffn_w_down):

    def _L0_attn_ref(x, Wq, Wk, Wv, Wo, omega, mu_raw, sigma_raw, eta_raw, gamma_raw, tau, nu_raw):
        import jax, jax.numpy as jnp
        import numpy as np
        B, N, DE, H, DH = (2, 256, 256, 16, 64)
        DK = H * DH
        MIN_EXP = -30.0
        EPS = 0.0001
        B_, N_, _ = x.shape
        H_, d_half = omega.shape
        DH_ = 2 * d_half
        DKt = H_ * DH_

        def cproj(W):
            z = x @ W
            D = W.shape[1] // 2
            zc = jax.lax.complex(z[..., :D], z[..., D:])
            return zc.reshape(B_, N_, H_, DH_)
        q, k, v = (cproj(Wq), cproj(Wk), cproj(Wv))
        om = jnp.concatenate([omega, -omega], axis=-1)
        t = jnp.arange(N_, dtype=jnp.float32)
        ang = t[:, None, None] * om[None]
        phase = jax.lax.complex(jnp.cos(ang), jnp.sin(ang))
        qr = q * phase[None]
        kr = k * phase[None]
        mu = jax.nn.sigmoid(mu_raw) + EPS
        dt = jnp.abs(t[:, None] - t[None, :])
        E = jnp.exp(jnp.clip(-mu[:, None, None] * dt[None], MIN_EXP, 0.0))
        s = jnp.einsum('bihd,bjhd->bhij', qr, jnp.conj(kr)).real
        qn = (q.real ** 2 + q.imag ** 2).sum(-1).transpose(0, 2, 1)
        kn = (k.real ** 2 + k.imag ** 2).sum(-1).transpose(0, 2, 1)
        sigma_sq = jax.nn.softplus(sigma_raw)
        eta_sq = jax.nn.softplus(eta_raw)
        gamma_sq = jax.nn.softplus(gamma_raw)
        V = (sigma_sq / (2.0 * mu))[:, None, None] * (1.0 - E * E) + (eta_sq + gamma_sq)[:, None, None]
        maha = jnp.maximum(qn[..., None] + (E * E)[None] * kn[:, :, None, :] - 2.0 * E[None] * s, 0.0) / V[None]
        nu = jax.nn.softplus(nu_raw)
        coef = (-0.5 * tau * (nu + DH_))[None, :, None, None]
        logits = coef * jnp.log1p(maha / nu[None, :, None, None]) - 0.5 * DH_ * jnp.log(V)[None]
        causal = t[:, None] >= t[None, :]
        logits = jnp.where(causal[None, None], logits, -jnp.inf)
        A = jax.nn.softmax(logits, axis=-1)
        out = jnp.einsum('bhij,bjhd->bihd', A.astype(v.dtype), v)
        y = jnp.concatenate([out.real.reshape(B_, N_, DKt), out.imag.reshape(B_, N_, DKt)], axis=-1)
        return y @ Wo

    def _L0_ffn_ref(x, w_gate, w_up, w_down):
        import jax, jax.numpy as jnp
        import numpy as np
        DIM = 256
        HIDDEN = 768
        SCALE = 1.0 / 127.0

        def _dequant(w_int, dtype):
            return w_int.astype(dtype) * jnp.asarray(SCALE, dtype)
        wg = _dequant(w_gate, x.dtype)
        wu = _dequant(w_up, x.dtype)
        wd = _dequant(w_down, x.dtype)
        gate = jnp.einsum('bsd,hd->bsh', x, wg)
        up = jnp.einsum('bsd,hd->bsh', x, wu)
        h = jax.nn.silu(gate) * up
        return jnp.einsum('bsh,dh->bsd', h, wd)
    x = L0_attn_x
    x = x + _layernorm(_L0_attn_ref(_layernorm(x, axis=-1), L0_attn_Wq, L0_attn_Wk, L0_attn_Wv, L0_attn_Wo, L0_attn_omega, L0_attn_mu_raw, L0_attn_sigma_raw, L0_attn_eta_raw, L0_attn_gamma_raw, L0_attn_tau, L0_attn_nu_raw), axis=-1)
    x = x + _layernorm(_L0_ffn_ref(_layernorm(x, axis=-1), L0_ffn_w_gate, L0_ffn_w_up, L0_ffn_w_down), axis=-1)
    return x

_drawn_inputs = setup_inputs


def setup_inputs(seed=0):
    import zlib

    import numpy as np

    out = dict(_drawn_inputs(seed))
    spreads = {'L0_attn_eta_raw': (1.0, 0.2),
     'L0_attn_gamma_raw': (1.0, 0.2),
     'L0_attn_tau': (1.0, 0.2),
     'L0_attn_nu_raw': (4.0, 0.2)}
    factors = {}
    for name, (base, spread) in spreads.items():
        noise = np.random.default_rng([zlib.crc32(name.encode()), seed]).standard_normal(out[name].shape)
        drawn = base * np.exp(spread * noise) if base else spread * noise
        out[name] = jnp.asarray(drawn.astype(out[name].dtype))
    for name, factor in factors.items():
        out[name] = (out[name] * factor).astype(out[name].dtype)
    return out
```

```python
import math
from contextlib import ExitStack

import numpy as np
import concourse.bass as bass
from concourse import mybir

F32 = mybir.dt.float32
F32R = mybir.dt.float32r
I32 = mybir.dt.int32
ALU = mybir.AluOpType
ACT = mybir.ActivationFunctionType

B, N, D = 8, 512, 256
H, DH = 16, 64
DK = H * DH
HID = 768
P = 128
KT = D // P
NT = N // P
HH = 2
G = H // HH
FT = HID // P
W2 = HH * 2 * DH
EPS_LN = 1e-5
EPS_MU = 1e-4
MIN_EXP = -30.0
BIG = 1e18
SCALE = 1.0 / 127.0
MAGIC = 1.5 * 2.0 ** 23
VEC = N + P
E_T, VN_T, T3_T = range(3)
V_EXP, V_LN, V_TABLES = 17, 22, 30
V_ANGLE = [V_TABLES + 10 * k + 7 for k in range(4)]
V_ROPE = [V_TABLES + 10 * k + 10 for k in range(4)]
NCO = 22
TILES = tuple(range(NT - 1, -1, -1))
POOL_SCALES = (0,)


def build(nc, x_d, wq_d, wk_d, wv_d, wo_d, omega_d, raw_d, tau_d, wg_d, wu_d, wd_d, out_d):
    ctx = ExitStack()
    with ctx:
        def sb(name, shape, dt=F32):
            return ctx.enter_context(nc.sbuf_tensor(name, shape, dt))

        def sem(name):
            return ctx.enter_context(nc.semaphore(name))

        def scratch(name, shape):
            return nc.dram_tensor(name, shape, F32, kind="Internal").ap()

        xs_d = scratch("xs_d", (B, P, KT * 2 * N))
        ws_d = scratch("ws_d", (G, P, 3 * KT * 2 * W2))
        wos_d = scratch("wos_d", (G, P, HH * 2 * D))
        vec_d = scratch("vec_d", (3, H, VEC))
        tab_d = scratch("tab_d", (G, P, HH, 3, N))
        rope_d = scratch("rope_d", (G, P, HH, 2, N))
        nco_d = scratch("nco_d", (1, H))

        acc = sb("acc", [P, B, NT, D])
        tabs = [sb(f"tabs{i}", [P, 5 * HH, N]) for i in range(2)]
        wt = sb("wt", [P, 2, 3 * KT * 2 * W2], F32R)
        wot = sb("wot", [P, 2, HH * 2 * D], F32R)
        xt = [sb(f"xt{i}", [P, KT, 2, N], F32R) for i in range(2)]
        qkb = sb("qkb", [P, 3 * HH, N])
        sq = sb("sq", [P, 2, N])
        swt = sb("swt", [P, 4, N])
        ek = sb("ek", [P, 2, N])
        t1 = sb("t1", [P, 2, N])
        lg = sb("lg", [P, 2, N])
        pr = sb("pr", [P, 2, N])
        pt = sb("pt", [P, 2, N])
        vt = sb("vt", [P, NT, HH * P])
        ysb = sb("ysb", [P, NT, P])
        yhl = sb("yhl", [P, HH, 2, N], F32R)
        wgt = sb("wgt", [P, KT, HID], F32R)
        wut = sb("wut", [P, KT, HID], F32R)
        wdt = sb("wdt", [P, FT, D], F32R)
        ident = sb("ident", [P, P])
        ones = sb("ones", [P, P])
        qn = sb("qn", [P, HH, 2, NT])
        nmax = sb("nmax", [P, 2 * NT])
        den = sb("den", [P, 2 * NT])
        rden = sb("rden", [P, 2 * NT])
        nco = sb("nco", [P, H])
        ncog = sb("ncog", [P, 2, HH])
        hp = sb("hp", [H, 40])
        om = sb("om", [P, 4])
        stats = sb("stats", [P, NT, 6])
        mv = sb("mv", [P, NT, 2])
        rstd = sb("rstd", [P, NT])
        mhalf = sb("mhalf", [P, NT])

        accf = acc[:, :, :, :].rearrange("p b j n -> p (b j n)")
        dist, v_e, v_vn, v_t3, v_v, v_lnv = [accf[0:H, k * VEC:(k + 1) * VEC] for k in range(6)]
        tokens, ang, turns, half_sin = lg[:, 1, :], sq[:, 0, :], sq[:, 1, :], ysb[:, :, :].rearrange("p j n -> p (j n)")
        rope_sn = [accf[:, 4096 + k * N:4096 + (k + 1) * N] for k in range(4)]
        rope_sp = [accf[:, 6144 + k * N:6144 + (k + 1) * N] for k in range(4)]
        rope_cs = [pr[:, 0, :], pr[:, 1, :], pt[:, 0, :], pt[:, 1, :]]
        xraw = [z[:, :, :].rearrange("p a n -> p (a n)").rearrange("p (j n) -> p j n", j=NT) for z in (ek, vt)]
        xnorm = [z[:, :, :].rearrange("p a n -> p (a n)").rearrange("p (j n) -> p j n", j=NT) for z in (t1, lg)]

        def seq(s, k):
            return tabs[s][:, k:k + 2, :].rearrange("p a n -> p (a n)").rearrange("p (j n) -> p j n", j=NT)
        f_xin = [seq(0, 0), seq(1, 0)]
        f_outs = [seq(0, 2), seq(1, 2)]
        f_nrm = seq(0, 4)
        f_tmp = seq(1, 6)
        f_y = seq(1, 4)

        def f_gate(r):
            return tabs[0][:, 6 + r % 2, :]

        def f_hid(r):
            return tabs[0][:, 8 + r % 2, :]

        def hpart(r, a):
            o = (r * 2 + a) * N
            return wt[:, :, :].rearrange("p a n -> p (a n)")[:, o:o + N]

        def bank(name):
            return ctx.enter_context(nc.psum_tensor(name, [P, N], F32))
        pa = [bank("pa0"), bank("pa1")]
        ps = [bank("ps0"), bank("ps1")]
        pp = [bank("pp0"), bank("pp1")]
        py = bank("py")
        po = bank("po")

        consts = sem("consts")
        p_load = sem("p_load")
        p_dve = sem("p_dve")
        p_act = sem("p_act")
        vec_out = sem("vec_out")
        tab_out = sem("tab_out")
        rope_out = sem("rope_out")
        nco_in = sem("nco_in")
        raww = [sem(f"raww{i}") for i in range(2)]
        split_hi = sem("split_hi")
        split_lo = sem("split_lo")
        split_out = [sem(f"split_out{i}") for i in range(2)]
        ffn_in = sem("ffn_in")
        ffn_cast = sem("ffn_cast")
        ffn_tr = sem("ffn_tr")
        ffn_ev = sem("ffn_ev")
        x_in = [sem(f"x_in{i}") for i in range(2)]
        x_ln = sem("x_ln")
        x_root = sem("x_root")
        x_norm = sem("x_norm")
        x_tr = sem("x_tr")
        x_hi = sem("x_hi")
        x_lo = sem("x_lo")
        x_out = [sem(f"x_out{i}") for i in range(2)]

        grp = [sem(f"grp{i}") for i in range(2)]
        xt_in = sem("xt_in")
        proj = sem("proj")
        s_rdy = sem("s_rdy")
        tr_rdy = sem("tr_rdy")
        av_rdy = sem("av_rdy")
        yt_rdy = sem("yt_rdy")
        o_rdy = sem("o_rdy")
        pa_act = sem("pa_act")
        ln_act = sem("ln_act")
        ex_act = sem("ex_act")
        pt_act = sem("pt_act")
        yh_act = sem("yh_act")
        pa_dve = sem("pa_dve")
        rope = sem("rope")
        a_dve = sem("a_dve")
        b_dve = sem("b_dve")
        b_pool = sem("b_pool")
        cd_dve = sem("cd_dve")
        f_dve = sem("f_dve")
        rd_dve = sem("rd_dve")
        y_dve = sem("y_dve")
        yl_dve = sem("yl_dve")
        acc_dve = sem("acc_dve")
        ek_pool = sem("ek_pool")
        t2_pool = sem("t2_pool")

        NPB = len(POOL_SCALES)

        f_x = [sem(f"f_x{i}") for i in range(2)]
        f_ln = sem("f_ln")
        f_root = sem("f_root")
        f_rootb = sem("f_rootb")
        f_norm = sem("f_norm")
        f_tr = sem("f_tr")
        f_hi = sem("f_hi")
        f_lo = sem("f_lo")
        f_g = sem("f_g")
        f_u = sem("f_u")
        f_silu = sem("f_silu")
        f_h = sem("f_h")
        f_hh = sem("f_hh")
        f_hl = sem("f_hl")
        f_dn = sem("f_dn")
        f_ev = sem("f_ev")
        f_res = sem("f_res")
        f_l3 = sem("f_l3")
        f_out = [sem(f"f_out{i}") for i in range(2)]
        settled = sem("settled")
        ncog_dve = sem("ncog_dve")

        block = ctx.enter_context(nc.Block())

        def counts(eng, t, pers):
            if isinstance(t, int):
                return {p: (t + 1) * p for p in pers}
            t = eng.snap(t + 1)
            return {p: eng.snap(t * p) if p > 1 else t for p in pers}

        def credit(eng, *pairs):
            for s, n in pairs:
                if n:
                    eng.sem_inc(s, n)

        def run_groups(eng, group):
            with eng.Fori(0, G // 2 - 1) as gg:
                group(gg, 0, False)
                group(gg, 1, False)
            group(G // 2 - 1, 0, False)
            group(G // 2 - 1, 1, True)

        def iterations(eng, gg, par, last, half0, half1, start=None):
            if start:
                start(gg, par)
            with eng.Fori(0, B - 1) as b:
                t = eng.snap(gg * 2 * B + par * B + b) if not isinstance(gg, int) else eng.snap(b + (gg * 2 * B + par * B))
                half0(t, b, par)
                half1(t, b, par, par, None)
            t = gg * 2 * B + par * B + B - 1
            if not isinstance(t, int):
                t = eng.snap(t)
            half0(t, B - 1, par)
            half1(t, B - 1, par, None if last else 1 - par, gg + par)

        def tab(par, hh, k, lo=0, hi=N):
            return tabs[par][:, hh * 3 + k, lo:hi]

        def ropet(par, hh, k):
            return tabs[par][:, 3 * HH + hh * 2 + k, :]

        def wproj(par, m, kt, part, lo, hi):
            o = ((m * KT + kt) * 2 + part) * W2
            return wt[:, par, o + lo:o + hi]

        def width(n):
            return (TILES[n] + 1) * P

        PARTS = ((0, 0), (0, 1), (1, 0))

        def split_views(m, s):
            stage = wt[:, (4 * m + s) % 2, 0:2048]
            raw = tabs[m % 2][:, 0:8, :].rearrange("p a n -> p (a n)")
            if m < 3:
                kt, gh = s // 2, s % 2
                out = stage.rearrange("p (g a h c d) -> p a c g h d", g=4, a=2, h=HH, c=2)
                for c in range(2):
                    o = kt * 2 * DK + c * DK + gh * DK // 2
                    yield out[:, 0, c], out[:, 1, c], raw[:, o:o + DK // 2].rearrange("p (g h d) -> p g h d", g=4, h=HH)
            else:
                out = stage.rearrange("p (h a n) -> p a h n", h=2 * HH, a=2)
                yield out[:, 0], out[:, 1], raw[:, s * 1024:(s + 1) * 1024].rearrange("p (h n) -> p h n", h=2 * HH)

        def ffn_jobs():
            jobs = []
            for raw, dst in ((qkb[:, 0:3, :], wgt), (qkb[:, 3:6, :], wut)):
                r6 = raw.rearrange("p a n -> p (a n)").rearrange("p (r n) -> p r n", r=FT)
                for kt in range(KT):
                    for r in range(FT):
                        o = kt * HID + r * P
                        jobs.append((r6[:, r, kt * P:(kt + 1) * P],
                                     dst[:, :, :].rearrange("p k n -> p (k n)")[:, o:min(o + 4 * P, KT * HID)]))
            w2 = swt[:, 0:3, :].rearrange("p a n -> p (a n)").rearrange("p (r n) -> p r n", r=KT)
            for r in range(FT):
                for d in range(KT):
                    o = r * D + d * P
                    jobs.append((w2[:, d, r * P:(r + 1) * P], wdt[:, :, :].rearrange("p r n -> p (r n)")[:, o:min(o + 4 * P, FT * D)]))
            return jobs

        @block.sync
        def _(sp):
            credit(sp, (x_out[0], 16), (x_out[1], 16), (f_out[0], 16), (f_out[1], 16))
            for k in range(5):
                sp.dma_start(hp[:, k:k + 1], raw_d[k].rearrange("(h a) -> h a", a=1)).then_inc(p_load, 16)
            sp.dma_start(hp[:, 5:6], tau_d.rearrange("(h a) -> h a", a=1)).then_inc(p_load, 16)
            for k in range(4):
                sp.dma_start(om[:, k:k + 1], omega_d[4 * k:4 * k + 4, :].rearrange("a (d e) -> (a d) e", e=1)).then_inc(p_load, 16)
            for s in range(2):
                sp.dma_start(xraw[s], x_d[s].rearrange("(j p) n -> p j n", p=P)).then_inc(x_in[s], 16)
            raws = [wq_d.rearrange("(k p) n -> p k n", p=P), wk_d.rearrange("(k p) n -> p k n", p=P),
                    wv_d.rearrange("(k p) n -> p k n", p=P), None]

            def load_raw(m):
                dst = tabs[m % 2][:, 0:8, :].rearrange("p a n -> p (a n)")
                if m < 3:
                    sp.dma_start(dst.rearrange("p (k n) -> p k n", k=KT), raws[m]).then_inc(raww[m % 2], 16)
                else:
                    for c in range(2):
                        sp.dma_start(dst[c * DH:(c + 1) * DH, :].rearrange("p (h n) -> p h n", h=H),
                                     wo_d[c * DK:(c + 1) * DK, :].rearrange("(h d) n -> d h n", d=DH)
                                     ).then_inc(raww[1], 16)
            load_raw(0)
            load_raw(1)
            sp.dma_start(qkb[:, 0:3, :].rearrange("p a n -> p (a n)").bitcast(I32).rearrange("p (r n) -> p r n", r=FT),
                         wg_d.rearrange("(r p) n -> p r n", p=P)).then_inc(ffn_in, 16)
            sp.dma_start(qkb[:, 3:6, :].rearrange("p a n -> p (a n)").bitcast(I32).rearrange("p (r n) -> p r n", r=FT),
                         wu_d.rearrange("(r p) n -> p r n", p=P)).then_inc(ffn_in, 16)
            sp.dma_start(swt[:, 0:3, :].rearrange("p a n -> p (a n)").bitcast(I32).rearrange("p (r n) -> p r n", r=KT),
                         wd_d.rearrange("(r p) n -> p r n", p=P)).then_inc(ffn_in, 16)
            sp.wait_ge(p_dve, V_TABLES)
            for k in range(3):
                sp.dma_start(vec_d[k], (v_e, v_vn, v_t3)[k]).then_inc(vec_out, 16)
            sp.dma_start(nco_d.rearrange("a h -> h a"), hp[:, NCO:NCO + 1]).then_inc(vec_out, 16)
            sp.wait_ge(vec_out, 64)
            sp.dma_start(nco[:, :], bass.AP(tensor=nco_d.tensor, offset=0, ap=[[0, P], [1, H]])).then_inc(nco_in, 16)
            for g in range(G):
                for k in range(3):
                    src = bass.AP(tensor=vec_d.tensor, offset=(k * H + g * HH) * VEC + P - 1,
                                  ap=[[VEC, HH], [-1, P], [1, N]])
                    sp.dma_start(tab_d[g, :, :, k, :].rearrange("p h n -> h p n"), src).then_inc(tab_out, 16)
            for k in range(4):
                sp.wait_ge(p_dve, V_ROPE[k])
                for row in range(4):
                    h0 = 4 * k
                    for c, src in ((0, rope_cs[k]), (1, rope_sp[k] if row in (1, 2) else rope_sn[k])):
                        for a in range(2):
                            dst = rope_d[(h0 + 2 * a) // HH, row * 32:(row + 1) * 32, :, c, :]
                            sp.dma_start(dst.rearrange("d h n -> h d n"), src[a * 64:(a + 1) * 64, :]
                                         ).then_inc(rope_out, 16)
            for m in range(4):
                for s in range(4):
                    i = 4 * m + s
                    sp.wait_ge(split_lo, i + 1)
                    sp.wait_ge(split_hi, i + 1)
                    stage = wt[:, i % 2, 0:2048].bitcast(F32)
                    if m < 3:
                        kt, gh = s // 2, s % 2
                        dst = ws_d[4 * gh:4 * gh + 4].rearrange("g p (m r) -> p g m r", m=3 * KT)[:, :, m * KT + kt, :]
                        sp.dma_start(dst, stage.rearrange("p (g r) -> p g r", g=4)).then_inc(split_out[i % 2], 16)
                    else:
                        sp.dma_start(wos_d[2 * s:2 * s + 2].rearrange("g p r -> p g r"),
                                     stage.rearrange("p (g r) -> p g r", g=2)).then_inc(split_out[i % 2], 16)
                if m < 2:
                    load_raw(m + 2)
            def x_load(b, s):
                src = x_d[b].rearrange("(j p) n -> p j n", p=P) if isinstance(b, int) else \
                    x_d[bass.ds(b, 1)].rearrange("b (j p) n -> p (b j) n", p=P)
                sp.dma_start(xraw[s], src).then_inc(x_in[s], 16)

            def x_store(b, s):
                dst = xs_d[b] if isinstance(b, int) else xs_d[bass.ds(b, 1)].rearrange("b p n -> (b p) n")
                sp.dma_start(dst, xt[s][:, :, :, :].rearrange("p k s n -> p (k s n)").bitcast(F32)).then_inc(x_out[s], 16)

            with sp.Fori(0, B // 2 - 1) as i:
                off = [sp.snap(i * 2 + s) for s in range(2)]
                nxt = [sp.snap(i * 2 + s + 2) for s in range(2)]
                nrm = [sp.snap(i * 2 + s + 3) for s in range(2)]
                hlo = [sp.snap(i * 4 + 2 * s + 4) for s in range(2)]
                for s in range(2):
                    sp.wait_ge(x_norm, nrm[s])
                    x_load(nxt[s], s)
                    sp.wait_ge(x_hi, hlo[s])
                    sp.wait_ge(x_lo, hlo[s])
                    x_store(off[s], s)
            for s in range(2):
                sp.wait_ge(x_hi, 2 * (B - 2 + s) + 4)
                sp.wait_ge(x_lo, 2 * (B - 2 + s) + 4)
                x_store(B - 2 + s, s)
            sp.wait_ge(tab_out, 16 * 3 * G)
            sp.wait_ge(rope_out, 16 * 64)
            for s in range(2):
                sp.wait_ge(split_out[s], 16 * 8)
                sp.wait_ge(x_out[s], 16 * (B // 2 + 1))
            sp.wait_ge(ffn_tr, 9)

            def load_group(g, par):
                one = (lambda d: d[g] if isinstance(g, int) else d[bass.ds(g, 1)])
                def flat(d, pat, pat1):
                    return one(d).rearrange(pat if isinstance(g, int) else pat1)
                sp.dma_start(tabs[par][:, 0:3 * HH, :], flat(tab_d, "p h k n -> p (h k) n", "g p h k n -> (g p) (h k) n")).then_inc(grp[par], 16)
                sp.dma_start(tabs[par][:, 3 * HH:5 * HH, :], flat(rope_d, "p h k n -> p (h k) n", "g p h k n -> (g p) (h k) n")).then_inc(grp[par], 16)
                sp.dma_start(wt[:, par, :].bitcast(F32), flat(ws_d, "p r -> p r", "g p r -> (g p) r")).then_inc(grp[par], 16)
                sp.dma_start(wot[:, par, :].bitcast(F32), flat(wos_d, "p r -> p r", "g p r -> (g p) r")).then_inc(grp[par], 16)

            def load_x(b):
                src = xs_d[b] if isinstance(b, int) else xs_d[bass.ds(b, 1)].rearrange("b p n -> (b p) n")
                sp.dma_start(xt[0][:, :, :, :].rearrange("p k s n -> p (k s n)").bitcast(F32), src).then_inc(xt_in, 16)

            load_group(0, 0)
            load_x(0)
            load_group(1, 1)

            def sequences(t0, last):
                with sp.Fori(0, B - 1) as b:
                    nb = sp.snap(b + 1)
                    v = sp.snap((b + (t0 + 1)) * 10 + 8)
                    sp.wait_ge(proj, v)
                    load_x(nb)
                if not last:
                    v = (t0 + B) * 10 + 8
                    sp.wait_ge(proj, v if isinstance(v, int) else sp.snap(v))
                    load_x(0)

            def refill(g, par, t0):
                t = t0 * 1
                v8 = (t + 0) * 8 + 8
                v2 = (t + 0) * 2 + 2
                vb = (t + 0) * 2 * NPB + 2 * NPB
                if not isinstance(t0, int):
                    v8, v2 = sp.snap(v8), sp.snap(v2)
                    vb = sp.snap(vb) if NPB else 0
                sp.wait_ge(f_dve, v8)
                sp.wait_ge(ek_pool, v8)
                if NPB:
                    sp.wait_ge(b_pool, vb)
                sp.wait_ge(o_rdy, v2)
                load_group(g, par)

            sequences(0, False)
            with sp.Fori(0, G // 2 - 1) as gg:
                g2 = sp.snap(gg * 2 + 2)
                g3 = sp.snap(gg * 2 + 3)
                ta = sp.snap(gg * (2 * B) + B)
                tb = sp.snap(gg * (2 * B) + 2 * B)
                refill(g2, 0, ta)
                sequences(ta, False)
                refill(g3, 1, tb)
                sequences(tb, False)
            sequences((G - 1) * B, True)

            def f_load(b, s):
                src = x_d[b].rearrange("(j p) n -> p j n", p=P) if isinstance(b, int) else \
                    x_d[bass.ds(b, 1)].rearrange("b (j p) n -> p (b j) n", p=P)
                sp.dma_start(f_xin[s], src).then_inc(f_x[s], 16)

            def f_store(b, s):
                dst = out_d[b].rearrange("(j p) n -> p j n", p=P) if isinstance(b, int) else \
                    out_d[bass.ds(b, 1)].rearrange("b (j p) n -> p (b j) n", p=P)
                sp.dma_start(dst, f_outs[s]).then_inc(f_out[s], 16)

            sp.wait_ge(f_dve, 8 * B * G + 8)
            sp.wait_ge(ek_pool, 8 * B * G + 8)
            f_load(0, 0)
            f_load(1, 1)
            with sp.Fori(0, B // 2 - 1) as i:
                off = [sp.snap(i * 2 + s) for s in range(2)]
                nxt = [sp.snap(i * 2 + s + 2) for s in range(2)]
                cnt = [sp.snap(i * 2 + s + 3) for s in range(2)]
                for s in range(2):
                    sp.wait_ge(f_norm, cnt[s])
                    f_load(nxt[s], s)
                    sp.wait_ge(f_res, cnt[s])
                    f_store(off[s], s)
            for s in range(2):
                sp.wait_ge(f_res, B - 2 + s + 3)
                f_store(B - 2 + s, s)
            for s in range(2):
                sp.wait_ge(f_out[s], 16 * (B // 2 + 1))

        @block.gpsimd
        def _(pool):
            credit(pool, (ek_pool, 8), (b_pool, 2 * NPB), (t2_pool, 4))
            pool.memset(ident[:, :], 0.0).then_inc(consts, 1)
            pool.memset(ones[:, :], 1.0).then_inc(consts, 1)
            pool.memset(mhalf[:, :], -0.5).then_inc(consts, 1)
            pool.iota(dist, pattern=[[-1, VEC]], base=N - 1, channel_multiplier=0,
                      allow_small_or_imprecise_dtypes=True).then_inc(consts, 1)
            pool.iota(tokens, pattern=[[1, N]], base=0, channel_multiplier=0,
                      allow_small_or_imprecise_dtypes=True).then_inc(consts, 1)
            pool.wait_ge(consts, 5)
            pool.affine_select(out=ident[:, :], in_=ident[:, :], compare_op=ALU.not_equal, fill=1.0,
                               base=0, pattern=[[-1, P]], channel_multiplier=1).then_inc(consts, 1)


            def root(chain, v, mark):
                pool.wait_ge(chain, v)
                pool.tensor_tensor(rstd[:, :], rstd[:, :], mhalf[:, :], ALU.pow).then_inc(mark, 1)

            credit(pool, (x_root, 1), (f_root, 2), (f_rootb, 1))
            with pool.Fori(0, B) as b:
                root(x_ln, pool.snap(b * 3 + 3 + 3), x_root)

            pool.wait_ge(vec_out, 64)
            pool.wait_ge(rope_out, 16 * 64)
            pool.memset(accf, 0.0).then_inc(consts, 1)

            def rope_sin(t, c, hh, par):
                for m in range(2):
                    pool.wait_ge(pa_act, c[8] + (0, 5)[hh] + m + 1)
                    pool.wait_ge(rope, c[4] + 2 * hh + m + 1 - 2)
                    pool.tensor_tensor(swt[:, 2 + m, :], swt[:, m, :], ropet(par, hh, 1), ALU.mult).then_inc(t2_pool, 1)

            def decay_norm(c, hh, n, par):
                i, m = n % 2, 4 * hh + n
                w = width(n)
                if n == 0:
                    pool.wait_ge(pa_act, c[8] + (3, 8)[hh])
                pool.wait_ge(a_dve, c[8] + m + 1 - 2)
                pool.tensor_tensor(ek[:, i, 0:w], tab(par, hh, E_T, N - w), qkb[:, 3 * hh + 2, 0:w],
                                   ALU.mult).then_inc(ek_pool, 1)

            def times_decay(c, hh, n, par):
                i, m = n % 2, 4 * hh + n
                w = width(n)
                pool.wait_ge(a_dve, c[8] + m + 1)
                pool.tensor_tensor(t1[:, i, 0:w], t1[:, i, 0:w], tab(par, hh, E_T, N - w), ALU.mult).then_inc(b_pool, 1)

            def unit(t, hh, par, nxt):
                c = counts(pool, t, (8, 4))
                decay_norm(c, hh, 0, par)
                decay_norm(c, hh, 1, par)
                for n in POOL_SCALES:
                    times_decay(c, hh, n, par)
                if nxt is not None:
                    nt, nh, npar = nxt
                    rope_sin(nt, c if nh else {p: v + p for p, v in c.items()}, nh, npar)
                decay_norm(c, hh, 2, par)
                decay_norm(c, hh, 3, par)

            def half0(t, b, par):
                unit(t, 0, par, (t, 1, par))

            def half1(t, b, par, npar, ng):
                nt = t + 1
                if npar is not None and ng is not None:
                    pool.wait_ge(grp[npar], (ng + 1) * 64 if isinstance(ng, int) else pool.snap((ng + 1) * 64))
                unit(t, 1, par, None if npar is None else (nt, 0, npar))

            pool.wait_ge(grp[0], 64)
            rope_sin(0, counts(pool, 0, (8, 4)), 0, 0)
            run_groups(pool, lambda gg, par, last: iterations(pool, gg, par, last, half0, half1))

            credit(pool, (f_hl, FT))

            def hidden_low(c, r):
                pool.wait_ge(f_hh, c[FT] + r + 1)
                if r == 0:
                    pool.wait_ge(f_dn, c[2])
                pool.tensor_tensor(hpart(r, 1), f_hid(r), hpart(r, 0).bitcast(F32), ALU.subtract).then_inc(f_hl, 1)

            def f_body(b, nxt):
                c = counts(pool, b, (FT, 8, 4, 2))
                hidden_low(c, 0)
                if nxt:
                    root(f_ln, c[8] + 8 + 3, f_root)
                hidden_low(c, 1)
                if nxt:
                    root(f_ln, c[8] + 8 + 8, f_root)
                for r in range(2, FT):
                    hidden_low(c, r)
                root(f_l3, c[4] + 3, f_rootb)

            root(f_ln, 8 + 3, f_root)
            root(f_ln, 8 + 8, f_root)
            with pool.Fori(0, B - 1) as b:
                f_body(b, True)
            f_body(B - 1, False)

        @block.tensor
        def _(pe):
            credit(pe, (proj, 10), (s_rdy, 8), (tr_rdy, 8), (av_rdy, 8), (yt_rdy, 2), (o_rdy, 2), (x_tr, 2))
            mm = pe.matmul
            pe.wait_ge(consts, 6)
            jobs = ffn_jobs()
            pe.wait_ge(ffn_cast, 3)
            for n in range(9):
                if n >= 2:
                    pe.wait_ge(ffn_ev, n - 1)
                for k, (src, _) in enumerate(jobs[4 * n:4 * n + 4]):
                    last = pe.transpose(ps[n % 2][:, k * P:(k + 1) * P], src, ident[:, :])
                last.then_inc(ffn_tr, 1)

            with pe.Fori(0, B // 2) as i:
                for s in range(2):
                    nrm = pe.snap(i * 2 + s + 3)
                    c = pe.snap(i * 4 + 2 * s + 2)
                    pe.wait_ge(x_norm, nrm)
                    for kt in range(KT):
                        pe.wait_ge(x_hi, c + kt + 1 - 2)
                        pe.wait_ge(x_lo, c + kt + 1 - 2)
                        for j in range(NT):
                            last = pe.transpose(pp[kt][:, j * P:(j + 1) * P], xnorm[s][:, j, kt * P:(kt + 1) * P],
                                                ident[:, :])
                        last.then_inc(x_tr, 1)

            def project(t, c, hh, par, m):
                use = (1, 7)[hh] + m
                if hh == 0 and m == 0:
                    v = (t + 1) * 16
                    pe.wait_ge(xt_in, v if isinstance(v, int) else pe.snap(v))
                if hh == 0:
                    if m == 0:
                        pe.wait_ge(pa_act, c[8] + 8 - 8)
                    else:
                        pe.wait_ge(pa_dve, c[6] + 6 - 6)
                else:
                    pe.wait_ge(pa_act, c[8] + (4, 5)[m])
                n = 0
                for kt in range(KT):
                    for a, b in PARTS:
                        last = mm(pa[m][:, :], wproj(par, m, kt, a, hh * P, (hh + 1) * P), xt[0][:, kt, b, :],
                                  start=(n == 0), stop=(n == 3 * KT - 1))
                        n += 1
                last.then_inc(proj, 1)

            def norm_k(c, hh):
                pe.wait_ge(pa_act, c[8] + (2, 7)[hh])
                pe.wait_ge(pa_dve, c[6] + (1, 4)[hh])
                mm(pa[0][:, :], ones[:, :], sq[:, 1, :], start=True, stop=True).then_inc(proj, 1)

            def norm_q(c, hh):
                pe.wait_ge(pa_dve, c[6] + (2, 5)[hh])
                for i in range(NT):
                    last = mm(pa[1][:, i:i + 1], sq[:, 0, i * P:(i + 1) * P], ones[:, 0:1], start=True, stop=True)
                last.then_inc(proj, 1)

            def values(c, par):
                for half in range(2):
                    if half == 0:
                        pe.wait_ge(pa_act, c[8] + 3)
                    else:
                        pe.wait_ge(pa_dve, c[6] + 3)
                    for jj in range(2):
                        j = 2 * half + jj
                        n = 0
                        for kt in range(KT):
                            for a, b in PARTS:
                                last = mm(pa[half][:, jj * W2:(jj + 1) * W2], xt[0][:, kt, a, j * P:(j + 1) * P],
                                          wproj(par, 2, kt, b, 0, W2), start=(n == 0), stop=(n == 3 * KT - 1))
                                n += 1
                    last.then_inc(proj, 1)

            def scores(c, hh, n):
                i, m = n % 2, 4 * hh + n
                w = width(n)
                if n == 0:
                    pe.wait_ge(rope, c[4] + 2 * hh + 2)
                pe.wait_ge(a_dve, c[8] + m + 1 - 2)
                mm(ps[i][:, 0:w], qkb[:, 3 * hh, TILES[n] * P:(TILES[n] + 1) * P], qkb[:, 3 * hh + 1, 0:w],
                   start=True, stop=True).then_inc(s_rdy, 1)

            def turn(c, hh, n):
                i, m = n % 2, 4 * hh + n
                pe.wait_ge(ex_act, c[8] + m + 1)
                pe.wait_ge(pt_act, c[8] + m + 1 - 2)
                for j in range(TILES[n] + 1):
                    last = pe.transpose(pp[i][:, j * P:(j + 1) * P], pr[:, i, j * P:(j + 1) * P], ident[:, :])
                last.then_inc(tr_rdy, 1)

            def attend(c, hh, n):
                i, m = n % 2, 4 * hh + n
                I = TILES[n]
                pe.wait_ge(pt_act, c[8] + m + 1)
                if n == 0:
                    pe.wait_ge(pa_act, c[8] + 5)
                    if hh == 0:
                        pe.wait_ge(acc_dve, c[2] + 2 - 2)
                    pe.wait_ge(y_dve, c[2] + hh + 1 - 1)
                for j in range(I + 1):
                    last = mm(py[:, I * P:(I + 1) * P], pt[:, i, j * P:(j + 1) * P], vt[:, j, hh * P:(hh + 1) * P],
                              start=(j == 0), stop=(j == I))
                last.then_inc(av_rdy, 1)

            def turn_y(c, hh):
                pe.wait_ge(y_dve, c[2] + hh + 1)
                if hh == 0:
                    pe.wait_ge(acc_dve, c[2] + 1 - 2)
                else:
                    pe.wait_ge(yl_dve, c[2] + 1)
                for j in range(NT):
                    last = pe.transpose(po[:, j * P:(j + 1) * P], ysb[:, j, :], ident[:, :])
                last.then_inc(yt_rdy, 1)

            def out_project(c, par):
                pe.wait_ge(yl_dve, c[2] + 2)
                for half, dst in enumerate((po, py)):
                    for jj in range(2):
                        j = 2 * half + jj
                        n = 0
                        for hh in range(HH):
                            for a, b in PARTS:
                                last = mm(dst[:, jj * D:(jj + 1) * D], yhl[:, hh, a, j * P:(j + 1) * P],
                                          wot[:, par, (hh * 2 + b) * D:(hh * 2 + b + 1) * D],
                                          start=(n == 0), stop=(n == 3 * HH - 1))
                                n += 1
                    last.then_inc(o_rdy, 1)

            def unit(t, c, hh, nxt):
                scores(c, hh, 0)
                scores(c, hh, 1)
                if nxt:
                    nt, cn, nh, npar = nxt
                    project(nt, cn, nh, npar, 0)
                scores(c, hh, 2)
                if nxt:
                    project(nt, cn, nh, npar, 1)
                scores(c, hh, 3)
                if nxt:
                    norm_k(cn, nh)
                turn(c, hh, 0)
                if nxt:
                    norm_q(cn, nh)
                turn(c, hh, 1)
                attend(c, hh, 0)
                turn(c, hh, 2)
                attend(c, hh, 1)
                turn(c, hh, 3)
                attend(c, hh, 2)
                if nxt and nh == 0:
                    values(cn, npar)
                attend(c, hh, 3)
                turn_y(c, hh)

            PERS = (8, 6, 4, 2)

            def half0(t, b, par):
                c = counts(pe, t, PERS)
                unit(t, c, 0, (t, c, 1, par))

            def half1(t, b, par, npar, ng):
                c = counts(pe, t, PERS)
                if npar is not None and ng is not None:
                    pe.wait_ge(grp[npar], (ng + 1) * 64 if isinstance(ng, int) else pe.snap((ng + 1) * 64))
                nxt = None
                if npar is not None:
                    nxt = (t + 1, {p: v + p for p, v in c.items()}, 0, npar)
                unit(t, c, 1, nxt)
                out_project(c, par)

            pe.wait_ge(grp[0], 64)
            c0 = counts(pe, 0, PERS)
            project(0, c0, 0, 0, 0)
            project(0, c0, 0, 0, 1)
            norm_k(c0, 0)
            norm_q(c0, 0)
            values(c0, 0)
            run_groups(pe, lambda gg, par, last: iterations(pe, gg, par, last, half0, half1))

            credit(pe, (f_tr, 2), (f_g, FT), (f_u, FT), (f_dn, 2))

            def f_transposes(c, s):
                pe.wait_ge(f_norm, c[1] + 2)
                for kt in range(KT):
                    pe.wait_ge(f_hi, c[2] + kt + 1 - 2)
                    pe.wait_ge(f_lo, c[2] + kt + 1 - 2)
                    for j in range(NT):
                        last = pe.transpose(pp[kt][:, j * P:(j + 1) * P], f_nrm[:, j, kt * P:(kt + 1) * P], ident[:, :])
                    last.then_inc(f_tr, 1)

            def gate_up(c, s, r):
                i = r % 2
                if r == 0:
                    pe.wait_ge(f_hi, c[2] + 2)
                    pe.wait_ge(f_lo, c[2] + 2)
                for dst, w, free, done in ((pa, wgt, f_silu, f_g), (ps, wut, f_h, f_u)):
                    pe.wait_ge(free, c[FT] + r + 1 - 2)
                    n = 0
                    for kt in range(KT):
                        for a in range(2):
                            last = mm(dst[i][:, :], w[:, kt, r * P:(r + 1) * P], xt[s][:, kt, a, :],
                                      start=(n == 0), stop=(n == 2 * KT - 1))
                            n += 1
                    last.then_inc(done, 1)

            def down(c):
                for half, dst in enumerate((py, po)):
                    pe.wait_ge(f_ev, c[2] + half + 1 - 2)
                    if half == 0:
                        pe.wait_ge(f_hl, c[FT] + FT)
                    for jj in range(2):
                        j = 2 * half + jj
                        n = 0
                        for r in range(FT):
                            for a in range(2):
                                last = mm(dst[:, jj * D:(jj + 1) * D], hpart(r, a)[:, j * P:(j + 1) * P], wdt[:, r, :],
                                          start=(n == 0), stop=(n == 2 * FT - 1))
                                n += 1
                    last.then_inc(f_dn, 1)

            def f_body(b, s, nxt):
                c = counts(pe, b, (FT, 2, 1))
                for r in range(FT):
                    gate_up(c, s, r)
                if nxt:
                    f_transposes({p: v + p for p, v in c.items()}, 1 - s)
                down(c)

            f_transposes(counts(pe, 0, (FT, 2, 1)), 0)
            with pe.Fori(0, B // 2 - 1) as i:
                f_body(pe.snap(i * 2), 0, True)
                f_body(pe.snap(i * 2 + 1), 1, True)
            f_body(B - 2, 0, True)
            f_body(B - 1, 1, False)

        @block.scalar
        def _(act):
            credit(act, (pa_act, 8), (ln_act, 8), (ex_act, 8), (pt_act, 8), (yh_act, 2), (x_hi, 2))
            n_act = [0]

            def a_step(ins):
                n_act[0] += 1
                ins.then_inc(p_act, 1)
                act.wait_ge(p_act, n_act[0])

            act.wait_ge(p_load, 16 * 10)
            a_step(act.activation(hp[:, 6:11], hp[:, 0:5], ACT.Abs))
            a_step(act.activation(hp[:, 11:16], hp[:, 6:11], ACT.Exp, scale=-1.0))
            a_step(act.activation(hp[:, 16:21], hp[:, 11:16], ACT.Ln, bias=1.0))
            act.wait_ge(p_dve, V_EXP)
            a_step(act.activation(v_e, v_e, ACT.Exp))
            act.wait_ge(p_dve, V_LN)
            a_step(act.activation(v_lnv, v_v, ACT.Ln))
            a_step(act.activation(v_t3, v_vn, ACT.Ln))
            for k in range(4):
                act.wait_ge(p_dve, V_ANGLE[k])
                a_step(act.activation(rope_sp[k], ang, ACT.Sin))
                a_step(act.activation(half_sin, ang, ACT.Sin, scale=0.5))
            for m in range(4):
                for s in range(4):
                    i = 4 * m + s
                    if s == 0:
                        act.wait_ge(raww[m % 2], (16, 16, 32, 48)[m])
                    if i >= 2:
                        act.wait_ge(split_out[i % 2], 16 * (i // 2))
                    for hi, lo, raw in split_views(m, s):
                        last = act.activation(hi, raw, ACT.Copy)
                    last.then_inc(split_hi, 1)
            jobs = ffn_jobs()
            for n in range(9):
                act.wait_ge(ffn_tr, n + 1)
                act.activation(jobs[4 * n][1], ps[n % 2][:, :], ACT.Copy).then_inc(ffn_ev, 1)
            with act.Fori(0, B // 2) as i:
                c16 = act.snap(i * 16 + 16)
                for s in range(2):
                    c = act.snap(i * 4 + 2 * s + 2)
                    for kt in range(KT):
                        act.wait_ge(x_tr, c + kt + 1)
                        if kt == 0:
                            act.wait_ge(x_out[s], c16)
                        act.activation(xt[s][:, kt, 0, :], pp[kt][:, :], ACT.Copy).then_inc(x_hi, 1)

            def swap(c, hh, m):
                act.wait_ge(proj, c[10] + (1, 7)[hh] + m)
                act.wait_ge(t2_pool, c[4] + 2 * hh + m + 1 - 2)
                act.activation(sq[:, m, :], pa[m][:, :], ACT.Square)
                scale = -2.0 if m == 0 else 1.0
                act.activation(swt[0:DH, m, :], pa[m][DH:P, :], ACT.Copy, scale=scale)
                act.activation(swt[DH:P, m, :], pa[m][0:DH, :], ACT.Copy, scale=scale).then_inc(pa_act, 1)

            def keep_norm_k(c, hh):
                act.wait_ge(proj, c[10] + (3, 9)[hh])
                act.wait_ge(ek_pool, c[8] + 4 * hh + 4 - 8)
                act.activation(qkb[:, 3 * hh + 2, :], pa[0][:, :], ACT.Copy).then_inc(pa_act, 1)

            def keep_values(c):
                for half in range(2):
                    act.wait_ge(proj, c[10] + 5 + half)
                    if half == 0:
                        act.wait_ge(av_rdy, c[8] + 8 - 8)
                    act.activation(vt[:, 2 * half:2 * half + 2, :].rearrange("p a n -> p (a n)"), pa[half][:, :],
                                   ACT.Copy).then_inc(pa_act, 1)

            def log(c, hh, n):
                i, m = n % 2, 4 * hh + n
                w = width(n)
                act.wait_ge(cd_dve, c[8] + m + 1)
                act.wait_ge(ex_act, c[8] + m + 1 - 2)
                act.activation(lg[:, i, 0:w], t1[:, i, 0:w], ACT.Ln,
                               bias=qn[:, hh, 0, TILES[n]:TILES[n] + 1]).then_inc(ln_act, 1)

            def exp(c, hh, n):
                i, m = n % 2, 4 * hh + n
                w = width(n)
                q = NT * hh + TILES[n]
                act.wait_ge(f_dve, c[8] + m + 1)
                act.wait_ge(tr_rdy, c[8] + m + 1 - 2)
                act.activation(pr[:, i, 0:w], lg[:, i, 0:w], ACT.Exp, bias=nmax[:, q:q + 1], scale=-1.0,
                               accum_out=den[:, q:q + 1]).then_inc(ex_act, 1)

            def keep_turned(c, hh, n):
                i, m = n % 2, 4 * hh + n
                w = width(n)
                act.wait_ge(tr_rdy, c[8] + m + 1)
                act.wait_ge(av_rdy, c[8] + m + 1 - 2)
                act.activation(pt[:, i, 0:w], pp[i][:, 0:w], ACT.Copy).then_inc(pt_act, 1)

            def y_high(c, hh):
                act.wait_ge(yt_rdy, c[2] + hh + 1)
                if hh == 0:
                    act.wait_ge(o_rdy, c[2] + 2 - 2)
                act.activation(yhl[:, hh, 0, :], po[:, :], ACT.Copy).then_inc(yh_act, 1)

            def unit(c, hh, nxt):
                if nxt:
                    cn, nh = nxt
                    swap(cn, nh, 0)
                log(c, hh, 0)
                if nxt:
                    swap(cn, nh, 1)
                log(c, hh, 1)
                exp(c, hh, 0)
                if nxt:
                    keep_norm_k(cn, nh)
                log(c, hh, 2)
                exp(c, hh, 1)
                keep_turned(c, hh, 0)
                log(c, hh, 3)
                exp(c, hh, 2)
                keep_turned(c, hh, 1)
                exp(c, hh, 3)
                keep_turned(c, hh, 2)
                keep_turned(c, hh, 3)
                y_high(c, hh)
                if nxt and nh == 0:
                    keep_values(cn)

            PERS = (10, 8, 4, 2)

            def half0(t, b, par):
                c = counts(act, t, PERS)
                unit(c, 0, (c, 1))

            def half1(t, b, par, npar, ng):
                c = counts(act, t, PERS)
                nxt = None
                if npar is not None:
                    nxt = ({p: v + p for p, v in c.items()}, 0)
                unit(c, 1, nxt)

            c0 = counts(act, 0, PERS)
            swap(c0, 0, 0)
            swap(c0, 0, 1)
            keep_norm_k(c0, 0)
            keep_values(c0)
            run_groups(act, lambda gg, par, last: iterations(act, gg, par, last, half0, half1))

            credit(act, (f_hi, 2), (f_silu, FT), (f_hh, FT), (f_ev, 2))

            def f_high(c, s):
                for kt in range(KT):
                    act.wait_ge(f_tr, c[2] + kt + 1)
                    if kt == 0:
                        act.wait_ge(f_u, c[FT])
                    act.activation(xt[s][:, kt, 0, :], pp[kt][:, :], ACT.Copy).then_inc(f_hi, 1)

            def silu(c, r):
                act.wait_ge(f_g, c[FT] + r + 1)
                act.wait_ge(f_h, c[FT] + r + 1 - 2)
                act.activation(f_gate(r), pa[r % 2][:, :], ACT.Silu, scale=SCALE).then_inc(f_silu, 1)

            def hidden_high(c, r):
                act.wait_ge(f_h, c[FT] + r + 1)
                if r == 0:
                    act.wait_ge(f_dn, c[2] + 2 - 2)
                act.activation(hpart(r, 0), f_hid(r), ACT.Copy).then_inc(f_hh, 1)

            def f_body(b, s, nxt):
                c = counts(act, b, (FT, 2, 1))
                silu(c, 0)
                for r in range(1, FT):
                    silu(c, r)
                    hidden_high(c, r - 1)
                hidden_high(c, FT - 1)
                if nxt:
                    f_high({p: v + p for p, v in c.items()}, 1 - s)
                for half, src in enumerate((py, po)):
                    act.wait_ge(f_dn, c[2] + half + 1)
                    act.wait_ge(f_res, c[1] + 1)
                    act.activation(f_y[:, 2 * half:2 * half + 2, :], src[:, :].rearrange("p (j n) -> p j n", j=2),
                                   ACT.Copy, scale=SCALE).then_inc(f_ev, 1)

            f_high(counts(act, 0, (FT, 2)), 0)
            with act.Fori(0, B // 2 - 1) as i:
                f_body(act.snap(i * 2), 0, True)
                f_body(act.snap(i * 2 + 1), 1, True)
            f_body(B - 2, 0, True)
            f_body(B - 1, 1, False)

        @block.vector
        def _(dve):
            credit(dve, (pa_dve, 6), (rope, 4), (a_dve, 8), (b_dve, 8 - 2 * NPB), (cd_dve, 8), (f_dve, 8), (rd_dve, 2),
                   (y_dve, 2), (yl_dve, 2), (acc_dve, 2), (x_norm, 2), (x_lo, 2), (x_ln, 3))
            tt, ts, stt, rec = dve.tensor_tensor, dve.tensor_scalar, dve.scalar_tensor_tensor, dve.reciprocal
            done = [0]

            def step(ins):
                done[0] += 1
                ins.then_inc(p_dve, 1)
                dve.wait_ge(p_dve, done[0])

            def settle(v):
                if not isinstance(v, int):
                    dve.sem_inc(settled, 1)

            def col(k, n=1):
                return hp[:, k:k + n]
            MU, TAU, E0 = 0, 5, 11
            SP, NMU, C1, C2, RL, RB = 26, 36, 37, 38, 23, 24
            dve.wait_ge(p_load, 16 * 10)
            dve.wait_ge(p_act, 3)
            step(ts(col(21, 5), col(0, 5), 0.0, None, ALU.max))
            step(tt(col(SP, 5), col(21, 5), col(16, 5), ALU.add))
            step(ts(col(31), col(MU), 0.0, None, ALU.is_ge))
            step(tt(col(32), col(31), col(E0), ALU.max))
            step(ts(col(33), col(E0), 1.0, None, ALU.add))
            step(rec(col(34), col(33)))
            step(stt(col(35), col(32), 1.0, col(34), ALU.mult, ALU.mult))
            step(ts(col(35), col(35), EPS_MU, None, ALU.add))
            step(ts(col(NMU), col(35), -1.0, None, ALU.mult))
            step(ts(col(39), col(35), 2.0, None, ALU.mult))
            step(rec(col(39), col(39)))
            step(tt(col(C1), col(SP + 1), col(39), ALU.mult))
            step(tt(col(C2), col(SP + 2), col(SP + 3), ALU.add))
            step(ts(col(21), col(SP + 4), float(DH), -0.5, ALU.add, ALU.mult))
            dve.wait_ge(consts, 5)
            step(ts(v_e, dist, 0.0, None, ALU.max))
            step(ts(v_e, v_e, col(NMU), MIN_EXP, ALU.mult, ALU.max))
            step(ts(v_e, v_e, 0.0, None, ALU.min))
            dve.wait_ge(p_act, 4)
            step(tt(v_v, v_e, v_e, ALU.mult))
            step(ts(v_v, v_v, -1.0, 1.0, ALU.mult, ALU.add))
            step(ts(v_v, v_v, col(C1), col(C2), ALU.mult, ALU.add))
            step(ts(v_vn, v_v, col(SP + 4), None, ALU.mult))
            step(tt(col(22), col(21), col(TAU), ALU.mult))
            step(ts(col(21), col(22), 0.0, 1e-20, ALU.is_equal, ALU.mult))
            step(tt(col(22), col(22), col(21), ALU.add))
            step(rec(col(25), col(22)))
            step(ts(col(NCO), col(22), -1.0, None, ALU.mult))
            step(ts(col(RL), col(25), -0.5 * DH, None, ALU.mult))
            step(ts(col(RB), col(25), -BIG, None, ALU.mult))
            dve.wait_ge(p_act, 6)
            step(stt(v_t3, v_lnv, col(RL), v_t3, ALU.mult, ALU.subtract))
            step(ts(v_t3[:, N:VEC], v_t3[:, N:VEC], col(RB), None, ALU.add))
            assert done[0] == V_TABLES, done
            TWO_PI = (6.28125, 1.9350051879882812e-3, 3.0199159819567529e-7)
            for k in range(4):
                step(ts(ang, tokens, om[:, k:k + 1], None, ALU.mult))
                step(ts(turns, ang, 1.0 / (2 * math.pi), MAGIC, ALU.mult, ALU.add))
                step(ts(turns, turns, MAGIC, None, ALU.subtract))
                for c in TWO_PI:
                    step(stt(ang, turns, -c, ang, ALU.mult, ALU.add))
                step(ts(ang, ang, 3.1415925, -3.1415925, ALU.min, ALU.max))
                dve.wait_ge(p_act, 8 + 2 * k)
                step(ts(rope_sn[k], rope_sp[k], -1.0, None, ALU.mult))
                step(tt(half_sin, half_sin, half_sin, ALU.mult))
                step(ts(rope_cs[k], half_sin, -2.0, 1.0, ALU.mult, ALU.add))
                assert done[0] == V_ROPE[k]
            dve.wait_ge(ffn_in, 48)
            for z in (qkb[:, 0:3, :], qkb[:, 3:6, :], swt[:, 0:3, :]):
                dve.tensor_copy(z, z.bitcast(I32)).then_inc(ffn_cast, 1)
            for m in range(4):
                for s in range(4):
                    dve.wait_ge(split_hi, 4 * m + s + 1)
                    for hi, lo, raw in split_views(m, s):
                        last = tt(lo, raw, hi.bitcast(F32), ALU.subtract)
                    last.then_inc(split_lo, 1)

            def norm(src, dst, chain, c, k, made, v, mark):
                for j in range(NT):
                    last = dve.bn_stats(stats[:, j, :], src(j))
                last.then_inc(chain, 1)
                dve.wait_ge(chain, c + k + 1)
                settle(c)
                for j in range(NT):
                    last = dve.bn_aggr(mv[:, j, :], stats[:, j, :])
                last.then_inc(chain, 1)
                dve.wait_ge(chain, c + k + 2)
                ts(rstd[:, :], mv[:, :, 1], EPS_LN, None, ALU.add).then_inc(chain, 1)
                dve.wait_ge(made, v)
                for j in range(NT):
                    last = ts(dst(j), src(j), mv[:, j, 0:1], rstd[:, j:j + 1], ALU.subtract, ALU.mult)
                last.then_inc(mark, 1)

            with dve.Fori(0, B // 2) as i:
                i16 = dve.snap(i * 16 + 16)
                for s in range(2):
                    c3 = dve.snap(i * 6 + 3 * s + 3)
                    c1 = dve.snap(i * 2 + s + 2)
                    c2 = dve.snap(i * 4 + 2 * s + 2)
                    dve.wait_ge(x_in[s], i16)
                    dve.wait_ge(x_tr, c2)
                    norm(lambda j: xraw[s][:, j, :], lambda j: xnorm[s][:, j, :], x_ln, c3, 0, x_root, c1, x_norm)
                    for kt in range(KT):
                        dve.wait_ge(x_hi, c2 + kt + 1)
                        tt(xt[s][:, kt, 1, :], pp[kt][:, :], xt[s][:, kt, 0, :].bitcast(F32), ALU.subtract).then_inc(x_lo, 1)

            def rotate(c, hh, par, m):
                dve.wait_ge(pa_act, c[8] + (1, 6)[hh] + m)
                dst = qkb[:, 3 * hh + m, :]
                if m == 0:
                    stt(dst, pa[0][:, :], -2.0, ropet(par, hh, 0), ALU.mult, ALU.mult).then_inc(pa_dve, 1)
                else:
                    tt(dst, pa[1][:, :], ropet(par, hh, 0), ALU.mult).then_inc(pa_dve, 1)

            def rotated(c, hh, m):
                dst = qkb[:, 3 * hh + m, :]
                dve.wait_ge(pa_dve, c[6] + 3 * hh + m + 1)
                dve.wait_ge(t2_pool, c[4] + 2 * hh + m + 1)
                tt(dst, dst, swt[:, 2 + m, :], ALU.add).then_inc(rope, 1)

            def keep_norm_q(c, hh):
                dve.wait_ge(proj, c[10] + (4, 10)[hh])
                dve.tensor_copy(qn[:, hh, 0, :], pa[1][:, 0:NT])
                ts(qn[:, hh, 1, :], pa[1][:, 0:NT], -1.0, None, ALU.mult).then_inc(pa_dve, 1)

            def distance_a(c, hh, n):
                i, m, w = n % 2, 4 * hh + n, width(n)
                dve.wait_ge(s_rdy, c[8] + m + 1)
                dve.wait_ge(ek_pool, c[8] + m + 1)
                dve.wait_ge(ln_act, c[8] + m + 1 - 2)
                tt(t1[:, i, 0:w], ps[i][:, 0:w], ek[:, i, 0:w], ALU.add).then_inc(a_dve, 1)

            def distance_b(c, hh, n, par):
                if n in POOL_SCALES:
                    return
                i, m, w = n % 2, 4 * hh + n, width(n)
                dve.wait_ge(a_dve, c[8] + m + 1)
                tt(t1[:, i, 0:w], t1[:, i, 0:w], tab(par, hh, E_T, N - w), ALU.mult).then_inc(b_dve, 1)

            def distance_c(c, hh, n, par):
                i, m, w = n % 2, 4 * hh + n, width(n)
                before = sum(1 for q in POOL_SCALES if q <= n)
                if n in POOL_SCALES:
                    dve.wait_ge(b_pool, c[2] * NPB + NPB * hh + before)
                else:
                    dve.wait_ge(b_dve, c[2] * (4 - NPB) + (4 - NPB) * hh + n + 1 - before)
                stt(t1[:, i, 0:w], t1[:, i, 0:w], qn[:, hh, 1, TILES[n]:TILES[n] + 1], tab(par, hh, VN_T, N - w),
                    ALU.max, ALU.add).then_inc(cd_dve, 1)

            def logits(c, hh, n, par):
                i, m, w = n % 2, 4 * hh + n, width(n)
                q = NT * hh + TILES[n]
                dve.wait_ge(ln_act, c[8] + m + 1)
                settle(c[8])
                dve.tensor_tensor_reduce(lg[:, i, 0:w], lg[:, i, 0:w], tab(par, hh, T3_T, N - w), ncog[:, par, hh:hh + 1],
                                         3e38, ALU.add, ALU.min, nmax[:, q:q + 1]).then_inc(f_dve, 1)

            def keep_y(c, hh):
                dve.wait_ge(ex_act, c[8] + 4 * hh + 4)
                rec(rden[:, NT * hh:NT * hh + NT], den[:, NT * hh:NT * hh + NT]).then_inc(rd_dve, 1)
                dve.wait_ge(rd_dve, c[2] + hh + 1)
                dve.wait_ge(av_rdy, c[8] + 4 * hh + 4)
                dve.wait_ge(yt_rdy, c[2] + hh + 1 - 1)
                tt(ysb[:, :, :], py[:, :].rearrange("p (j n) -> p j n", j=NT),
                   rden[:, NT * hh:NT * hh + NT].unsqueeze(2).broadcast_to([P, NT, P]), ALU.mult).then_inc(y_dve, 1)

            def y_low(c, hh):
                dve.wait_ge(yh_act, c[2] + hh + 1)
                tt(yhl[:, hh, 1, :], po[:, :], yhl[:, hh, 0, :].bitcast(F32), ALU.subtract).then_inc(yl_dve, 1)

            def add_output(c, b):
                for half, src in enumerate((po, py)):
                    dve.wait_ge(o_rdy, c[2] + half + 1)
                    if isinstance(b, int):
                        dst = accf[:, b * NT * D + half * N:b * NT * D + half * N + N]
                    else:
                        dst = accf[:, bass.ds(b * (NT * D) + half * N, N)]
                    tt(dst, dst, src[:, :], ALU.add).then_inc(acc_dve, 1)

            def unit(c, hh, par, nxt):
                distance_a(c, hh, 0)
                distance_a(c, hh, 1)
                if nxt:
                    cn, nh, npar = nxt
                    rotate(cn, nh, npar, 0)
                distance_b(c, hh, 0, par)
                distance_b(c, hh, 1, par)
                distance_c(c, hh, 0, par)
                if nxt:
                    rotated(cn, nh, 0)
                    rotate(cn, nh, npar, 1)
                distance_c(c, hh, 1, par)
                logits(c, hh, 0, par)
                distance_a(c, hh, 2)
                if nxt:
                    rotated(cn, nh, 1)
                distance_b(c, hh, 2, par)
                logits(c, hh, 1, par)
                distance_a(c, hh, 3)
                distance_c(c, hh, 2, par)
                distance_b(c, hh, 3, par)
                if nxt:
                    keep_norm_q(cn, nh)
                distance_c(c, hh, 3, par)
                logits(c, hh, 2, par)
                logits(c, hh, 3, par)
                keep_y(c, hh)
                y_low(c, hh)

            PERS = (10, 8, 6, 4, 2)

            def half0(t, b, par):
                c = counts(dve, t, PERS)
                unit(c, 0, par, (c, 1, par))

            def half1(t, b, par, npar, ng):
                c = counts(dve, t, PERS)
                if npar is not None and ng is not None:
                    dve.wait_ge(grp[npar], (ng + 1) * 64 if isinstance(ng, int) else dve.snap((ng + 1) * 64))
                nxt = None
                if npar is not None:
                    nxt = ({p: v + p for p, v in c.items()}, 0, npar)
                unit(c, 1, par, nxt)
                add_output(c, b)

            def start(gg, par):
                g = gg * 2 + par
                if isinstance(g, int):
                    src, v = nco[:, g * HH:(g + 1) * HH], g + 1
                else:
                    src, v = nco[:, bass.ds(g * HH, HH)], dve.snap(g + 1)
                dve.tensor_copy(ncog[:, par, :], src).then_inc(ncog_dve, 1)
                dve.wait_ge(ncog_dve, v)
                settle(v)

            dve.wait_ge(nco_in, 16)
            dve.wait_ge(consts, 7)
            dve.wait_ge(grp[0], 64)
            c0 = counts(dve, 0, PERS)
            rotate(c0, 0, 0, 0)
            rotated(c0, 0, 0)
            rotate(c0, 0, 0, 1)
            rotated(c0, 0, 1)
            keep_norm_q(c0, 0)
            run_groups(dve, lambda gg, par, last: iterations(dve, gg, par, last, half0, half1, start))

            credit(dve, (f_norm, 2), (f_lo, 2), (f_h, FT), (f_res, 2), (f_ln, 8), (f_l3, 4))

            def acc_of(b, j0=0, n=NT):
                if isinstance(b, int):
                    return accf[:, (b * NT + j0) * D:(b * NT + j0 + n) * D]
                return accf[:, bass.ds(b * (NT * D) + j0 * D, n * D)]

            def front(b, c, s, xv):
                def part0():
                    dve.wait_ge(f_x[s], xv)
                    settle(c[2])
                    norm(lambda j: acc_of(b, j, 1), lambda j: f_tmp[:, j, :], f_ln, c[8], 0, f_root, c[2] + 1, f_ln)

                def part1():
                    dve.wait_ge(f_ln, c[8] + 4)
                    tt(acc_of(b), f_tmp.rearrange("p j n -> p (j n)"), f_xin[s].rearrange("p j n -> p (j n)"),
                       ALU.add).then_inc(f_ln, 1)
                    dve.wait_ge(f_ln, c[8] + 5)

                def part2():
                    dve.wait_ge(f_tr, c[2])
                    settle(xv)
                    norm(lambda j: acc_of(b, j, 1), lambda j: f_nrm[:, j, :], f_ln, c[8], 5, f_root, c[2] + 2, f_norm)
                return [part0, part1, part2]

            def split_low(c, s):
                for kt in range(KT):
                    dve.wait_ge(f_hi, c[2] + kt + 1)
                    tt(xt[s][:, kt, 1, :], pp[kt][:, :], xt[s][:, kt, 0, :].bitcast(F32), ALU.subtract).then_inc(f_lo, 1)

            def hidden(c, r):
                dve.wait_ge(f_silu, c[FT] + r + 1)
                dve.wait_ge(f_u, c[FT] + r + 1)
                dve.wait_ge(f_hl, c[FT] + r + 1 - 2)
                dve.wait_ge(f_hh, c[FT] + r + 1 - 2)
                stt(f_hid(r), ps[r % 2][:, :], SCALE, f_gate(r), ALU.mult, ALU.mult).then_inc(f_h, 1)

            def back(b, c, s, ov):
                dve.wait_ge(f_ev, c[2] + 2)
                norm(lambda j: f_y[:, j, :], lambda j: f_tmp[:, j, :], f_l3, c[4], 0, f_rootb, c[1] + 1, f_l3)
                dve.wait_ge(f_l3, c[4] + 4)
                dve.wait_ge(f_out[s], ov)
                tt(f_outs[s].rearrange("p j n -> p (j n)"), f_tmp.rearrange("p j n -> p (j n)"), acc_of(b),
                   ALU.add).then_inc(f_res, 1)

            FP = (FT, 8, 4, 2, 1)

            def f_body(b, s, i, nxt):
                c = counts(dve, b, FP)
                parts = [None] * 3
                if nxt:
                    cn = {p: v + p for p, v in c.items()}
                    xv = (i + (2 if s else 1)) * 16
                    parts = front(b + 1 if isinstance(b, int) else dve.snap(b + 1), cn, 1 - s,
                                  xv if isinstance(xv, int) else dve.snap(xv))
                for r in range(FT):
                    hidden(c, r)
                    if nxt and r < 3:
                        parts[r]()
                if nxt:
                    split_low(cn, 1 - s)
                ov = (i + 1) * 16
                back(b, c, s, ov if isinstance(ov, int) else dve.snap(ov))

            c0 = counts(dve, 0, FP)
            for part in front(0, c0, 0, 16):
                part()
            split_low(c0, 0)
            with dve.Fori(0, B // 2 - 1) as i:
                f_body(dve.snap(i * 2), 0, i, True)
                f_body(dve.snap(i * 2 + 1), 1, i, True)
            f_body(B - 2, 0, B // 2 - 1, True)
            f_body(B - 1, 1, B // 2 - 1, False)


_INS = ['L0_attn_x', 'L0_attn_Wq', 'L0_attn_Wk', 'L0_attn_Wv', 'L0_attn_Wo', 'L0_attn_omega', 'L0_attn_mu_raw',
        'L0_attn_sigma_raw', 'L0_attn_eta_raw', 'L0_attn_gamma_raw', 'L0_attn_nu_raw', 'L0_attn_tau',
        'L0_ffn_w_gate', 'L0_ffn_w_up', 'L0_ffn_w_down']


def kernel(**inputs):
    import concourse.bacc as _bacc
    from concourse.bass_utils import run_bass_kernel_spmd as _run

    nc = _bacc.Bacc("TRN2", target_bir_lowering=False, num_devices=1)
    arrays, args = {}, []
    for name in _INS:
        a = np.ascontiguousarray(inputs[name])
        arrays[f"in_{name}"] = a
        args.append(nc.dram_tensor(f"in_{name}", a.shape, mybir.dt.from_np(a.dtype), kind="ExternalInput").ap())
    out = nc.dram_tensor("out", (B, N, D), F32, kind="ExternalOutput").ap()
    build(nc, *args[0:6], args[6:11], *args[11:15], out)
    r = _run(nc, [arrays], core_ids=[0])
    return r.results[0]["out"]
```

```python
import math
from collections import namedtuple
from contextlib import ExitStack

import numpy as np
import concourse.bass as bass
from concourse import mybir

F32 = mybir.dt.float32
F32R = mybir.dt.float32r
I32 = mybir.dt.int32
ALU = mybir.AluOpType
ACT = mybir.ActivationFunctionType

It = namedtuple("It", "t half b par slot before behind b_before new opens")
B, N, D = 8, 512, 256
H, DH = 16, 64
DK = H * DH
HID = 768
P = 128
KT = D // P
NT = N // P
HH = 2
G = H // HH
FT = HID // P
W2 = HH * 2 * DH
EPS_LN = 1e-5
EPS_MU = 1e-4
MIN_EXP = -30.0
BIG = 1e18
SCALE = 1.0 / 127.0
MAGIC = 1.5 * 2.0 ** 23
VEC = N + P
E_T, VN_T, T3_T = range(3)
V_EXP, V_LN, V_TABLES = 17, 22, 30
V_ANGLE = [V_TABLES + 10 * k + 7 for k in range(4)]
V_ROPE = [V_TABLES + 10 * k + 10 for k in range(4)]
NCO = 22
TILES = tuple(range(NT - 1, -1, -1))
WS = sum(i + 1 for i in TILES) * P
POOL_SCALES = (0,)


def build(nc, x_d, wq_d, wk_d, wv_d, wo_d, omega_d, raw_d, tau_d, wg_d, wu_d, wd_d, out_d):
    ctx = ExitStack()
    with ctx:
        def sb(name, shape, dt=F32):
            return ctx.enter_context(nc.sbuf_tensor(name, shape, dt))

        def sem(name):
            return ctx.enter_context(nc.semaphore(name))

        def scratch(name, shape):
            return nc.dram_tensor(name, shape, F32, kind="Internal").ap()

        xs_d = scratch("xs_d", (B, P, KT * 2 * N))
        ws_d = scratch("ws_d", (G, P, 3 * KT * 2 * W2))
        wos_d = scratch("wos_d", (G, P, HH * 2 * D))
        vec_d = scratch("vec_d", (3, H, VEC))
        tab_d = scratch("tab_d", (G, P, HH, 3, N))
        rope_d = scratch("rope_d", (G, P, HH, 2, N))
        nco_d = scratch("nco_d", (1, H))

        acc = sb("acc", [P, B, NT, D])
        tabs = [sb(f"tabs{i}", [P, 5 * HH, N]) for i in range(2)]
        wt = sb("wt", [P, 2, 3 * KT * 2 * W2], F32R)
        wot = sb("wot", [P, 2, HH * 2 * D], F32R)
        xt = [sb(f"xt{i}", [P, KT, 2, N], F32R) for i in range(2)]
        qkb = sb("qkb", [P, 3 * HH, N])
        sq = sb("sq", [P, 2, N])
        swt = sb("swt", [P, 4, N])
        ek = sb("ek", [P, 2, N])
        lg = sb("lg", [P, 2, WS])
        pr = sb("pr", [P, WS])
        pt = sb("pt", [P, 2, N])
        vt = sb("vt", [P, NT, HH * P])
        ysb = sb("ysb", [P, NT, P])
        yhl = sb("yhl", [P, HH, 2, N], F32R)
        wgt = sb("wgt", [P, KT, HID], F32R)
        wut = sb("wut", [P, KT, HID], F32R)
        wdt = sb("wdt", [P, FT, D], F32R)
        ident = sb("ident", [P, P])
        ones = sb("ones", [P, P])
        qn = sb("qn", [P, HH, 2, NT])
        nmax = sb("nmax", [P, 2 * NT])
        den = sb("den", [P, 2 * NT])
        rden = sb("rden", [P, 2 * NT])
        nco = sb("nco", [P, H])
        ncog = sb("ncog", [P, 2, HH])
        hp = sb("hp", [H, 40])
        om = sb("om", [P, 4])
        stats = sb("stats", [P, NT, 6])
        mv = sb("mv", [P, NT, 2])
        rstd = sb("rstd", [P, NT])
        mhalf = sb("mhalf", [P, NT])

        accf = acc[:, :, :, :].rearrange("p b j n -> p (b j n)")
        dist, v_e, v_vn, v_t3, v_v, v_lnv = [accf[0:H, k * VEC:(k + 1) * VEC] for k in range(6)]
        tokens, ang, turns, half_sin = lg[:, 1, N:2 * N], sq[:, 0, :], sq[:, 1, :], ysb[:, :, :].rearrange("p j n -> p (j n)")
        rope_sn = [accf[:, 4096 + k * N:4096 + (k + 1) * N] for k in range(4)]
        rope_sp = [accf[:, 6144 + k * N:6144 + (k + 1) * N] for k in range(4)]
        rope_cs = [pr[:, 0:N], pr[:, N:2 * N], pt[:, 0, :], pt[:, 1, :]]
        xraw = [z[:, :, :].rearrange("p a n -> p (a n)").rearrange("p (j n) -> p j n", j=NT) for z in (ek, vt)]
        xnorm = [lg[:, a, 0:NT * D].rearrange("p (j n) -> p j n", j=NT) for a in range(2)]

        def seq(s, k):
            return tabs[s][:, k:k + 2, :].rearrange("p a n -> p (a n)").rearrange("p (j n) -> p j n", j=NT)
        f_xin = [seq(0, 0), seq(1, 0)]
        f_outs = [seq(0, 2), seq(1, 2)]
        f_nrm = seq(0, 4)
        f_tmp = seq(1, 6)
        f_y = seq(1, 4)

        def f_gate(r):
            return tabs[0][:, 6 + r % 2, :]

        def f_hid(r):
            return tabs[0][:, 8 + r % 2, :]

        def hpart(r, a):
            o = (r * 2 + a) * N
            return wt[:, :, :].rearrange("p a n -> p (a n)")[:, o:o + N]

        def bank(name):
            return ctx.enter_context(nc.psum_tensor(name, [P, N], F32))
        pa = [bank("pa0"), bank("pa1")]
        ps = [bank("ps0"), bank("ps1")]
        pp = [bank("pp0"), bank("pp1")]
        py = bank("py")
        po = bank("po")

        consts = sem("consts")
        p_load = sem("p_load")
        p_dve = sem("p_dve")
        p_act = sem("p_act")
        vec_out = sem("vec_out")
        tab_out = sem("tab_out")
        rope_out = sem("rope_out")
        nco_in = sem("nco_in")
        raww = [sem(f"raww{i}") for i in range(2)]
        split_hi = sem("split_hi")
        split_lo = sem("split_lo")
        split_out = [sem(f"split_out{i}") for i in range(2)]
        ffn_in = sem("ffn_in")
        ffn_cast = sem("ffn_cast")
        ffn_tr = sem("ffn_tr")
        ffn_ev = sem("ffn_ev")
        x_in = [sem(f"x_in{i}") for i in range(2)]
        x_ln = sem("x_ln")
        x_root = sem("x_root")
        x_norm = sem("x_norm")
        x_tr = sem("x_tr")
        x_hi = sem("x_hi")
        x_lo = sem("x_lo")
        x_out = [sem(f"x_out{i}") for i in range(2)]

        grp = [sem(f"grp{i}") for i in range(2)]
        xt_in = [sem(f"xt_in{i}") for i in range(2)]
        proj = sem("proj")
        s_rdy = sem("s_rdy")
        tr_rdy = sem("tr_rdy")
        av_rdy = sem("av_rdy")
        yt_rdy = sem("yt_rdy")
        o_rdy = sem("o_rdy")
        pa_act = sem("pa_act")
        ln_act = sem("ln_act")
        ex_act = sem("ex_act")
        pt_act = sem("pt_act")
        yh_act = sem("yh_act")
        pa_dve = sem("pa_dve")
        rope = sem("rope")
        a_dve = sem("a_dve")
        b_dve = sem("b_dve")
        b_pool = sem("b_pool")
        cd_dve = sem("cd_dve")
        f_dve = sem("f_dve")
        rd_dve = sem("rd_dve")
        y_dve = sem("y_dve")
        yl_dve = sem("yl_dve")
        acc_dve = sem("acc_dve")
        ek_pool = sem("ek_pool")
        t2_pool = sem("t2_pool")

        NPB = len(POOL_SCALES)

        f_x = [sem(f"f_x{i}") for i in range(2)]
        f_ln = sem("f_ln")
        f_root = sem("f_root")
        f_rootb = sem("f_rootb")
        f_norm = sem("f_norm")
        f_tr = sem("f_tr")
        f_hi = sem("f_hi")
        f_lo = sem("f_lo")
        f_g = sem("f_g")
        f_u = sem("f_u")
        f_silu = sem("f_silu")
        f_h = sem("f_h")
        f_hh = sem("f_hh")
        f_hl = sem("f_hl")
        f_dn = sem("f_dn")
        f_ev = sem("f_ev")
        f_res = sem("f_res")
        f_l3 = sem("f_l3")
        f_out = [sem(f"f_out{i}") for i in range(2)]
        settled = sem("settled")
        ncog_dve = sem("ncog_dve")

        block = ctx.enter_context(nc.Block())

        def counts(eng, t, pers):
            if isinstance(t, int):
                return {p: (t + 1) * p for p in pers}
            t = eng.snap(t + 1)
            return {p: eng.snap(t * p) if p > 1 else t for p in pers}

        def credit(eng, *pairs):
            for s, n in pairs:
                if n:
                    eng.sem_inc(s, n)

        def run_iterations(eng, body):
            def snap(v):
                return v if isinstance(v, int) else eng.snap(v)

            body(It(t=0, half=0, b=0, par=0, slot=0, before=None, behind=0, b_before=None, new=0, opens=None))

            def group(gg, par, last):
                t0, h0, g = gg * 2 * B + par * B, gg * B + par * B // 2, gg * 2 + par
                with eng.Fori(0, B // 2 - 1) as i:
                    for k in (1, 2):
                        body(It(t=snap(i * 2 + t0 + k), half=snap(i + h0 + k - 1), b=snap(i * 2 + k), par=par, slot=k % 2,
                                before=par, behind=par, b_before=snap(i * 2 + k - 1), new=None, opens=None))
                body(It(t=snap(t0 + B - 1), half=snap(h0 + B // 2 - 1), b=B - 1, par=par, slot=1, before=par,
                        behind=None if last else 1 - par, b_before=B - 2, new=None,
                        opens=None if last else snap(((g + 1) // 2 + 1) * 64 if isinstance(g, int) else (gg + (1 + par)) * 64)))
                if not last:
                    body(It(t=snap(t0 + B), half=snap(h0 + B // 2), b=0, par=1 - par, slot=0, before=par,
                            behind=1 - par, b_before=B - 1, new=snap(g + 1), opens=None))

            with eng.Fori(0, G // 2 - 1) as gg:
                group(gg, 0, False)
                group(gg, 1, False)
            group(G // 2 - 1, 0, False)
            group(G // 2 - 1, 1, True)

        def following(c):
            return {p: v + p for p, v in c.items()}

        def previous(c):
            return {p: v - p for p, v in c.items()}

        def tab(par, hh, k, lo=0, hi=N):
            return tabs[par][:, hh * 3 + k, lo:hi]

        def ropet(par, hh, k):
            return tabs[par][:, 3 * HH + hh * 2 + k, :]

        def wproj(par, m, kt, part, lo, hi):
            o = ((m * KT + kt) * 2 + part) * W2
            return wt[:, par, o + lo:o + hi]

        def width(n):
            return (TILES[n] + 1) * P

        def at(n):
            o = sum(width(k) for k in range(n))
            return slice(o, o + width(n))

        PARTS = ((0, 0), (0, 1), (1, 0))

        def split_views(m, s):
            stage = wt[:, (4 * m + s) % 2, 0:2048]
            raw = tabs[m % 2][:, 0:8, :].rearrange("p a n -> p (a n)")
            if m < 3:
                kt, gh = s // 2, s % 2
                out = stage.rearrange("p (g a h c d) -> p a c g h d", g=4, a=2, h=HH, c=2)
                for c in range(2):
                    o = kt * 2 * DK + c * DK + gh * DK // 2
                    yield out[:, 0, c], out[:, 1, c], raw[:, o:o + DK // 2].rearrange("p (g h d) -> p g h d", g=4, h=HH)
            else:
                out = stage.rearrange("p (h a n) -> p a h n", h=2 * HH, a=2)
                yield out[:, 0], out[:, 1], raw[:, s * 1024:(s + 1) * 1024].rearrange("p (h n) -> p h n", h=2 * HH)

        def ffn_jobs():
            jobs = []
            for raw, dst in ((qkb[:, 0:3, :], wgt), (qkb[:, 3:6, :], wut)):
                r6 = raw.rearrange("p a n -> p (a n)").rearrange("p (r n) -> p r n", r=FT)
                for kt in range(KT):
                    for r in range(FT):
                        o = kt * HID + r * P
                        jobs.append((r6[:, r, kt * P:(kt + 1) * P],
                                     dst[:, :, :].rearrange("p k n -> p (k n)")[:, o:min(o + 4 * P, KT * HID)]))
            w2 = swt[:, 0:3, :].rearrange("p a n -> p (a n)").rearrange("p (r n) -> p r n", r=KT)
            for r in range(FT):
                for d in range(KT):
                    o = r * D + d * P
                    jobs.append((w2[:, d, r * P:(r + 1) * P], wdt[:, :, :].rearrange("p r n -> p (r n)")[:, o:min(o + 4 * P, FT * D)]))
            return jobs

        @block.sync
        def _(sp):
            credit(sp, (x_out[0], 16), (x_out[1], 16), (f_out[0], 16), (f_out[1], 16))
            for k in range(5):
                sp.dma_start(hp[:, k:k + 1], raw_d[k].rearrange("(h a) -> h a", a=1)).then_inc(p_load, 16)
            sp.dma_start(hp[:, 5:6], tau_d.rearrange("(h a) -> h a", a=1)).then_inc(p_load, 16)
            for k in range(4):
                sp.dma_start(om[:, k:k + 1], omega_d[4 * k:4 * k + 4, :].rearrange("a (d e) -> (a d) e", e=1)).then_inc(p_load, 16)
            for s in range(2):
                sp.dma_start(xraw[s], x_d[s].rearrange("(j p) n -> p j n", p=P)).then_inc(x_in[s], 16)
            raws = [wq_d.rearrange("(k p) n -> p k n", p=P), wk_d.rearrange("(k p) n -> p k n", p=P),
                    wv_d.rearrange("(k p) n -> p k n", p=P), None]

            def load_raw(m):
                dst = tabs[m % 2][:, 0:8, :].rearrange("p a n -> p (a n)")
                if m < 3:
                    sp.dma_start(dst.rearrange("p (k n) -> p k n", k=KT), raws[m]).then_inc(raww[m % 2], 16)
                else:
                    for c in range(2):
                        sp.dma_start(dst[c * DH:(c + 1) * DH, :].rearrange("p (h n) -> p h n", h=H),
                                     wo_d[c * DK:(c + 1) * DK, :].rearrange("(h d) n -> d h n", d=DH)
                                     ).then_inc(raww[1], 16)
            load_raw(0)
            load_raw(1)
            sp.dma_start(qkb[:, 0:3, :].rearrange("p a n -> p (a n)").bitcast(I32).rearrange("p (r n) -> p r n", r=FT),
                         wg_d.rearrange("(r p) n -> p r n", p=P)).then_inc(ffn_in, 16)
            sp.dma_start(qkb[:, 3:6, :].rearrange("p a n -> p (a n)").bitcast(I32).rearrange("p (r n) -> p r n", r=FT),
                         wu_d.rearrange("(r p) n -> p r n", p=P)).then_inc(ffn_in, 16)
            sp.dma_start(swt[:, 0:3, :].rearrange("p a n -> p (a n)").bitcast(I32).rearrange("p (r n) -> p r n", r=KT),
                         wd_d.rearrange("(r p) n -> p r n", p=P)).then_inc(ffn_in, 16)
            sp.wait_ge(p_dve, V_TABLES)
            for k in range(3):
                sp.dma_start(vec_d[k], (v_e, v_vn, v_t3)[k]).then_inc(vec_out, 16)
            sp.dma_start(nco_d.rearrange("a h -> h a"), hp[:, NCO:NCO + 1]).then_inc(vec_out, 16)
            sp.wait_ge(vec_out, 64)
            sp.dma_start(nco[:, :], bass.AP(tensor=nco_d.tensor, offset=0, ap=[[0, P], [1, H]])).then_inc(nco_in, 16)
            for g in range(G):
                for k in range(3):
                    src = bass.AP(tensor=vec_d.tensor, offset=(k * H + g * HH) * VEC + P - 1,
                                  ap=[[VEC, HH], [-1, P], [1, N]])
                    sp.dma_start(tab_d[g, :, :, k, :].rearrange("p h n -> h p n"), src).then_inc(tab_out, 16)
            for k in range(4):
                sp.wait_ge(p_dve, V_ROPE[k])
                for row in range(4):
                    h0 = 4 * k
                    for c, src in ((0, rope_cs[k]), (1, rope_sp[k] if row in (1, 2) else rope_sn[k])):
                        for a in range(2):
                            dst = rope_d[(h0 + 2 * a) // HH, row * 32:(row + 1) * 32, :, c, :]
                            sp.dma_start(dst.rearrange("d h n -> h d n"), src[a * 64:(a + 1) * 64, :]
                                         ).then_inc(rope_out, 16)
            for m in range(4):
                for s in range(4):
                    i = 4 * m + s
                    sp.wait_ge(split_lo, i + 1)
                    sp.wait_ge(split_hi, i + 1)
                    stage = wt[:, i % 2, 0:2048].bitcast(F32)
                    if m < 3:
                        kt, gh = s // 2, s % 2
                        dst = ws_d[4 * gh:4 * gh + 4].rearrange("g p (m r) -> p g m r", m=3 * KT)[:, :, m * KT + kt, :]
                        sp.dma_start(dst, stage.rearrange("p (g r) -> p g r", g=4)).then_inc(split_out[i % 2], 16)
                    else:
                        sp.dma_start(wos_d[2 * s:2 * s + 2].rearrange("g p r -> p g r"),
                                     stage.rearrange("p (g r) -> p g r", g=2)).then_inc(split_out[i % 2], 16)
                if m < 2:
                    load_raw(m + 2)
            def x_load(b, s):
                src = x_d[b].rearrange("(j p) n -> p j n", p=P) if isinstance(b, int) else \
                    x_d[bass.ds(b, 1)].rearrange("b (j p) n -> p (b j) n", p=P)
                sp.dma_start(xraw[s], src).then_inc(x_in[s], 16)

            def x_store(b, s):
                dst = xs_d[b] if isinstance(b, int) else xs_d[bass.ds(b, 1)].rearrange("b p n -> (b p) n")
                sp.dma_start(dst, xt[s][:, :, :, :].rearrange("p k s n -> p (k s n)").bitcast(F32)).then_inc(x_out[s], 16)

            with sp.Fori(0, B // 2 - 1) as i:
                off = [sp.snap(i * 2 + s) for s in range(2)]
                nxt = [sp.snap(i * 2 + s + 2) for s in range(2)]
                nrm = [sp.snap(i * 2 + s + 3) for s in range(2)]
                hlo = [sp.snap(i * 4 + 2 * s + 4) for s in range(2)]
                for s in range(2):
                    sp.wait_ge(x_norm, nrm[s])
                    x_load(nxt[s], s)
                    sp.wait_ge(x_hi, hlo[s])
                    sp.wait_ge(x_lo, hlo[s])
                    x_store(off[s], s)
            for s in range(2):
                sp.wait_ge(x_hi, 2 * (B - 2 + s) + 4)
                sp.wait_ge(x_lo, 2 * (B - 2 + s) + 4)
                x_store(B - 2 + s, s)
            sp.wait_ge(tab_out, 16 * 3 * G)
            sp.wait_ge(rope_out, 16 * 64)
            for s in range(2):
                sp.wait_ge(split_out[s], 16 * 8)
                sp.wait_ge(x_out[s], 16 * (B // 2 + 1))
            sp.wait_ge(ffn_tr, 9)

            def load_group(g, par):
                one = (lambda d: d[g] if isinstance(g, int) else d[bass.ds(g, 1)])
                def flat(d, pat, pat1):
                    return one(d).rearrange(pat if isinstance(g, int) else pat1)
                sp.dma_start(tabs[par][:, 0:3 * HH, :], flat(tab_d, "p h k n -> p (h k) n", "g p h k n -> (g p) (h k) n")).then_inc(grp[par], 16)
                sp.dma_start(tabs[par][:, 3 * HH:5 * HH, :], flat(rope_d, "p h k n -> p (h k) n", "g p h k n -> (g p) (h k) n")).then_inc(grp[par], 16)
                sp.dma_start(wt[:, par, :].bitcast(F32), flat(ws_d, "p r -> p r", "g p r -> (g p) r")).then_inc(grp[par], 16)
                sp.dma_start(wot[:, par, :].bitcast(F32), flat(wos_d, "p r -> p r", "g p r -> (g p) r")).then_inc(grp[par], 16)

            def load_x(b, s):
                src = xs_d[b] if isinstance(b, int) else xs_d[bass.ds(b, 1)].rearrange("b p n -> (b p) n")
                sp.dma_start(xt[s][:, :, :, :].rearrange("p k s n -> p (k s n)").bitcast(F32), src).then_inc(xt_in[s], 16)

            load_group(0, 0)
            load_x(0, 0)
            load_x(1, 1)
            load_group(1, 1)

            def sequences(t0, last):
                with sp.Fori(0, B // 2 - 1) as i:
                    for s in range(2):
                        nb = sp.snap(i * 2 + s + 2)
                        v = sp.snap((i * 2 + (t0 + (s + 1))) * 10 + 10)
                        sp.wait_ge(proj, v)
                        load_x(nb, s)
                if not last:
                    for s in range(2):
                        v = (t0 + (B - 1 + s)) * 10 + 10
                        sp.wait_ge(proj, v if isinstance(v, int) else sp.snap(v))
                        load_x(s, s)

            def refill(g, par, t0):
                v8, v2, vb = t0 * 8 + 8, t0 * 2 + 2, t0 * (2 * NPB) + 2 * NPB
                if not isinstance(t0, int):
                    v8, v2 = sp.snap(v8), sp.snap(v2)
                    vb = sp.snap(vb) if NPB else 0
                sp.wait_ge(f_dve, v8)
                sp.wait_ge(ek_pool, v8)
                if NPB:
                    sp.wait_ge(b_pool, vb)
                sp.wait_ge(o_rdy, v2)
                load_group(g, par)

            sequences(0, False)
            with sp.Fori(0, G // 2 - 1) as gg:
                g2 = sp.snap(gg * 2 + 2)
                g3 = sp.snap(gg * 2 + 3)
                ta = sp.snap(gg * (2 * B) + B)
                tb = sp.snap(gg * (2 * B) + 2 * B)
                refill(g2, 0, ta)
                sequences(ta, False)
                refill(g3, 1, tb)
                sequences(tb, False)
            sequences((G - 1) * B, True)

            def f_load(b, s):
                src = x_d[b].rearrange("(j p) n -> p j n", p=P) if isinstance(b, int) else \
                    x_d[bass.ds(b, 1)].rearrange("b (j p) n -> p (b j) n", p=P)
                sp.dma_start(f_xin[s], src).then_inc(f_x[s], 16)

            def f_store(b, s):
                dst = out_d[b].rearrange("(j p) n -> p j n", p=P) if isinstance(b, int) else \
                    out_d[bass.ds(b, 1)].rearrange("b (j p) n -> p (b j) n", p=P)
                sp.dma_start(dst, f_outs[s]).then_inc(f_out[s], 16)

            sp.wait_ge(f_dve, 8 * B * G + 8)
            sp.wait_ge(ek_pool, 8 * B * G + 8)
            f_load(0, 0)
            f_load(1, 1)
            with sp.Fori(0, B // 2 - 1) as i:
                off = [sp.snap(i * 2 + s) for s in range(2)]
                nxt = [sp.snap(i * 2 + s + 2) for s in range(2)]
                cnt = [sp.snap(i * 2 + s + 3) for s in range(2)]
                for s in range(2):
                    sp.wait_ge(f_norm, cnt[s])
                    f_load(nxt[s], s)
                    sp.wait_ge(f_res, cnt[s])
                    f_store(off[s], s)
            for s in range(2):
                sp.wait_ge(f_res, B - 2 + s + 3)
                f_store(B - 2 + s, s)
            for s in range(2):
                sp.wait_ge(f_out[s], 16 * (B // 2 + 1))

        @block.gpsimd
        def _(pool):
            credit(pool, (ek_pool, 8), (b_pool, 2 * NPB), (t2_pool, 4))
            pool.memset(ident[:, :], 0.0).then_inc(consts, 1)
            pool.memset(ones[:, :], 1.0).then_inc(consts, 1)
            pool.memset(mhalf[:, :], -0.5).then_inc(consts, 1)
            pool.iota(dist, pattern=[[-1, VEC]], base=N - 1, channel_multiplier=0,
                      allow_small_or_imprecise_dtypes=True).then_inc(consts, 1)
            pool.iota(tokens, pattern=[[1, N]], base=0, channel_multiplier=0,
                      allow_small_or_imprecise_dtypes=True).then_inc(consts, 1)
            pool.wait_ge(consts, 5)
            pool.affine_select(out=ident[:, :], in_=ident[:, :], compare_op=ALU.not_equal, fill=1.0,
                               base=0, pattern=[[-1, P]], channel_multiplier=1).then_inc(consts, 1)


            def root(chain, v, mark):
                pool.wait_ge(chain, v)
                pool.tensor_tensor(rstd[:, :], rstd[:, :], mhalf[:, :], ALU.pow).then_inc(mark, 1)

            credit(pool, (x_root, 1), (f_root, 2), (f_rootb, 1))
            with pool.Fori(0, B) as b:
                root(x_ln, pool.snap(b * 3 + 3 + 3), x_root)

            pool.wait_ge(vec_out, 64)
            pool.wait_ge(rope_out, 16 * 64)
            pool.memset(accf, 0.0).then_inc(consts, 1)

            def rope_sin(c, hh, par):
                for m in range(2):
                    pool.wait_ge(pa_act, c[8] + 3 * hh + m + 1)
                    pool.wait_ge(rope, c[4] + 2 * hh + m + 1 - 2)
                    pool.tensor_tensor(swt[:, 2 + m, :], swt[:, m, :], ropet(par, hh, 1), ALU.mult).then_inc(t2_pool, 1)

            def decay_norm(c, hh, n, par):
                i, m = n % 2, 4 * hh + n
                w = width(n)
                if n == 0:
                    pool.wait_ge(pa_act, c[8] + 3 * hh + 3)
                pool.wait_ge(a_dve, c[8] + m + 1 - 2)
                pool.tensor_tensor(ek[:, i, 0:w], tab(par, hh, E_T, N - w), qkb[:, 3 * hh + 2, 0:w],
                                   ALU.mult).then_inc(ek_pool, 1)

            def times_decay(c, hh, n, par):
                m, w = 4 * hh + n, width(n)
                pool.wait_ge(a_dve, c[8] + m + 1)
                pool.tensor_tensor(lg[:, hh, at(n)], lg[:, hh, at(n)], tab(par, hh, E_T, N - w), ALU.mult).then_inc(b_pool, 1)

            def ahead(c, hh, par):
                rope_sin(c, hh, par)
                decay_norm(c, hh, 0, par)
                decay_norm(c, hh, 1, par)

            def unit(c, hh, par):
                for n in POOL_SCALES:
                    times_decay(c, hh, n, par)
                decay_norm(c, hh, 2, par)
                decay_norm(c, hh, 3, par)

            def body(it):
                c = counts(pool, it.t, (8, 4))
                unit(c, 0, it.par)
                ahead(c, 1, it.par)
                unit(c, 1, it.par)
                if it.behind is not None:
                    if it.opens is not None:
                        pool.wait_ge(grp[it.behind], it.opens)
                    ahead(following(c), 0, it.behind)

            pool.wait_ge(grp[0], 64)
            ahead(counts(pool, 0, (8, 4)), 0, 0)
            run_iterations(pool, body)

            credit(pool, (f_hl, FT))

            def hidden_low(c, r):
                pool.wait_ge(f_hh, c[FT] + r + 1)
                if r == 0:
                    pool.wait_ge(f_dn, c[2])
                pool.tensor_tensor(hpart(r, 1), f_hid(r), hpart(r, 0).bitcast(F32), ALU.subtract).then_inc(f_hl, 1)

            def f_body(b, nxt):
                c = counts(pool, b, (FT, 8, 4, 2))
                hidden_low(c, 0)
                if nxt:
                    root(f_ln, c[8] + 8 + 3, f_root)
                hidden_low(c, 1)
                if nxt:
                    root(f_ln, c[8] + 8 + 8, f_root)
                for r in range(2, FT):
                    hidden_low(c, r)
                root(f_l3, c[4] + 3, f_rootb)

            root(f_ln, 8 + 3, f_root)
            root(f_ln, 8 + 8, f_root)
            with pool.Fori(0, B - 1) as b:
                f_body(b, True)
            f_body(B - 1, False)

        @block.tensor
        def _(pe):
            credit(pe, (proj, 10), (s_rdy, 8), (tr_rdy, 8), (av_rdy, 8), (yt_rdy, 2), (o_rdy, 2), (x_tr, 2))
            mm = pe.matmul
            pe.wait_ge(consts, 6)
            jobs = ffn_jobs()
            pe.wait_ge(ffn_cast, 3)
            for n in range(9):
                if n >= 2:
                    pe.wait_ge(ffn_ev, n - 1)
                for k, (src, _) in enumerate(jobs[4 * n:4 * n + 4]):
                    last = pe.transpose(ps[n % 2][:, k * P:(k + 1) * P], src, ident[:, :])
                last.then_inc(ffn_tr, 1)

            with pe.Fori(0, B // 2) as i:
                for s in range(2):
                    nrm = pe.snap(i * 2 + s + 3)
                    c = pe.snap(i * 4 + 2 * s + 2)
                    pe.wait_ge(x_norm, nrm)
                    for kt in range(KT):
                        pe.wait_ge(x_hi, c + kt + 1 - 2)
                        pe.wait_ge(x_lo, c + kt + 1 - 2)
                        for j in range(NT):
                            last = pe.transpose(pp[kt][:, j * P:(j + 1) * P], xnorm[s][:, j, kt * P:(kt + 1) * P],
                                                ident[:, :])
                        last.then_inc(x_tr, 1)

            def project(half, c, hh, par, slot, m):
                if hh == 0 and m == 0:
                    v = (half + 1) * 16
                    pe.wait_ge(xt_in[slot], v if isinstance(v, int) else pe.snap(v))
                if hh == 0:
                    pe.wait_ge(pa_act, c[8] + 7 + m - 8)
                elif m == 0:
                    pe.wait_ge(pa_act, c[8] + 3)
                else:
                    pe.wait_ge(pa_dve, c[6] + 3)
                n = 0
                for kt in range(KT):
                    for a, b in PARTS:
                        last = mm(pa[m][:, :], wproj(par, m, kt, a, hh * P, (hh + 1) * P), xt[slot][:, kt, b, :],
                                  start=(n == 0), stop=(n == 3 * KT - 1))
                        n += 1
                last.then_inc(proj, 1)

            def norm_k(c, hh):
                pe.wait_ge(pa_act, c[8] + 3 * hh + 2)
                pe.wait_ge(pa_dve, c[6] + 3 * hh + 1)
                mm(pa[0][:, :], ones[:, :], sq[:, 1, :], start=True, stop=True).then_inc(proj, 1)

            def norm_q(c, hh):
                pe.wait_ge(pa_dve, c[6] + 3 * hh + 2)
                for i in range(NT):
                    last = mm(pa[1][:, i:i + 1], sq[:, 0, i * P:(i + 1) * P], ones[:, 0:1], start=True, stop=True)
                last.then_inc(proj, 1)

            def values(c, par, slot):
                for half in range(2):
                    if half == 0:
                        pe.wait_ge(pa_act, c[8] + 6)
                    else:
                        pe.wait_ge(pa_dve, c[6] + 6)
                    for jj in range(2):
                        j = 2 * half + jj
                        n = 0
                        for kt in range(KT):
                            for a, b in PARTS:
                                last = mm(pa[half][:, jj * W2:(jj + 1) * W2], xt[slot][:, kt, a, j * P:(j + 1) * P],
                                          wproj(par, 2, kt, b, 0, W2), start=(n == 0), stop=(n == 3 * KT - 1))
                                n += 1
                    last.then_inc(proj, 1)

            def scores(c, hh, n):
                i, m = n % 2, 4 * hh + n
                w = width(n)
                if n == 0:
                    pe.wait_ge(rope, c[4] + 2 * hh + 2)
                pe.wait_ge(a_dve, c[8] + m + 1 - 2)
                mm(ps[i][:, 0:w], qkb[:, 3 * hh, TILES[n] * P:(TILES[n] + 1) * P], qkb[:, 3 * hh + 1, 0:w],
                   start=True, stop=True).then_inc(s_rdy, 1)

            def turn(c, hh, n):
                i, m = n % 2, 4 * hh + n
                pe.wait_ge(ex_act, c[8] + m + 1)
                pe.wait_ge(pt_act, c[8] + m + 1 - 2)
                for j in range(TILES[n] + 1):
                    o = at(n).start + j * P
                    last = pe.transpose(pp[i][:, j * P:(j + 1) * P], pr[:, o:o + P], ident[:, :])
                last.then_inc(tr_rdy, 1)

            def attend(c, hh, n):
                i, m = n % 2, 4 * hh + n
                I = TILES[n]
                pe.wait_ge(pt_act, c[8] + m + 1)
                if n == 0:
                    pe.wait_ge(pa_act, c[8] + 8)
                    if hh == 0:
                        pe.wait_ge(acc_dve, c[2] + 2 - 2)
                    pe.wait_ge(y_dve, c[2] + hh + 1 - 1)
                for j in range(I + 1):
                    last = mm(py[:, I * P:(I + 1) * P], pt[:, i, j * P:(j + 1) * P], vt[:, j, hh * P:(hh + 1) * P],
                              start=(j == 0), stop=(j == I))
                last.then_inc(av_rdy, 1)

            def turn_y(c, hh):
                pe.wait_ge(y_dve, c[2] + hh + 1)
                if hh == 0:
                    pe.wait_ge(acc_dve, c[2] + 1 - 2)
                else:
                    pe.wait_ge(yl_dve, c[2] + 1)
                for j in range(NT):
                    last = pe.transpose(po[:, j * P:(j + 1) * P], ysb[:, j, :], ident[:, :])
                last.then_inc(yt_rdy, 1)

            def out_project(c, par):
                pe.wait_ge(yl_dve, c[2] + 2)
                for half, dst in enumerate((po, py)):
                    for jj in range(2):
                        j = 2 * half + jj
                        n = 0
                        for hh in range(HH):
                            for a, b in PARTS:
                                last = mm(dst[:, jj * D:(jj + 1) * D], yhl[:, hh, a, j * P:(j + 1) * P],
                                          wot[:, par, (hh * 2 + b) * D:(hh * 2 + b + 1) * D],
                                          start=(n == 0), stop=(n == 3 * HH - 1))
                                n += 1
                    last.then_inc(o_rdy, 1)

            def unit(c, hh, old, nxt, mid=(), end=()):
                def turned(n):
                    if old:
                        turn(*old, n)

                def attended(n):
                    if old:
                        attend(*old, n)
                scores(c, hh, 0)
                scores(c, hh, 1)
                for f in mid:
                    f()
                if nxt:
                    project(*nxt, 0)
                turned(0)
                turned(1)
                scores(c, hh, 2)
                if nxt:
                    project(*nxt, 1)
                attended(0)
                turned(2)
                scores(c, hh, 3)
                attended(1)
                turned(3)
                attended(2)
                if nxt:
                    norm_k(nxt[1], nxt[2])
                attended(3)
                if nxt:
                    norm_q(nxt[1], nxt[2])
                for f in end:
                    f()
                if old:
                    turn_y(*old)

            PERS = (8, 6, 4, 2)

            def body(it):
                c = counts(pe, it.t, PERS)
                cp, cn = previous(c), following(c)
                unit(c, 0, None if it.before is None else (cp, 1), (it.half, c, 1, it.par, it.slot),
                     end=[lambda: values(c, it.par, it.slot)])
                if it.opens is not None:
                    pe.wait_ge(grp[it.behind], it.opens)
                half = it.half + it.slot
                unit(c, 1, (c, 0), None if it.behind is None else (half, cn, 0, it.behind, 1 - it.slot),
                     mid=[] if it.before is None else [lambda: out_project(cp, it.before)])

            pe.wait_ge(grp[0], 64)
            c0 = counts(pe, 0, PERS)
            project(0, c0, 0, 0, 0, 0)
            project(0, c0, 0, 0, 0, 1)
            norm_k(c0, 0)
            norm_q(c0, 0)
            run_iterations(pe, body)
            c = counts(pe, G * B - 1, PERS)
            for n in range(NT):
                turn(c, 1, n)
                attend(c, 1, n)
            turn_y(c, 1)
            out_project(c, 1)

            credit(pe, (f_tr, 2), (f_g, FT), (f_u, FT), (f_dn, 2))

            def f_transposes(c, s):
                pe.wait_ge(f_norm, c[1] + 2)
                for kt in range(KT):
                    pe.wait_ge(f_hi, c[2] + kt + 1 - 2)
                    pe.wait_ge(f_lo, c[2] + kt + 1 - 2)
                    for j in range(NT):
                        last = pe.transpose(pp[kt][:, j * P:(j + 1) * P], f_nrm[:, j, kt * P:(kt + 1) * P], ident[:, :])
                    last.then_inc(f_tr, 1)

            def gate_up(c, s, r):
                i = r % 2
                if r == 0:
                    pe.wait_ge(f_hi, c[2] + 2)
                    pe.wait_ge(f_lo, c[2] + 2)
                for dst, w, free, done in ((pa, wgt, f_silu, f_g), (ps, wut, f_h, f_u)):
                    pe.wait_ge(free, c[FT] + r + 1 - 2)
                    n = 0
                    for kt in range(KT):
                        for a in range(2):
                            last = mm(dst[i][:, :], w[:, kt, r * P:(r + 1) * P], xt[s][:, kt, a, :],
                                      start=(n == 0), stop=(n == 2 * KT - 1))
                            n += 1
                    last.then_inc(done, 1)

            def down(c):
                for half, dst in enumerate((py, po)):
                    pe.wait_ge(f_ev, c[2] + half + 1 - 2)
                    if half == 0:
                        pe.wait_ge(f_hl, c[FT] + FT)
                    for jj in range(2):
                        j = 2 * half + jj
                        n = 0
                        for r in range(FT):
                            for a in range(2):
                                last = mm(dst[:, jj * D:(jj + 1) * D], hpart(r, a)[:, j * P:(j + 1) * P], wdt[:, r, :],
                                          start=(n == 0), stop=(n == 2 * FT - 1))
                                n += 1
                    last.then_inc(f_dn, 1)

            def f_body(b, s, nxt):
                c = counts(pe, b, (FT, 2, 1))
                for r in range(FT):
                    gate_up(c, s, r)
                if nxt:
                    f_transposes({p: v + p for p, v in c.items()}, 1 - s)
                down(c)

            f_transposes(counts(pe, 0, (FT, 2, 1)), 0)
            with pe.Fori(0, B // 2 - 1) as i:
                f_body(pe.snap(i * 2), 0, True)
                f_body(pe.snap(i * 2 + 1), 1, True)
            f_body(B - 2, 0, True)
            f_body(B - 1, 1, False)

        @block.scalar
        def _(act):
            credit(act, (pa_act, 8), (ln_act, 8), (ex_act, 8), (pt_act, 8), (yh_act, 2), (x_hi, 2))
            n_act = [0]

            def a_step(ins):
                n_act[0] += 1
                ins.then_inc(p_act, 1)
                act.wait_ge(p_act, n_act[0])

            act.wait_ge(p_load, 16 * 10)
            a_step(act.activation(hp[:, 6:11], hp[:, 0:5], ACT.Abs))
            a_step(act.activation(hp[:, 11:16], hp[:, 6:11], ACT.Exp, scale=-1.0))
            a_step(act.activation(hp[:, 16:21], hp[:, 11:16], ACT.Ln, bias=1.0))
            act.wait_ge(p_dve, V_EXP)
            a_step(act.activation(v_e, v_e, ACT.Exp))
            act.wait_ge(p_dve, V_LN)
            a_step(act.activation(v_lnv, v_v, ACT.Ln))
            a_step(act.activation(v_t3, v_vn, ACT.Ln))
            for k in range(4):
                act.wait_ge(p_dve, V_ANGLE[k])
                a_step(act.activation(rope_sp[k], ang, ACT.Sin))
                a_step(act.activation(half_sin, ang, ACT.Sin, scale=0.5))
            for m in range(4):
                for s in range(4):
                    i = 4 * m + s
                    if s == 0:
                        act.wait_ge(raww[m % 2], (16, 16, 32, 48)[m])
                    if i >= 2:
                        act.wait_ge(split_out[i % 2], 16 * (i // 2))
                    for hi, lo, raw in split_views(m, s):
                        last = act.activation(hi, raw, ACT.Copy)
                    last.then_inc(split_hi, 1)
            jobs = ffn_jobs()
            for n in range(9):
                act.wait_ge(ffn_tr, n + 1)
                act.activation(jobs[4 * n][1], ps[n % 2][:, :], ACT.Copy).then_inc(ffn_ev, 1)
            with act.Fori(0, B // 2) as i:
                c16 = act.snap(i * 16 + 16)
                for s in range(2):
                    c = act.snap(i * 4 + 2 * s + 2)
                    for kt in range(KT):
                        act.wait_ge(x_tr, c + kt + 1)
                        if kt == 0:
                            act.wait_ge(x_out[s], c16)
                        act.activation(xt[s][:, kt, 0, :], pp[kt][:, :], ACT.Copy).then_inc(x_hi, 1)

            def swap(c, hh, m):
                act.wait_ge(proj, c[10] + 4 * hh + 1 + m)
                act.wait_ge(t2_pool, c[4] + 2 * hh + m + 1 - 2)
                act.activation(sq[:, m, :], pa[m][:, :], ACT.Square)
                scale = -2.0 if m == 0 else 1.0
                act.activation(swt[0:DH, m, :], pa[m][DH:P, :], ACT.Copy, scale=scale)
                act.activation(swt[DH:P, m, :], pa[m][0:DH, :], ACT.Copy, scale=scale).then_inc(pa_act, 1)

            def keep_norm_k(c, hh):
                act.wait_ge(proj, c[10] + 4 * hh + 3)
                act.wait_ge(ek_pool, c[8] + 4 * hh + 4 - 8)
                act.activation(qkb[:, 3 * hh + 2, :], pa[0][:, :], ACT.Copy).then_inc(pa_act, 1)

            def keep_values(c):
                for half in range(2):
                    act.wait_ge(proj, c[10] + 9 + half)
                    if half == 0:
                        act.wait_ge(av_rdy, c[8] + 8 - 8)
                    act.activation(vt[:, 2 * half:2 * half + 2, :].rearrange("p a n -> p (a n)"), pa[half][:, :],
                                   ACT.Copy).then_inc(pa_act, 1)

            def log(c, hh, n):
                m = 4 * hh + n
                act.wait_ge(cd_dve, c[8] + m + 1)
                act.activation(lg[:, hh, at(n)], lg[:, hh, at(n)], ACT.Ln,
                               bias=qn[:, hh, 0, TILES[n]:TILES[n] + 1]).then_inc(ln_act, 1)

            def exp(c, hh, n):
                m, q = 4 * hh + n, NT * hh + TILES[n]
                act.wait_ge(f_dve, c[8] + m + 1)
                act.wait_ge(tr_rdy, c[8] + m + 1 - 4)
                act.activation(pr[:, at(n)], lg[:, hh, at(n)], ACT.Exp, bias=nmax[:, q:q + 1], scale=-1.0,
                               accum_out=den[:, q:q + 1]).then_inc(ex_act, 1)

            def keep_turned(c, hh, n):
                i, m = n % 2, 4 * hh + n
                w = width(n)
                act.wait_ge(tr_rdy, c[8] + m + 1)
                act.wait_ge(av_rdy, c[8] + m + 1 - 2)
                act.activation(pt[:, i, 0:w], pp[i][:, 0:w], ACT.Copy).then_inc(pt_act, 1)

            def y_high(c, hh):
                act.wait_ge(yt_rdy, c[2] + hh + 1)
                if hh == 0:
                    act.wait_ge(o_rdy, c[2] + 2 - 2)
                act.activation(yhl[:, hh, 0, :], po[:, :], ACT.Copy).then_inc(yh_act, 1)

            def unit(c, hh, old, nxt, end=()):
                def turned(n):
                    if old:
                        keep_turned(*old, n)
                if nxt:
                    swap(*nxt, 0)
                turned(0)
                log(c, hh, 0)
                turned(1)
                log(c, hh, 1)
                if nxt:
                    swap(*nxt, 1)
                turned(2)
                log(c, hh, 2)
                turned(3)
                log(c, hh, 3)
                exp(c, hh, 0)
                if nxt:
                    keep_norm_k(*nxt)
                exp(c, hh, 1)
                exp(c, hh, 2)
                exp(c, hh, 3)
                for f in end:
                    f()
                if old:
                    y_high(*old)

            PERS = (10, 8, 4, 2)

            def body(it):
                c = counts(act, it.t, PERS)
                unit(c, 0, None if it.before is None else (previous(c), 1), (c, 1), end=[lambda: keep_values(c)])
                unit(c, 1, (c, 0), None if it.behind is None else (following(c), 0))

            c0 = counts(act, 0, PERS)
            swap(c0, 0, 0)
            swap(c0, 0, 1)
            keep_norm_k(c0, 0)
            run_iterations(act, body)
            c = counts(act, G * B - 1, PERS)
            for n in range(NT):
                keep_turned(c, 1, n)
            y_high(c, 1)

            credit(act, (f_hi, 2), (f_silu, FT), (f_hh, FT), (f_ev, 2))

            def f_high(c, s):
                for kt in range(KT):
                    act.wait_ge(f_tr, c[2] + kt + 1)
                    if kt == 0:
                        act.wait_ge(f_u, c[FT])
                    act.activation(xt[s][:, kt, 0, :], pp[kt][:, :], ACT.Copy).then_inc(f_hi, 1)

            def silu(c, r):
                act.wait_ge(f_g, c[FT] + r + 1)
                act.wait_ge(f_h, c[FT] + r + 1 - 2)
                act.activation(f_gate(r), pa[r % 2][:, :], ACT.Silu, scale=SCALE).then_inc(f_silu, 1)

            def hidden_high(c, r):
                act.wait_ge(f_h, c[FT] + r + 1)
                if r == 0:
                    act.wait_ge(f_dn, c[2] + 2 - 2)
                act.activation(hpart(r, 0), f_hid(r), ACT.Copy).then_inc(f_hh, 1)

            def f_body(b, s, nxt):
                c = counts(act, b, (FT, 2, 1))
                silu(c, 0)
                for r in range(1, FT):
                    silu(c, r)
                    hidden_high(c, r - 1)
                hidden_high(c, FT - 1)
                if nxt:
                    f_high({p: v + p for p, v in c.items()}, 1 - s)
                for half, src in enumerate((py, po)):
                    act.wait_ge(f_dn, c[2] + half + 1)
                    act.wait_ge(f_res, c[1] + 1)
                    act.activation(f_y[:, 2 * half:2 * half + 2, :], src[:, :].rearrange("p (j n) -> p j n", j=2),
                                   ACT.Copy, scale=SCALE).then_inc(f_ev, 1)

            act.preload_act_table(ACT.Silu)
            f_high(counts(act, 0, (FT, 2)), 0)
            with act.Fori(0, B // 2 - 1) as i:
                f_body(act.snap(i * 2), 0, True)
                f_body(act.snap(i * 2 + 1), 1, True)
            f_body(B - 2, 0, True)
            f_body(B - 1, 1, False)

        @block.vector
        def _(dve):
            credit(dve, (pa_dve, 6), (rope, 4), (a_dve, 8), (b_dve, 8 - 2 * NPB), (cd_dve, 8), (f_dve, 8), (rd_dve, 2),
                   (y_dve, 2), (yl_dve, 2), (acc_dve, 2), (x_norm, 2), (x_lo, 2), (x_ln, 3))
            tt, ts, stt, rec = dve.tensor_tensor, dve.tensor_scalar, dve.scalar_tensor_tensor, dve.reciprocal
            done = [0]

            def step(ins):
                done[0] += 1
                ins.then_inc(p_dve, 1)
                dve.wait_ge(p_dve, done[0])

            def settle(v):
                if not isinstance(v, int):
                    dve.sem_inc(settled, 1)

            def col(k, n=1):
                return hp[:, k:k + n]
            MU, TAU, E0 = 0, 5, 11
            SP, NMU, C1, C2, RL, RB = 26, 36, 37, 38, 23, 24
            dve.wait_ge(p_load, 16 * 10)
            dve.wait_ge(p_act, 3)
            step(ts(col(21, 5), col(0, 5), 0.0, None, ALU.max))
            step(tt(col(SP, 5), col(21, 5), col(16, 5), ALU.add))
            step(ts(col(31), col(MU), 0.0, None, ALU.is_ge))
            step(tt(col(32), col(31), col(E0), ALU.max))
            step(ts(col(33), col(E0), 1.0, None, ALU.add))
            step(rec(col(34), col(33)))
            step(stt(col(35), col(32), 1.0, col(34), ALU.mult, ALU.mult))
            step(ts(col(35), col(35), EPS_MU, None, ALU.add))
            step(ts(col(NMU), col(35), -1.0, None, ALU.mult))
            step(ts(col(39), col(35), 2.0, None, ALU.mult))
            step(rec(col(39), col(39)))
            step(tt(col(C1), col(SP + 1), col(39), ALU.mult))
            step(tt(col(C2), col(SP + 2), col(SP + 3), ALU.add))
            step(ts(col(21), col(SP + 4), float(DH), -0.5, ALU.add, ALU.mult))
            dve.wait_ge(consts, 5)
            step(ts(v_e, dist, 0.0, None, ALU.max))
            step(ts(v_e, v_e, col(NMU), MIN_EXP, ALU.mult, ALU.max))
            step(ts(v_e, v_e, 0.0, None, ALU.min))
            dve.wait_ge(p_act, 4)
            step(tt(v_v, v_e, v_e, ALU.mult))
            step(ts(v_v, v_v, -1.0, 1.0, ALU.mult, ALU.add))
            step(ts(v_v, v_v, col(C1), col(C2), ALU.mult, ALU.add))
            step(ts(v_vn, v_v, col(SP + 4), None, ALU.mult))
            step(tt(col(22), col(21), col(TAU), ALU.mult))
            step(ts(col(21), col(22), 0.0, 1e-20, ALU.is_equal, ALU.mult))
            step(tt(col(22), col(22), col(21), ALU.add))
            step(rec(col(25), col(22)))
            step(ts(col(NCO), col(22), -1.0, None, ALU.mult))
            step(ts(col(RL), col(25), -0.5 * DH, None, ALU.mult))
            step(ts(col(RB), col(25), -BIG, None, ALU.mult))
            dve.wait_ge(p_act, 6)
            step(stt(v_t3, v_lnv, col(RL), v_t3, ALU.mult, ALU.subtract))
            step(ts(v_t3[:, N:VEC], v_t3[:, N:VEC], col(RB), None, ALU.add))
            assert done[0] == V_TABLES, done
            TWO_PI = (6.28125, 1.9350051879882812e-3, 3.0199159819567529e-7)
            for k in range(4):
                step(ts(ang, tokens, om[:, k:k + 1], None, ALU.mult))
                step(ts(turns, ang, 1.0 / (2 * math.pi), MAGIC, ALU.mult, ALU.add))
                step(ts(turns, turns, MAGIC, None, ALU.subtract))
                for c in TWO_PI:
                    step(stt(ang, turns, -c, ang, ALU.mult, ALU.add))
                step(ts(ang, ang, 3.1415925, -3.1415925, ALU.min, ALU.max))
                dve.wait_ge(p_act, 8 + 2 * k)
                step(ts(rope_sn[k], rope_sp[k], -1.0, None, ALU.mult))
                step(tt(half_sin, half_sin, half_sin, ALU.mult))
                step(ts(rope_cs[k], half_sin, -2.0, 1.0, ALU.mult, ALU.add))
                assert done[0] == V_ROPE[k]
            dve.wait_ge(ffn_in, 48)
            for z in (qkb[:, 0:3, :], qkb[:, 3:6, :], swt[:, 0:3, :]):
                dve.tensor_copy(z, z.bitcast(I32)).then_inc(ffn_cast, 1)
            for m in range(4):
                for s in range(4):
                    dve.wait_ge(split_hi, 4 * m + s + 1)
                    for hi, lo, raw in split_views(m, s):
                        last = tt(lo, raw, hi.bitcast(F32), ALU.subtract)
                    last.then_inc(split_lo, 1)

            def norm(src, dst, chain, c, k, made, v, mark):
                for j in range(NT):
                    last = dve.bn_stats(stats[:, j, :], src(j))
                last.then_inc(chain, 1)
                dve.wait_ge(chain, c + k + 1)
                settle(c)
                for j in range(NT):
                    last = dve.bn_aggr(mv[:, j, :], stats[:, j, :])
                last.then_inc(chain, 1)
                dve.wait_ge(chain, c + k + 2)
                ts(rstd[:, :], mv[:, :, 1], EPS_LN, None, ALU.add).then_inc(chain, 1)
                dve.wait_ge(made, v)
                for j in range(NT):
                    last = ts(dst(j), src(j), mv[:, j, 0:1], rstd[:, j:j + 1], ALU.subtract, ALU.mult)
                last.then_inc(mark, 1)

            with dve.Fori(0, B // 2) as i:
                i16 = dve.snap(i * 16 + 16)
                for s in range(2):
                    c3 = dve.snap(i * 6 + 3 * s + 3)
                    c1 = dve.snap(i * 2 + s + 2)
                    c2 = dve.snap(i * 4 + 2 * s + 2)
                    dve.wait_ge(x_in[s], i16)
                    dve.wait_ge(x_tr, c2)
                    norm(lambda j: xraw[s][:, j, :], lambda j: xnorm[s][:, j, :], x_ln, c3, 0, x_root, c1, x_norm)
                    for kt in range(KT):
                        dve.wait_ge(x_hi, c2 + kt + 1)
                        tt(xt[s][:, kt, 1, :], pp[kt][:, :], xt[s][:, kt, 0, :].bitcast(F32), ALU.subtract).then_inc(x_lo, 1)

            def rotate(c, hh, par, m):
                dve.wait_ge(pa_act, c[8] + 3 * hh + 1 + m)
                dst = qkb[:, 3 * hh + m, :]
                if m == 0:
                    stt(dst, pa[0][:, :], -2.0, ropet(par, hh, 0), ALU.mult, ALU.mult).then_inc(pa_dve, 1)
                else:
                    tt(dst, pa[1][:, :], ropet(par, hh, 0), ALU.mult).then_inc(pa_dve, 1)

            def rotated(c, hh, m):
                dst = qkb[:, 3 * hh + m, :]
                dve.wait_ge(pa_dve, c[6] + 3 * hh + m + 1)
                dve.wait_ge(t2_pool, c[4] + 2 * hh + m + 1)
                tt(dst, dst, swt[:, 2 + m, :], ALU.add).then_inc(rope, 1)

            def keep_norm_q(c, hh):
                dve.wait_ge(proj, c[10] + 4 * hh + 4)
                dve.tensor_copy(qn[:, hh, 0, :], pa[1][:, 0:NT])
                ts(qn[:, hh, 1, :], pa[1][:, 0:NT], -1.0, None, ALU.mult).then_inc(pa_dve, 1)

            def distance_a(c, hh, n):
                i, m, w = n % 2, 4 * hh + n, width(n)
                dve.wait_ge(s_rdy, c[8] + m + 1)
                dve.wait_ge(ek_pool, c[8] + m + 1)
                dve.wait_ge(ex_act, c[8] + m + 1 - 8)
                tt(lg[:, hh, at(n)], ps[i][:, 0:w], ek[:, i, 0:w], ALU.add).then_inc(a_dve, 1)

            def distance_b(c, hh, n, par):
                if n in POOL_SCALES:
                    return
                m, w = 4 * hh + n, width(n)
                dve.wait_ge(a_dve, c[8] + m + 1)
                tt(lg[:, hh, at(n)], lg[:, hh, at(n)], tab(par, hh, E_T, N - w), ALU.mult).then_inc(b_dve, 1)

            def distance_c(c, hh, n, par):
                w = width(n)
                before = sum(1 for q in POOL_SCALES if q <= n)
                if n in POOL_SCALES:
                    dve.wait_ge(b_pool, c[2] * NPB + NPB * hh + before)
                else:
                    dve.wait_ge(b_dve, c[2] * (4 - NPB) + (4 - NPB) * hh + n + 1 - before)
                stt(lg[:, hh, at(n)], lg[:, hh, at(n)], qn[:, hh, 1, TILES[n]:TILES[n] + 1], tab(par, hh, VN_T, N - w),
                    ALU.max, ALU.add).then_inc(cd_dve, 1)

            def logits(c, hh, n, par):
                m, w, q = 4 * hh + n, width(n), NT * hh + TILES[n]
                dve.wait_ge(ln_act, c[8] + m + 1)
                settle(c[8])
                dve.tensor_tensor_reduce(lg[:, hh, at(n)], lg[:, hh, at(n)], tab(par, hh, T3_T, N - w), ncog[:, par, hh:hh + 1],
                                         3e38, ALU.add, ALU.min, nmax[:, q:q + 1]).then_inc(f_dve, 1)

            def keep_y(c, hh):
                dve.wait_ge(ex_act, c[8] + 4 * hh + 4)
                rec(rden[:, NT * hh:NT * hh + NT], den[:, NT * hh:NT * hh + NT]).then_inc(rd_dve, 1)
                dve.wait_ge(rd_dve, c[2] + hh + 1)
                dve.wait_ge(av_rdy, c[8] + 4 * hh + 4)
                dve.wait_ge(yt_rdy, c[2] + hh + 1 - 1)
                tt(ysb[:, :, :], py[:, :].rearrange("p (j n) -> p j n", j=NT),
                   rden[:, NT * hh:NT * hh + NT].unsqueeze(2).broadcast_to([P, NT, P]), ALU.mult).then_inc(y_dve, 1)

            def y_low(c, hh):
                dve.wait_ge(yh_act, c[2] + hh + 1)
                tt(yhl[:, hh, 1, :], po[:, :], yhl[:, hh, 0, :].bitcast(F32), ALU.subtract).then_inc(yl_dve, 1)

            def add_output(c, b):
                for half, src in enumerate((po, py)):
                    dve.wait_ge(o_rdy, c[2] + half + 1)
                    if isinstance(b, int):
                        dst = accf[:, b * NT * D + half * N:b * NT * D + half * N + N]
                    else:
                        dst = accf[:, bass.ds(b * (NT * D) + half * N, N)]
                    tt(dst, dst, src[:, :], ALU.add).then_inc(acc_dve, 1)

            def unit(c, hh, par, old, nxt, mid=()):
                distance_a(c, hh, 0)
                distance_a(c, hh, 1)
                for f in mid:
                    f()
                if nxt:
                    rotate(*nxt, 0)
                distance_b(c, hh, 0, par)
                distance_b(c, hh, 1, par)
                distance_c(c, hh, 0, par)
                distance_c(c, hh, 1, par)
                distance_a(c, hh, 2)
                distance_a(c, hh, 3)
                if nxt:
                    rotate(*nxt, 1)
                distance_b(c, hh, 2, par)
                distance_b(c, hh, 3, par)
                distance_c(c, hh, 2, par)
                distance_c(c, hh, 3, par)
                if nxt:
                    rotated(nxt[0], nxt[1], 0)
                logits(c, hh, 0, par)
                logits(c, hh, 1, par)
                if nxt:
                    rotated(nxt[0], nxt[1], 1)
                if old:
                    keep_y(*old)
                logits(c, hh, 2, par)
                logits(c, hh, 3, par)
                if nxt:
                    keep_norm_q(nxt[0], nxt[1])
                if old:
                    y_low(*old)

            PERS = (10, 8, 6, 4, 2)

            def body(it):
                c = counts(dve, it.t, PERS)
                cp, cn = previous(c), following(c)
                if it.new is not None:
                    start(it.new, it.par)
                unit(c, 0, it.par, None if it.before is None else (cp, 1), (c, 1, it.par))
                if it.opens is not None:
                    dve.wait_ge(grp[it.behind], it.opens)
                unit(c, 1, it.par, (c, 0), None if it.behind is None else (cn, 0, it.behind),
                     mid=[] if it.before is None else [lambda: add_output(cp, it.b_before)])

            def start(g, par):
                if isinstance(g, int):
                    src, v = nco[:, g * HH:(g + 1) * HH], g + 1
                else:
                    src, v = nco[:, bass.ds(g * HH, HH)], dve.snap(g + 1)
                dve.tensor_copy(ncog[:, par, :], src).then_inc(ncog_dve, 1)
                dve.wait_ge(ncog_dve, v)
                settle(v)

            dve.wait_ge(nco_in, 16)
            dve.wait_ge(consts, 7)
            dve.wait_ge(grp[0], 64)
            c0 = counts(dve, 0, PERS)
            rotate(c0, 0, 0, 0)
            rotated(c0, 0, 0)
            rotate(c0, 0, 0, 1)
            rotated(c0, 0, 1)
            keep_norm_q(c0, 0)
            run_iterations(dve, body)
            c = counts(dve, G * B - 1, PERS)
            keep_y(c, 1)
            y_low(c, 1)
            add_output(c, B - 1)

            credit(dve, (f_norm, 2), (f_lo, 2), (f_h, FT), (f_res, 2), (f_ln, 8), (f_l3, 4))

            def acc_of(b, j0=0, n=NT):
                if isinstance(b, int):
                    return accf[:, (b * NT + j0) * D:(b * NT + j0 + n) * D]
                return accf[:, bass.ds(b * (NT * D) + j0 * D, n * D)]

            def front(b, c, s, xv):
                def part0():
                    dve.wait_ge(f_x[s], xv)
                    settle(c[2])
                    norm(lambda j: acc_of(b, j, 1), lambda j: f_tmp[:, j, :], f_ln, c[8], 0, f_root, c[2] + 1, f_ln)

                def part1():
                    dve.wait_ge(f_ln, c[8] + 4)
                    tt(acc_of(b), f_tmp.rearrange("p j n -> p (j n)"), f_xin[s].rearrange("p j n -> p (j n)"),
                       ALU.add).then_inc(f_ln, 1)
                    dve.wait_ge(f_ln, c[8] + 5)

                def part2():
                    dve.wait_ge(f_tr, c[2])
                    settle(xv)
                    norm(lambda j: acc_of(b, j, 1), lambda j: f_nrm[:, j, :], f_ln, c[8], 5, f_root, c[2] + 2, f_norm)
                return [part0, part1, part2]

            def split_low(c, s):
                for kt in range(KT):
                    dve.wait_ge(f_hi, c[2] + kt + 1)
                    tt(xt[s][:, kt, 1, :], pp[kt][:, :], xt[s][:, kt, 0, :].bitcast(F32), ALU.subtract).then_inc(f_lo, 1)

            def hidden(c, r):
                dve.wait_ge(f_silu, c[FT] + r + 1)
                dve.wait_ge(f_u, c[FT] + r + 1)
                dve.wait_ge(f_hl, c[FT] + r + 1 - 2)
                dve.wait_ge(f_hh, c[FT] + r + 1 - 2)
                stt(f_hid(r), ps[r % 2][:, :], SCALE, f_gate(r), ALU.mult, ALU.mult).then_inc(f_h, 1)

            def back(b, c, s, ov):
                dve.wait_ge(f_ev, c[2] + 2)
                norm(lambda j: f_y[:, j, :], lambda j: f_tmp[:, j, :], f_l3, c[4], 0, f_rootb, c[1] + 1, f_l3)
                dve.wait_ge(f_l3, c[4] + 4)
                dve.wait_ge(f_out[s], ov)
                tt(f_outs[s].rearrange("p j n -> p (j n)"), f_tmp.rearrange("p j n -> p (j n)"), acc_of(b),
                   ALU.add).then_inc(f_res, 1)

            FP = (FT, 8, 4, 2, 1)

            def f_body(b, s, i, nxt):
                c = counts(dve, b, FP)
                parts = [None] * 3
                if nxt:
                    cn = {p: v + p for p, v in c.items()}
                    xv = (i + (2 if s else 1)) * 16
                    parts = front(b + 1 if isinstance(b, int) else dve.snap(b + 1), cn, 1 - s,
                                  xv if isinstance(xv, int) else dve.snap(xv))
                for r in range(FT):
                    hidden(c, r)
                    if nxt and r < 3:
                        parts[r]()
                if nxt:
                    split_low(cn, 1 - s)
                ov = (i + 1) * 16
                back(b, c, s, ov if isinstance(ov, int) else dve.snap(ov))

            c0 = counts(dve, 0, FP)
            for part in front(0, c0, 0, 16):
                part()
            split_low(c0, 0)
            with dve.Fori(0, B // 2 - 1) as i:
                f_body(dve.snap(i * 2), 0, i, True)
                f_body(dve.snap(i * 2 + 1), 1, i, True)
            f_body(B - 2, 0, B // 2 - 1, True)
            f_body(B - 1, 1, B // 2 - 1, False)


_INS = ['L0_attn_x', 'L0_attn_Wq', 'L0_attn_Wk', 'L0_attn_Wv', 'L0_attn_Wo', 'L0_attn_omega', 'L0_attn_mu_raw',
        'L0_attn_sigma_raw', 'L0_attn_eta_raw', 'L0_attn_gamma_raw', 'L0_attn_nu_raw', 'L0_attn_tau',
        'L0_ffn_w_gate', 'L0_ffn_w_up', 'L0_ffn_w_down']


def kernel(**inputs):
    import concourse.bacc as _bacc
    from concourse.bass_utils import run_bass_kernel_spmd as _run

    nc = _bacc.Bacc("TRN2", target_bir_lowering=False, num_devices=1)
    arrays, args = {}, []
    for name in _INS:
        a = np.ascontiguousarray(inputs[name])
        arrays[f"in_{name}"] = a
        args.append(nc.dram_tensor(f"in_{name}", a.shape, mybir.dt.from_np(a.dtype), kind="ExternalInput").ap())
    out = nc.dram_tensor("out", (B, N, D), F32, kind="ExternalOutput").ap()
    build(nc, *args[0:6], args[6:11], *args[11:15], out)
    r = _run(nc, [arrays], core_ids=[0])
    return r.results[0]["out"]
```

```python
import math
from collections import namedtuple
from contextlib import ExitStack

import numpy as np
import concourse.bass as bass
from concourse import mybir

F32 = mybir.dt.float32
F32R = mybir.dt.float32r
I32 = mybir.dt.int32
ALU = mybir.AluOpType
ACT = mybir.ActivationFunctionType

It = namedtuple("It", "t half b par slot before behind b_before new opens")
B, N, D = 8, 512, 256
H, DH = 16, 64
DK = H * DH
HID = 768
P = 128
KT = D // P
NT = N // P
HH = 2
G = H // HH
FT = HID // P
W2 = HH * 2 * DH
EPS_LN = 1e-5
EPS_MU = 1e-4
MIN_EXP = -30.0
BIG = 1e18
SCALE = 1.0 / 127.0
MAGIC = 1.5 * 2.0 ** 23
VEC = N + P
E_T, VN_T, T3_T = range(3)
V_EXP, V_LN, V_TABLES = 17, 22, 30
V_ANGLE = [V_TABLES + 10 * k + 7 for k in range(4)]
V_ROPE = [V_TABLES + 10 * k + 10 for k in range(4)]
NCO = 22
TILES = tuple(range(NT - 1, -1, -1))
WS = sum(i + 1 for i in TILES) * P
POOL_SCALES = (0,)


def build(nc, x_d, wq_d, wk_d, wv_d, wo_d, omega_d, raw_d, tau_d, wg_d, wu_d, wd_d, out_d):
    ctx = ExitStack()
    with ctx:
        def sb(name, shape, dt=F32):
            return ctx.enter_context(nc.sbuf_tensor(name, shape, dt))

        def sem(name):
            return ctx.enter_context(nc.semaphore(name))

        def scratch(name, shape):
            return nc.dram_tensor(name, shape, F32, kind="Internal").ap()

        xs_d = scratch("xs_d", (B, P, KT * 2 * N))
        ws_d = scratch("ws_d", (G, P, 3 * KT * 2 * W2))
        wos_d = scratch("wos_d", (G, P, HH * 2 * D))
        vec_d = scratch("vec_d", (3, H, VEC))
        tab_d = scratch("tab_d", (G, P, HH, 3, N))
        rope_d = scratch("rope_d", (G, P, HH, 2, N))
        nco_d = scratch("nco_d", (1, H))

        acc = sb("acc", [P, B, NT, D])
        tabs = [sb(f"tabs{i}", [P, 5 * HH, N]) for i in range(2)]
        wt = sb("wt", [P, 2, 3 * KT * 2 * W2], F32R)
        wot = sb("wot", [P, 2, HH * 2 * D], F32R)
        xt = [sb(f"xt{i}", [P, KT, 2, N], F32R) for i in range(2)]
        qkb = sb("qkb", [P, 3 * HH, N])
        sq = sb("sq", [P, 2, N])
        swt = sb("swt", [P, 4, N])
        ek = sb("ek", [P, 2, N])
        lg = sb("lg", [P, 2, WS])
        pr = sb("pr", [P, 2, WS])
        pt = sb("pt", [P, 2, N])
        vt = sb("vt", [P, NT, HH * P])
        ysb = sb("ysb", [P, NT, P])
        yhl = sb("yhl", [P, HH, 2, N], F32R)
        wgt = sb("wgt", [P, KT, HID], F32R)
        wut = sb("wut", [P, KT, HID], F32R)
        wdt = sb("wdt", [P, FT, D], F32R)
        ident = sb("ident", [P, P])
        ones = sb("ones", [P, P])
        qn = sb("qn", [P, HH, 2, NT])
        nmax = sb("nmax", [P, 2 * NT])
        den = sb("den", [P, 2 * NT])
        rden = sb("rden", [P, 2 * NT])
        nco = sb("nco", [P, H])
        ncog = sb("ncog", [P, 2, HH])
        hp = sb("hp", [H, 40])
        om = sb("om", [P, 4])
        stats = sb("stats", [P, NT, 6])
        mv = sb("mv", [P, NT, 2])
        rstd = sb("rstd", [P, NT])
        mhalf = sb("mhalf", [P, NT])

        accf = acc[:, :, :, :].rearrange("p b j n -> p (b j n)")
        dist, v_e, v_vn, v_t3, v_v, v_lnv = [accf[0:H, k * VEC:(k + 1) * VEC] for k in range(6)]
        tokens, ang, turns, half_sin = lg[:, 1, N:2 * N], sq[:, 0, :], sq[:, 1, :], ysb[:, :, :].rearrange("p j n -> p (j n)")
        rope_sn = [accf[:, 4096 + k * N:4096 + (k + 1) * N] for k in range(4)]
        rope_sp = [accf[:, 6144 + k * N:6144 + (k + 1) * N] for k in range(4)]
        rope_cs = [pr[:, 0, 0:N], pr[:, 0, N:2 * N], pt[:, 0, :], pt[:, 1, :]]
        xraw = [z[:, :, :].rearrange("p a n -> p (a n)").rearrange("p (j n) -> p j n", j=NT) for z in (ek, vt)]
        xnorm = [lg[:, a, 0:NT * D].rearrange("p (j n) -> p j n", j=NT) for a in range(2)]

        def seq(s, k):
            return tabs[s][:, k:k + 2, :].rearrange("p a n -> p (a n)").rearrange("p (j n) -> p j n", j=NT)
        f_xin = [seq(0, 0), seq(1, 0)]
        f_outs = [seq(0, 2), seq(1, 2)]
        f_nrm = seq(0, 4)
        f_tmp = seq(1, 6)
        f_y = seq(1, 4)

        def f_gate(r):
            return tabs[0][:, 6 + r % 2, :]

        def f_hid(r):
            return tabs[0][:, 8 + r % 2, :]

        def hpart(r, a):
            o = (r * 2 + a) * N
            return wt[:, :, :].rearrange("p a n -> p (a n)")[:, o:o + N]

        def bank(name):
            return ctx.enter_context(nc.psum_tensor(name, [P, N], F32))
        pa = [bank("pa0"), bank("pa1")]
        ps = [bank("ps0"), bank("ps1")]
        pp = [bank("pp0"), bank("pp1")]
        py = bank("py")
        po = bank("po")

        consts = sem("consts")
        p_load = sem("p_load")
        p_dve = sem("p_dve")
        p_act = sem("p_act")
        vec_out = sem("vec_out")
        tab_out = sem("tab_out")
        rope_out = sem("rope_out")
        nco_in = sem("nco_in")
        raww = [sem(f"raww{i}") for i in range(2)]
        split_hi = sem("split_hi")
        split_lo = sem("split_lo")
        split_out = [sem(f"split_out{i}") for i in range(2)]
        ffn_in = sem("ffn_in")
        ffn_cast = sem("ffn_cast")
        ffn_tr = sem("ffn_tr")
        ffn_ev = sem("ffn_ev")
        x_in = [sem(f"x_in{i}") for i in range(2)]
        x_ln = sem("x_ln")
        x_root = sem("x_root")
        x_norm = sem("x_norm")
        x_tr = sem("x_tr")
        x_hi = sem("x_hi")
        x_lo = sem("x_lo")
        x_out = [sem(f"x_out{i}") for i in range(2)]

        grp = [sem(f"grp{i}") for i in range(2)]
        xt_in = [sem(f"xt_in{i}") for i in range(2)]
        proj = sem("proj")
        v_rdy = sem("v_rdy")
        s_rdy = sem("s_rdy")
        tr_rdy = sem("tr_rdy")
        av_rdy = sem("av_rdy")
        yt_rdy = sem("yt_rdy")
        o_rdy = sem("o_rdy")
        pa_act = sem("pa_act")
        v_act = sem("v_act")
        ln_act = sem("ln_act")
        ex_act = sem("ex_act")
        pt_act = sem("pt_act")
        yh_act = sem("yh_act")
        pa_dve = sem("pa_dve")
        rope = sem("rope")
        a_dve = sem("a_dve")
        b_dve = sem("b_dve")
        b_pool = sem("b_pool")
        cd_dve = sem("cd_dve")
        f_dve = sem("f_dve")
        rd_dve = sem("rd_dve")
        y_dve = sem("y_dve")
        yl_dve = sem("yl_dve")
        acc_dve = sem("acc_dve")
        ek_pool = sem("ek_pool")
        t2_pool = sem("t2_pool")

        NPB = len(POOL_SCALES)

        f_x = [sem(f"f_x{i}") for i in range(2)]
        f_ln = sem("f_ln")
        f_root = sem("f_root")
        f_rootb = sem("f_rootb")
        f_norm = sem("f_norm")
        f_tr = sem("f_tr")
        f_hi = sem("f_hi")
        f_lo = sem("f_lo")
        f_g = sem("f_g")
        f_u = sem("f_u")
        f_silu = sem("f_silu")
        f_h = sem("f_h")
        f_hh = sem("f_hh")
        f_hl = sem("f_hl")
        f_dn = sem("f_dn")
        f_ev = sem("f_ev")
        f_res = sem("f_res")
        f_l3 = sem("f_l3")
        f_out = [sem(f"f_out{i}") for i in range(2)]
        settled = sem("settled")
        ncog_dve = sem("ncog_dve")

        block = ctx.enter_context(nc.Block())

        def counts(eng, t, pers):
            if isinstance(t, int):
                return {p: (t + 1) * p for p in pers}
            t = eng.snap(t + 1)
            return {p: eng.snap(t * p) if p > 1 else t for p in pers}

        def credit(eng, *pairs):
            for s, n in pairs:
                if n:
                    eng.sem_inc(s, n)

        def run_iterations(eng, body):
            def snap(v):
                return v if isinstance(v, int) else eng.snap(v)

            body(It(t=0, half=0, b=0, par=0, slot=0, before=None, behind=0, b_before=None, new=0, opens=None))

            def group(gg, par, last):
                t0, h0, g = gg * 2 * B + par * B, gg * B + par * B // 2, gg * 2 + par
                with eng.Fori(0, B // 2 - 1) as i:
                    for k in (1, 2):
                        body(It(t=snap(i * 2 + t0 + k), half=snap(i + h0 + k - 1), b=snap(i * 2 + k), par=par, slot=k % 2,
                                before=par, behind=par, b_before=snap(i * 2 + k - 1), new=None, opens=None))
                body(It(t=snap(t0 + B - 1), half=snap(h0 + B // 2 - 1), b=B - 1, par=par, slot=1, before=par,
                        behind=None if last else 1 - par, b_before=B - 2, new=None,
                        opens=None if last else snap(((g + 1) // 2 + 1) * 64 if isinstance(g, int) else (gg + (1 + par)) * 64)))
                if not last:
                    body(It(t=snap(t0 + B), half=snap(h0 + B // 2), b=0, par=1 - par, slot=0, before=par,
                            behind=1 - par, b_before=B - 1, new=snap(g + 1), opens=None))

            with eng.Fori(0, G // 2 - 1) as gg:
                group(gg, 0, False)
                group(gg, 1, False)
            group(G // 2 - 1, 0, False)
            group(G // 2 - 1, 1, True)

        def following(c):
            return {p: v + p for p, v in c.items()}

        def previous(c):
            return {p: v - p for p, v in c.items()}

        def tab(par, hh, k, lo=0, hi=N):
            return tabs[par][:, hh * 3 + k, lo:hi]

        def ropet(par, hh, k):
            return tabs[par][:, 3 * HH + hh * 2 + k, :]

        def wproj(par, m, kt, part, lo, hi):
            o = ((m * KT + kt) * 2 + part) * W2
            return wt[:, par, o + lo:o + hi]

        def width(n):
            return (TILES[n] + 1) * P

        def at(n):
            o = sum(width(k) for k in range(n))
            return slice(o, o + width(n))

        PARTS = ((0, 0), (0, 1), (1, 0))

        def split_views(m, s):
            stage = wt[:, (4 * m + s) % 2, 0:2048]
            raw = tabs[m % 2][:, 0:8, :].rearrange("p a n -> p (a n)")
            if m < 3:
                kt, gh = s // 2, s % 2
                out = stage.rearrange("p (g a h c d) -> p a c g h d", g=4, a=2, h=HH, c=2)
                for c in range(2):
                    o = kt * 2 * DK + c * DK + gh * DK // 2
                    yield out[:, 0, c], out[:, 1, c], raw[:, o:o + DK // 2].rearrange("p (g h d) -> p g h d", g=4, h=HH)
            else:
                out = stage.rearrange("p (h a n) -> p a h n", h=2 * HH, a=2)
                yield out[:, 0], out[:, 1], raw[:, s * 1024:(s + 1) * 1024].rearrange("p (h n) -> p h n", h=2 * HH)

        def ffn_jobs():
            jobs = []
            for raw, dst in ((qkb[:, 0:3, :], wgt), (qkb[:, 3:6, :], wut)):
                r6 = raw.rearrange("p a n -> p (a n)").rearrange("p (r n) -> p r n", r=FT)
                for kt in range(KT):
                    for r in range(FT):
                        o = kt * HID + r * P
                        jobs.append((r6[:, r, kt * P:(kt + 1) * P],
                                     dst[:, :, :].rearrange("p k n -> p (k n)")[:, o:min(o + 4 * P, KT * HID)]))
            w2 = swt[:, 0:3, :].rearrange("p a n -> p (a n)").rearrange("p (r n) -> p r n", r=KT)
            for r in range(FT):
                for d in range(KT):
                    o = r * D + d * P
                    jobs.append((w2[:, d, r * P:(r + 1) * P], wdt[:, :, :].rearrange("p r n -> p (r n)")[:, o:min(o + 4 * P, FT * D)]))
            return jobs

        @block.sync
        def _(sp):
            credit(sp, (x_out[0], 16), (x_out[1], 16), (f_out[0], 16), (f_out[1], 16))
            for k in range(5):
                sp.dma_start(hp[:, k:k + 1], raw_d[k].rearrange("(h a) -> h a", a=1)).then_inc(p_load, 16)
            sp.dma_start(hp[:, 5:6], tau_d.rearrange("(h a) -> h a", a=1)).then_inc(p_load, 16)
            for k in range(4):
                sp.dma_start(om[:, k:k + 1], omega_d[4 * k:4 * k + 4, :].rearrange("a (d e) -> (a d) e", e=1)).then_inc(p_load, 16)
            for s in range(2):
                sp.dma_start(xraw[s], x_d[s].rearrange("(j p) n -> p j n", p=P)).then_inc(x_in[s], 16)
            raws = [wq_d.rearrange("(k p) n -> p k n", p=P), wk_d.rearrange("(k p) n -> p k n", p=P),
                    wv_d.rearrange("(k p) n -> p k n", p=P), None]

            def load_raw(m):
                dst = tabs[m % 2][:, 0:8, :].rearrange("p a n -> p (a n)")
                if m < 3:
                    sp.dma_start(dst.rearrange("p (k n) -> p k n", k=KT), raws[m]).then_inc(raww[m % 2], 16)
                else:
                    for c in range(2):
                        sp.dma_start(dst[c * DH:(c + 1) * DH, :].rearrange("p (h n) -> p h n", h=H),
                                     wo_d[c * DK:(c + 1) * DK, :].rearrange("(h d) n -> d h n", d=DH)
                                     ).then_inc(raww[1], 16)
            load_raw(0)
            load_raw(1)
            sp.dma_start(qkb[:, 0:3, :].rearrange("p a n -> p (a n)").bitcast(I32).rearrange("p (r n) -> p r n", r=FT),
                         wg_d.rearrange("(r p) n -> p r n", p=P)).then_inc(ffn_in, 16)
            sp.dma_start(qkb[:, 3:6, :].rearrange("p a n -> p (a n)").bitcast(I32).rearrange("p (r n) -> p r n", r=FT),
                         wu_d.rearrange("(r p) n -> p r n", p=P)).then_inc(ffn_in, 16)
            sp.dma_start(swt[:, 0:3, :].rearrange("p a n -> p (a n)").bitcast(I32).rearrange("p (r n) -> p r n", r=KT),
                         wd_d.rearrange("(r p) n -> p r n", p=P)).then_inc(ffn_in, 16)
            sp.wait_ge(p_dve, V_TABLES)
            for k in range(3):
                sp.dma_start(vec_d[k], (v_e, v_vn, v_t3)[k]).then_inc(vec_out, 16)
            sp.dma_start(nco_d.rearrange("a h -> h a"), hp[:, NCO:NCO + 1]).then_inc(vec_out, 16)
            sp.wait_ge(vec_out, 64)
            sp.dma_start(nco[:, :], bass.AP(tensor=nco_d.tensor, offset=0, ap=[[0, P], [1, H]])).then_inc(nco_in, 16)
            for g in range(G):
                for k in range(3):
                    src = bass.AP(tensor=vec_d.tensor, offset=(k * H + g * HH) * VEC + P - 1,
                                  ap=[[VEC, HH], [-1, P], [1, N]])
                    sp.dma_start(tab_d[g, :, :, k, :].rearrange("p h n -> h p n"), src).then_inc(tab_out, 16)
            for k in range(4):
                sp.wait_ge(p_dve, V_ROPE[k])
                for row in range(4):
                    h0 = 4 * k
                    for c, src in ((0, rope_cs[k]), (1, rope_sp[k] if row in (1, 2) else rope_sn[k])):
                        for a in range(2):
                            dst = rope_d[(h0 + 2 * a) // HH, row * 32:(row + 1) * 32, :, c, :]
                            sp.dma_start(dst.rearrange("d h n -> h d n"), src[a * 64:(a + 1) * 64, :]
                                         ).then_inc(rope_out, 16)
            for m in range(4):
                for s in range(4):
                    i = 4 * m + s
                    sp.wait_ge(split_lo, i + 1)
                    sp.wait_ge(split_hi, i + 1)
                    stage = wt[:, i % 2, 0:2048].bitcast(F32)
                    if m < 3:
                        kt, gh = s // 2, s % 2
                        dst = ws_d[4 * gh:4 * gh + 4].rearrange("g p (m r) -> p g m r", m=3 * KT)[:, :, m * KT + kt, :]
                        sp.dma_start(dst, stage.rearrange("p (g r) -> p g r", g=4)).then_inc(split_out[i % 2], 16)
                    else:
                        sp.dma_start(wos_d[2 * s:2 * s + 2].rearrange("g p r -> p g r"),
                                     stage.rearrange("p (g r) -> p g r", g=2)).then_inc(split_out[i % 2], 16)
                if m < 2:
                    load_raw(m + 2)
            def x_load(b, s):
                src = x_d[b].rearrange("(j p) n -> p j n", p=P) if isinstance(b, int) else \
                    x_d[bass.ds(b, 1)].rearrange("b (j p) n -> p (b j) n", p=P)
                sp.dma_start(xraw[s], src).then_inc(x_in[s], 16)

            def x_store(b, s):
                dst = xs_d[b] if isinstance(b, int) else xs_d[bass.ds(b, 1)].rearrange("b p n -> (b p) n")
                sp.dma_start(dst, xt[s][:, :, :, :].rearrange("p k s n -> p (k s n)").bitcast(F32)).then_inc(x_out[s], 16)

            with sp.Fori(0, B // 2 - 1) as i:
                off = [sp.snap(i * 2 + s) for s in range(2)]
                nxt = [sp.snap(i * 2 + s + 2) for s in range(2)]
                nrm = [sp.snap(i * 2 + s + 3) for s in range(2)]
                hlo = [sp.snap(i * 4 + 2 * s + 4) for s in range(2)]
                for s in range(2):
                    sp.wait_ge(x_norm, nrm[s])
                    x_load(nxt[s], s)
                    sp.wait_ge(x_hi, hlo[s])
                    sp.wait_ge(x_lo, hlo[s])
                    x_store(off[s], s)
            for s in range(2):
                sp.wait_ge(x_hi, 2 * (B - 2 + s) + 4)
                sp.wait_ge(x_lo, 2 * (B - 2 + s) + 4)
                x_store(B - 2 + s, s)
            sp.wait_ge(tab_out, 16 * 3 * G)
            sp.wait_ge(rope_out, 16 * 64)
            for s in range(2):
                sp.wait_ge(split_out[s], 16 * 8)
                sp.wait_ge(x_out[s], 16 * (B // 2 + 1))
            sp.wait_ge(ffn_tr, 9)

            def load_group(g, par):
                one = (lambda d: d[g] if isinstance(g, int) else d[bass.ds(g, 1)])
                def flat(d, pat, pat1):
                    return one(d).rearrange(pat if isinstance(g, int) else pat1)
                sp.dma_start(tabs[par][:, 0:3 * HH, :], flat(tab_d, "p h k n -> p (h k) n", "g p h k n -> (g p) (h k) n")).then_inc(grp[par], 16)
                sp.dma_start(tabs[par][:, 3 * HH:5 * HH, :], flat(rope_d, "p h k n -> p (h k) n", "g p h k n -> (g p) (h k) n")).then_inc(grp[par], 16)
                sp.dma_start(wt[:, par, :].bitcast(F32), flat(ws_d, "p r -> p r", "g p r -> (g p) r")).then_inc(grp[par], 16)
                sp.dma_start(wot[:, par, :].bitcast(F32), flat(wos_d, "p r -> p r", "g p r -> (g p) r")).then_inc(grp[par], 16)

            def load_x(b, s):
                src = xs_d[b] if isinstance(b, int) else xs_d[bass.ds(b, 1)].rearrange("b p n -> (b p) n")
                sp.dma_start(xt[s][:, :, :, :].rearrange("p k s n -> p (k s n)").bitcast(F32), src).then_inc(xt_in[s], 16)

            load_group(0, 0)
            load_x(0, 0)
            load_x(1, 1)
            load_group(1, 1)

            def sequences(t0, last):
                with sp.Fori(0, B // 2 - 1) as i:
                    for s in range(2):
                        nb = sp.snap(i * 2 + s + 2)
                        v = sp.snap((i * 2 + (t0 + (s + 1))) * 2 + 2)
                        sp.wait_ge(v_rdy, v)
                        load_x(nb, s)
                if not last:
                    for s in range(2):
                        v = (t0 + (B - 1 + s)) * 2 + 2
                        sp.wait_ge(v_rdy, v if isinstance(v, int) else sp.snap(v))
                        load_x(s, s)

            def refill(g, par, t0):
                v8, v2, vb = t0 * 8 + 8, t0 * 2 + 2, t0 * (2 * NPB) + 2 * NPB
                if not isinstance(t0, int):
                    v8, v2 = sp.snap(v8), sp.snap(v2)
                    vb = sp.snap(vb) if NPB else 0
                sp.wait_ge(f_dve, v8)
                sp.wait_ge(ek_pool, v8)
                if NPB:
                    sp.wait_ge(b_pool, vb)
                sp.wait_ge(o_rdy, v2)
                load_group(g, par)

            sequences(0, False)
            with sp.Fori(0, G // 2 - 1) as gg:
                g2 = sp.snap(gg * 2 + 2)
                g3 = sp.snap(gg * 2 + 3)
                ta = sp.snap(gg * (2 * B) + B)
                tb = sp.snap(gg * (2 * B) + 2 * B)
                refill(g2, 0, ta)
                sequences(ta, False)
                refill(g3, 1, tb)
                sequences(tb, False)
            sequences((G - 1) * B, True)

            def f_load(b, s):
                src = x_d[b].rearrange("(j p) n -> p j n", p=P) if isinstance(b, int) else \
                    x_d[bass.ds(b, 1)].rearrange("b (j p) n -> p (b j) n", p=P)
                sp.dma_start(f_xin[s], src).then_inc(f_x[s], 16)

            def f_store(b, s):
                dst = out_d[b].rearrange("(j p) n -> p j n", p=P) if isinstance(b, int) else \
                    out_d[bass.ds(b, 1)].rearrange("b (j p) n -> p (b j) n", p=P)
                sp.dma_start(dst, f_outs[s]).then_inc(f_out[s], 16)

            sp.wait_ge(f_dve, 8 * B * G + 8)
            sp.wait_ge(ek_pool, 8 * B * G + 8)
            f_load(0, 0)
            f_load(1, 1)
            with sp.Fori(0, B // 2 - 1) as i:
                off = [sp.snap(i * 2 + s) for s in range(2)]
                nxt = [sp.snap(i * 2 + s + 2) for s in range(2)]
                cnt = [sp.snap(i * 2 + s + 3) for s in range(2)]
                for s in range(2):
                    sp.wait_ge(f_norm, cnt[s])
                    f_load(nxt[s], s)
                    sp.wait_ge(f_res, cnt[s])
                    f_store(off[s], s)
            for s in range(2):
                sp.wait_ge(f_res, B - 2 + s + 3)
                f_store(B - 2 + s, s)
            for s in range(2):
                sp.wait_ge(f_out[s], 16 * (B // 2 + 1))

        @block.gpsimd
        def _(pool):
            credit(pool, (ek_pool, 8), (b_pool, 2 * NPB), (t2_pool, 4))
            pool.memset(ident[:, :], 0.0).then_inc(consts, 1)
            pool.memset(ones[:, :], 1.0).then_inc(consts, 1)
            pool.memset(mhalf[:, :], -0.5).then_inc(consts, 1)
            pool.iota(dist, pattern=[[-1, VEC]], base=N - 1, channel_multiplier=0,
                      allow_small_or_imprecise_dtypes=True).then_inc(consts, 1)
            pool.iota(tokens, pattern=[[1, N]], base=0, channel_multiplier=0,
                      allow_small_or_imprecise_dtypes=True).then_inc(consts, 1)
            pool.wait_ge(consts, 5)
            pool.affine_select(out=ident[:, :], in_=ident[:, :], compare_op=ALU.not_equal, fill=1.0,
                               base=0, pattern=[[-1, P]], channel_multiplier=1).then_inc(consts, 1)


            def root(chain, v, mark):
                pool.wait_ge(chain, v)
                pool.tensor_tensor(rstd[:, :], rstd[:, :], mhalf[:, :], ALU.pow).then_inc(mark, 1)

            credit(pool, (x_root, 1), (f_root, 2), (f_rootb, 1))
            with pool.Fori(0, B) as b:
                root(x_ln, pool.snap(b * 3 + 3 + 3), x_root)

            pool.wait_ge(vec_out, 64)
            pool.wait_ge(rope_out, 16 * 64)
            pool.memset(accf, 0.0).then_inc(consts, 1)

            def rope_sin(c, hh, par, m):
                pool.wait_ge(pa_act, c[6] + 3 * hh + m + 1)
                pool.wait_ge(rope, c[4] + 2 * hh + m + 1 - 2)
                pool.tensor_tensor(swt[:, 2 + m, :], swt[:, m, :], ropet(par, hh, 1), ALU.mult).then_inc(t2_pool, 1)

            def decay_norm(c, hh, n, par):
                i, m = n % 2, 4 * hh + n
                w = width(n)
                if n == 0:
                    pool.wait_ge(pa_act, c[6] + 3 * hh + 3)
                pool.wait_ge(a_dve, c[8] + m + 1 - 2)
                pool.tensor_tensor(ek[:, i, 0:w], tab(par, hh, E_T, N - w), qkb[:, 3 * hh + 2, 0:w],
                                   ALU.mult).then_inc(ek_pool, 1)

            def times_decay(c, hh, n, par):
                m, w = 4 * hh + n, width(n)
                pool.wait_ge(a_dve, c[8] + m + 1)
                pool.tensor_tensor(lg[:, hh, at(n)], lg[:, hh, at(n)], tab(par, hh, E_T, N - w), ALU.mult).then_inc(b_pool, 1)

            def body(it):
                c = counts(pool, it.t, (8, 6, 4))
                cn, nxt = following(c), it.behind is not None
                times_decay(c, 0, 0, it.par)
                rope_sin(c, 1, it.par, 0)
                decay_norm(c, 0, 2, it.par)
                rope_sin(c, 1, it.par, 1)
                decay_norm(c, 0, 3, it.par)
                decay_norm(c, 1, 0, it.par)
                times_decay(c, 1, 0, it.par)
                decay_norm(c, 1, 1, it.par)
                decay_norm(c, 1, 2, it.par)
                if it.opens is not None:
                    pool.wait_ge(grp[it.behind], it.opens)
                if nxt:
                    rope_sin(cn, 0, it.behind, 0)
                    rope_sin(cn, 0, it.behind, 1)
                decay_norm(c, 1, 3, it.par)
                if nxt:
                    decay_norm(cn, 0, 0, it.behind)
                    decay_norm(cn, 0, 1, it.behind)

            pool.wait_ge(grp[0], 64)
            c0 = counts(pool, 0, (8, 6, 4))
            rope_sin(c0, 0, 0, 0)
            rope_sin(c0, 0, 0, 1)
            decay_norm(c0, 0, 0, 0)
            decay_norm(c0, 0, 1, 0)
            run_iterations(pool, body)

            credit(pool, (f_hl, FT))

            def hidden_low(c, r):
                pool.wait_ge(f_hh, c[FT] + r + 1)
                if r == 0:
                    pool.wait_ge(f_dn, c[2])
                pool.tensor_tensor(hpart(r, 1), f_hid(r), hpart(r, 0).bitcast(F32), ALU.subtract).then_inc(f_hl, 1)

            def f_body(b, nxt):
                c = counts(pool, b, (FT, 8, 4, 2))
                hidden_low(c, 0)
                if nxt:
                    root(f_ln, c[8] + 8 + 3, f_root)
                hidden_low(c, 1)
                if nxt:
                    root(f_ln, c[8] + 8 + 8, f_root)
                for r in range(2, FT):
                    hidden_low(c, r)
                root(f_l3, c[4] + 3, f_rootb)

            root(f_ln, 8 + 3, f_root)
            root(f_ln, 8 + 8, f_root)
            with pool.Fori(0, B - 1) as b:
                f_body(b, True)
            f_body(B - 1, False)

        @block.tensor
        def _(pe):
            credit(pe, (proj, 8), (v_rdy, 2), (s_rdy, 8), (tr_rdy, 8), (av_rdy, 8), (yt_rdy, 2), (o_rdy, 2), (x_tr, 2))
            mm = pe.matmul
            pe.wait_ge(consts, 6)
            jobs = ffn_jobs()
            pe.wait_ge(ffn_cast, 3)
            for n in range(9):
                if n >= 2:
                    pe.wait_ge(ffn_ev, n - 1)
                for k, (src, _) in enumerate(jobs[4 * n:4 * n + 4]):
                    last = pe.transpose(ps[n % 2][:, k * P:(k + 1) * P], src, ident[:, :])
                last.then_inc(ffn_tr, 1)

            with pe.Fori(0, B // 2) as i:
                for s in range(2):
                    nrm = pe.snap(i * 2 + s + 3)
                    c = pe.snap(i * 4 + 2 * s + 2)
                    pe.wait_ge(x_norm, nrm)
                    for kt in range(KT):
                        pe.wait_ge(x_hi, c + kt + 1 - 2)
                        pe.wait_ge(x_lo, c + kt + 1 - 2)
                        for j in range(NT):
                            last = pe.transpose(pp[kt][:, j * P:(j + 1) * P], xnorm[s][:, j, kt * P:(kt + 1) * P],
                                                ident[:, :])
                        last.then_inc(x_tr, 1)

            def project(half, c, hh, par, slot, m):
                if hh == 0 and m == 0:
                    v = (half + 1) * 16
                    pe.wait_ge(xt_in[slot], v if isinstance(v, int) else pe.snap(v))
                pe.wait_ge(pa_dve if m else pa_act, c[6] + 3 * hh)
                n = 0
                for kt in range(KT):
                    for a, b in PARTS:
                        last = mm(pa[m][:, :], wproj(par, m, kt, a, hh * P, (hh + 1) * P), xt[slot][:, kt, b, :],
                                  start=(n == 0), stop=(n == 3 * KT - 1))
                        n += 1
                last.then_inc(proj, 1)

            def norm_k(c, hh):
                pe.wait_ge(pa_act, c[6] + 3 * hh + 2)
                pe.wait_ge(pa_dve, c[6] + 3 * hh + 1)
                mm(pa[0][:, :], ones[:, :], sq[:, 1, :], start=True, stop=True).then_inc(proj, 1)

            def norm_q(c, hh):
                pe.wait_ge(pa_dve, c[6] + 3 * hh + 2)
                for i in range(NT):
                    last = mm(pa[1][:, i:i + 1], sq[:, 0, i * P:(i + 1) * P], ones[:, 0:1], start=True, stop=True)
                last.then_inc(proj, 1)

            def values(c, par, slot, half):
                if half == 0:
                    pe.wait_ge(pt_act, c[8])
                for jj in range(2):
                    j = 2 * half + jj
                    n = 0
                    for kt in range(KT):
                        for a, b in PARTS:
                            last = mm(pp[half][:, jj * W2:(jj + 1) * W2], xt[slot][:, kt, a, j * P:(j + 1) * P],
                                      wproj(par, 2, kt, b, 0, W2), start=(n == 0), stop=(n == 3 * KT - 1))
                            n += 1
                last.then_inc(v_rdy, 1)

            def scores(c, hh, n):
                i, m = n % 2, 4 * hh + n
                w = width(n)
                if n == 0:
                    pe.wait_ge(rope, c[4] + 2 * hh + 2)
                pe.wait_ge(a_dve, c[8] + m + 1 - 2)
                mm(ps[i][:, 0:w], qkb[:, 3 * hh, TILES[n] * P:(TILES[n] + 1) * P], qkb[:, 3 * hh + 1, 0:w],
                   start=True, stop=True).then_inc(s_rdy, 1)

            def turn(c, hh, n):
                i, m = n % 2, 4 * hh + n
                pe.wait_ge(ex_act, c[8] + m + 1)
                if hh == 0 and n < 2:
                    pe.wait_ge(v_act, c[2] + n + 1)
                else:
                    pe.wait_ge(pt_act, c[8] + m + 1 - 2)
                for j in range(TILES[n] + 1):
                    o = at(n).start + j * P
                    last = pe.transpose(pp[i][:, j * P:(j + 1) * P], pr[:, hh, o:o + P], ident[:, :])
                last.then_inc(tr_rdy, 1)

            def attend(c, hh, n):
                i, m = n % 2, 4 * hh + n
                I = TILES[n]
                pe.wait_ge(pt_act, c[8] + m + 1)
                if n == 0:
                    pe.wait_ge(v_act, c[2] + 2)
                    if hh == 0:
                        pe.wait_ge(acc_dve, c[2] + 2 - 2)
                    pe.wait_ge(y_dve, c[2] + hh + 1 - 1)
                for j in range(I + 1):
                    last = mm(py[:, I * P:(I + 1) * P], pt[:, i, j * P:(j + 1) * P], vt[:, j, hh * P:(hh + 1) * P],
                              start=(j == 0), stop=(j == I))
                last.then_inc(av_rdy, 1)

            def turn_y(c, hh):
                pe.wait_ge(y_dve, c[2] + hh + 1)
                if hh == 0:
                    pe.wait_ge(acc_dve, c[2] + 1 - 2)
                else:
                    pe.wait_ge(yl_dve, c[2] + 1)
                for j in range(NT):
                    last = pe.transpose(po[:, j * P:(j + 1) * P], ysb[:, j, :], ident[:, :])
                last.then_inc(yt_rdy, 1)

            def out_project(c, par, half):
                if half == 0:
                    pe.wait_ge(yl_dve, c[2] + 2)
                for jj in range(2):
                    j = 2 * half + jj
                    n = 0
                    for hh in range(HH):
                        for a, b in PARTS:
                            last = mm((po, py)[half][:, jj * D:(jj + 1) * D], yhl[:, hh, a, j * P:(j + 1) * P],
                                      wot[:, par, (hh * 2 + b) * D:(hh * 2 + b + 1) * D],
                                      start=(n == 0), stop=(n == 3 * HH - 1))
                            n += 1
                last.then_inc(o_rdy, 1)

            PERS = (8, 6, 4, 2)

            def body(it):
                c = counts(pe, it.t, PERS)
                cp, cn = previous(c), following(c)
                old = it.before is not None
                nxt = it.behind is not None
                half = it.half + it.slot
                if old:
                    turn(cp, 0, 0)
                project(it.half, c, 1, it.par, it.slot, 0)
                if old:
                    turn(cp, 0, 1)
                project(it.half, c, 1, it.par, it.slot, 1)
                scores(c, 0, 0)
                scores(c, 0, 1)
                if old:
                    turn(cp, 0, 2)
                    attend(cp, 0, 0)
                scores(c, 0, 2)
                if old:
                    attend(cp, 0, 1)
                    turn(cp, 0, 3)
                norm_k(c, 1)
                if old:
                    turn(cp, 1, 0)
                    attend(cp, 0, 2)
                    attend(cp, 0, 3)
                    turn(cp, 1, 1)
                norm_q(c, 1)
                scores(c, 0, 3)
                if old:
                    turn(cp, 1, 2)
                if it.opens is not None:
                    pe.wait_ge(grp[it.behind], it.opens)
                if nxt:
                    project(half, cn, 0, it.behind, 1 - it.slot, 0)
                if old:
                    attend(cp, 1, 0)
                    turn_y(cp, 0)
                    attend(cp, 1, 1)
                    turn(cp, 1, 3)
                scores(c, 1, 0)
                if old:
                    attend(cp, 1, 2)
                if nxt:
                    project(half, cn, 0, it.behind, 1 - it.slot, 1)
                if old:
                    attend(cp, 1, 3)
                scores(c, 1, 1)
                values(c, it.par, it.slot, 0)
                if old:
                    turn_y(cp, 1)
                scores(c, 1, 2)
                values(c, it.par, it.slot, 1)
                if nxt:
                    norm_k(cn, 0)
                scores(c, 1, 3)
                if old:
                    out_project(cp, it.before, 0)
                    out_project(cp, it.before, 1)
                if nxt:
                    norm_q(cn, 0)

            pe.wait_ge(grp[0], 64)
            c0 = counts(pe, 0, PERS)
            project(0, c0, 0, 0, 0, 0)
            project(0, c0, 0, 0, 0, 1)
            norm_k(c0, 0)
            norm_q(c0, 0)
            run_iterations(pe, body)
            c = counts(pe, G * B - 1, PERS)
            for hh in range(HH):
                for n in range(NT):
                    turn(c, hh, n)
                    attend(c, hh, n)
                turn_y(c, hh)
            out_project(c, 1, 0)
            out_project(c, 1, 1)

            credit(pe, (f_tr, 2), (f_g, FT), (f_u, FT), (f_dn, 2))

            def f_transposes(c, s):
                pe.wait_ge(f_norm, c[1] + 2)
                for kt in range(KT):
                    pe.wait_ge(f_hi, c[2] + kt + 1 - 2)
                    pe.wait_ge(f_lo, c[2] + kt + 1 - 2)
                    for j in range(NT):
                        last = pe.transpose(pp[kt][:, j * P:(j + 1) * P], f_nrm[:, j, kt * P:(kt + 1) * P], ident[:, :])
                    last.then_inc(f_tr, 1)

            def gate_up(c, s, r):
                i = r % 2
                if r == 0:
                    pe.wait_ge(f_hi, c[2] + 2)
                    pe.wait_ge(f_lo, c[2] + 2)
                for dst, w, free, done in ((pa, wgt, f_silu, f_g), (ps, wut, f_h, f_u)):
                    pe.wait_ge(free, c[FT] + r + 1 - 2)
                    n = 0
                    for kt in range(KT):
                        for a in range(2):
                            last = mm(dst[i][:, :], w[:, kt, r * P:(r + 1) * P], xt[s][:, kt, a, :],
                                      start=(n == 0), stop=(n == 2 * KT - 1))
                            n += 1
                    last.then_inc(done, 1)

            def down(c):
                for half, dst in enumerate((py, po)):
                    pe.wait_ge(f_ev, c[2] + half + 1 - 2)
                    if half == 0:
                        pe.wait_ge(f_hl, c[FT] + FT)
                    for jj in range(2):
                        j = 2 * half + jj
                        n = 0
                        for r in range(FT):
                            for a in range(2):
                                last = mm(dst[:, jj * D:(jj + 1) * D], hpart(r, a)[:, j * P:(j + 1) * P], wdt[:, r, :],
                                          start=(n == 0), stop=(n == 2 * FT - 1))
                                n += 1
                    last.then_inc(f_dn, 1)

            def f_body(b, s, nxt):
                c = counts(pe, b, (FT, 2, 1))
                for r in range(FT):
                    gate_up(c, s, r)
                if nxt:
                    f_transposes({p: v + p for p, v in c.items()}, 1 - s)
                down(c)

            f_transposes(counts(pe, 0, (FT, 2, 1)), 0)
            with pe.Fori(0, B // 2 - 1) as i:
                f_body(pe.snap(i * 2), 0, True)
                f_body(pe.snap(i * 2 + 1), 1, True)
            f_body(B - 2, 0, True)
            f_body(B - 1, 1, False)

        @block.scalar
        def _(act):
            credit(act, (pa_act, 6), (v_act, 2), (ln_act, 8), (ex_act, 8), (pt_act, 8), (yh_act, 2), (x_hi, 2))
            n_act = [0]

            def a_step(ins):
                n_act[0] += 1
                ins.then_inc(p_act, 1)
                act.wait_ge(p_act, n_act[0])

            act.wait_ge(p_load, 16 * 10)
            a_step(act.activation(hp[:, 6:11], hp[:, 0:5], ACT.Abs))
            a_step(act.activation(hp[:, 11:16], hp[:, 6:11], ACT.Exp, scale=-1.0))
            a_step(act.activation(hp[:, 16:21], hp[:, 11:16], ACT.Ln, bias=1.0))
            act.wait_ge(p_dve, V_EXP)
            a_step(act.activation(v_e, v_e, ACT.Exp))
            act.wait_ge(p_dve, V_LN)
            a_step(act.activation(v_lnv, v_v, ACT.Ln))
            a_step(act.activation(v_t3, v_vn, ACT.Ln))
            for k in range(4):
                act.wait_ge(p_dve, V_ANGLE[k])
                a_step(act.activation(rope_sp[k], ang, ACT.Sin))
                a_step(act.activation(half_sin, ang, ACT.Sin, scale=0.5))
            for m in range(4):
                for s in range(4):
                    i = 4 * m + s
                    if s == 0:
                        act.wait_ge(raww[m % 2], (16, 16, 32, 48)[m])
                    if i >= 2:
                        act.wait_ge(split_out[i % 2], 16 * (i // 2))
                    for hi, lo, raw in split_views(m, s):
                        last = act.activation(hi, raw, ACT.Copy)
                    last.then_inc(split_hi, 1)
            jobs = ffn_jobs()
            for n in range(9):
                act.wait_ge(ffn_tr, n + 1)
                act.activation(jobs[4 * n][1], ps[n % 2][:, :], ACT.Copy).then_inc(ffn_ev, 1)
            with act.Fori(0, B // 2) as i:
                c16 = act.snap(i * 16 + 16)
                for s in range(2):
                    c = act.snap(i * 4 + 2 * s + 2)
                    for kt in range(KT):
                        act.wait_ge(x_tr, c + kt + 1)
                        if kt == 0:
                            act.wait_ge(x_out[s], c16)
                        act.activation(xt[s][:, kt, 0, :], pp[kt][:, :], ACT.Copy).then_inc(x_hi, 1)

            def swap(c, hh, m):
                act.wait_ge(proj, c[8] + 4 * hh + 1 + m)
                act.wait_ge(t2_pool, c[4] + 2 * hh + m + 1 - 2)
                act.activation(sq[:, m, :], pa[m][:, :], ACT.Square)
                scale = -2.0 if m == 0 else 1.0
                act.activation(swt[0:DH, m, :], pa[m][DH:P, :], ACT.Copy, scale=scale)
                act.activation(swt[DH:P, m, :], pa[m][0:DH, :], ACT.Copy, scale=scale).then_inc(pa_act, 1)

            def keep_norm_k(c, hh):
                act.wait_ge(proj, c[8] + 4 * hh + 3)
                act.wait_ge(ek_pool, c[8] + 4 * hh + 4 - 8)
                act.activation(qkb[:, 3 * hh + 2, :], pa[0][:, :], ACT.Copy).then_inc(pa_act, 1)

            def keep_values(c, half):
                act.wait_ge(v_rdy, c[2] + 1 + half)
                if half == 0:
                    act.wait_ge(av_rdy, c[8])
                act.activation(vt[:, 2 * half:2 * half + 2, :].rearrange("p a n -> p (a n)"), pp[half][:, :],
                               ACT.Copy).then_inc(v_act, 1)

            def log(c, hh, n):
                m = 4 * hh + n
                act.wait_ge(cd_dve, c[8] + m + 1)
                act.activation(lg[:, hh, at(n)], lg[:, hh, at(n)], ACT.Ln,
                               bias=qn[:, hh, 0, TILES[n]:TILES[n] + 1]).then_inc(ln_act, 1)

            def exp(c, hh, n):
                m, q = 4 * hh + n, NT * hh + TILES[n]
                act.wait_ge(f_dve, c[8] + m + 1)
                act.wait_ge(tr_rdy, c[8] + m + 1 - 8)
                act.activation(pr[:, hh, at(n)], lg[:, hh, at(n)], ACT.Exp, bias=nmax[:, q:q + 1], scale=-1.0,
                               accum_out=den[:, q:q + 1]).then_inc(ex_act, 1)

            def keep_turned(c, hh, n):
                i, m = n % 2, 4 * hh + n
                w = width(n)
                act.wait_ge(tr_rdy, c[8] + m + 1)
                act.wait_ge(av_rdy, c[8] + m + 1 - 2)
                act.activation(pt[:, i, 0:w], pp[i][:, 0:w], ACT.Copy).then_inc(pt_act, 1)

            def y_high(c, hh):
                act.wait_ge(yt_rdy, c[2] + hh + 1)
                if hh == 0:
                    act.wait_ge(o_rdy, c[2] + 2 - 2)
                act.activation(yhl[:, hh, 0, :], po[:, :], ACT.Copy).then_inc(yh_act, 1)

            PERS = (8, 6, 4, 2)

            def body(it):
                c = counts(act, it.t, PERS)
                cp, cn = previous(c), following(c)
                old, nxt = it.before is not None, it.behind is not None
                if old:
                    keep_turned(cp, 0, 0)
                    keep_turned(cp, 0, 1)
                swap(c, 1, 0)
                swap(c, 1, 1)
                if old:
                    keep_turned(cp, 0, 2)
                    exp(cp, 1, 0)
                    keep_turned(cp, 0, 3)
                    exp(cp, 1, 1)
                    exp(cp, 1, 2)
                keep_norm_k(c, 1)
                if old:
                    keep_turned(cp, 1, 0)
                    exp(cp, 1, 3)
                    keep_turned(cp, 1, 1)
                log(c, 0, 0)
                log(c, 0, 1)
                log(c, 0, 2)
                if old:
                    keep_turned(cp, 1, 2)
                if nxt:
                    swap(cn, 0, 0)
                if old:
                    y_high(cp, 0)
                log(c, 0, 3)
                if old:
                    keep_turned(cp, 1, 3)
                exp(c, 0, 0)
                if nxt:
                    swap(cn, 0, 1)
                if old:
                    y_high(cp, 1)
                exp(c, 0, 1)
                exp(c, 0, 2)
                keep_values(c, 0)
                keep_values(c, 1)
                log(c, 1, 0)
                if nxt:
                    keep_norm_k(cn, 0)
                log(c, 1, 1)
                log(c, 1, 2)
                log(c, 1, 3)
                exp(c, 0, 3)

            c0 = counts(act, 0, PERS)
            swap(c0, 0, 0)
            swap(c0, 0, 1)
            keep_norm_k(c0, 0)
            run_iterations(act, body)
            c = counts(act, G * B - 1, PERS)
            for n in range(NT):
                exp(c, 1, n)
            for hh in range(HH):
                for n in range(NT):
                    keep_turned(c, hh, n)
                y_high(c, hh)

            credit(act, (f_hi, 2), (f_silu, FT), (f_hh, FT), (f_ev, 2))

            def f_high(c, s):
                for kt in range(KT):
                    act.wait_ge(f_tr, c[2] + kt + 1)
                    if kt == 0:
                        act.wait_ge(f_u, c[FT])
                    act.activation(xt[s][:, kt, 0, :], pp[kt][:, :], ACT.Copy).then_inc(f_hi, 1)

            def silu(c, r):
                act.wait_ge(f_g, c[FT] + r + 1)
                act.wait_ge(f_h, c[FT] + r + 1 - 2)
                act.activation(f_gate(r), pa[r % 2][:, :], ACT.Silu, scale=SCALE).then_inc(f_silu, 1)

            def hidden_high(c, r):
                act.wait_ge(f_h, c[FT] + r + 1)
                if r == 0:
                    act.wait_ge(f_dn, c[2] + 2 - 2)
                act.activation(hpart(r, 0), f_hid(r), ACT.Copy).then_inc(f_hh, 1)

            def f_body(b, s, nxt):
                c = counts(act, b, (FT, 2, 1))
                silu(c, 0)
                for r in range(1, FT):
                    silu(c, r)
                    hidden_high(c, r - 1)
                hidden_high(c, FT - 1)
                if nxt:
                    f_high({p: v + p for p, v in c.items()}, 1 - s)
                for half, src in enumerate((py, po)):
                    act.wait_ge(f_dn, c[2] + half + 1)
                    act.wait_ge(f_res, c[1] + 1)
                    act.activation(f_y[:, 2 * half:2 * half + 2, :], src[:, :].rearrange("p (j n) -> p j n", j=2),
                                   ACT.Copy, scale=SCALE).then_inc(f_ev, 1)

            act.preload_act_table(ACT.Silu)
            f_high(counts(act, 0, (FT, 2)), 0)
            with act.Fori(0, B // 2 - 1) as i:
                f_body(act.snap(i * 2), 0, True)
                f_body(act.snap(i * 2 + 1), 1, True)
            f_body(B - 2, 0, True)
            f_body(B - 1, 1, False)

        @block.vector
        def _(dve):
            credit(dve, (pa_dve, 6), (rope, 4), (a_dve, 8), (b_dve, 8 - 2 * NPB), (cd_dve, 8), (f_dve, 8), (rd_dve, 2),
                   (y_dve, 2), (yl_dve, 2), (acc_dve, 2), (x_norm, 2), (x_lo, 2), (x_ln, 3))
            tt, ts, stt, rec = dve.tensor_tensor, dve.tensor_scalar, dve.scalar_tensor_tensor, dve.reciprocal
            done = [0]

            def step(ins):
                done[0] += 1
                ins.then_inc(p_dve, 1)
                dve.wait_ge(p_dve, done[0])

            def settle(v):
                if not isinstance(v, int):
                    dve.sem_inc(settled, 1)

            def col(k, n=1):
                return hp[:, k:k + n]
            MU, TAU, E0 = 0, 5, 11
            SP, NMU, C1, C2, RL, RB = 26, 36, 37, 38, 23, 24
            dve.wait_ge(p_load, 16 * 10)
            dve.wait_ge(p_act, 3)
            step(ts(col(21, 5), col(0, 5), 0.0, None, ALU.max))
            step(tt(col(SP, 5), col(21, 5), col(16, 5), ALU.add))
            step(ts(col(31), col(MU), 0.0, None, ALU.is_ge))
            step(tt(col(32), col(31), col(E0), ALU.max))
            step(ts(col(33), col(E0), 1.0, None, ALU.add))
            step(rec(col(34), col(33)))
            step(stt(col(35), col(32), 1.0, col(34), ALU.mult, ALU.mult))
            step(ts(col(35), col(35), EPS_MU, None, ALU.add))
            step(ts(col(NMU), col(35), -1.0, None, ALU.mult))
            step(ts(col(39), col(35), 2.0, None, ALU.mult))
            step(rec(col(39), col(39)))
            step(tt(col(C1), col(SP + 1), col(39), ALU.mult))
            step(tt(col(C2), col(SP + 2), col(SP + 3), ALU.add))
            step(ts(col(21), col(SP + 4), float(DH), -0.5, ALU.add, ALU.mult))
            dve.wait_ge(consts, 5)
            step(ts(v_e, dist, 0.0, None, ALU.max))
            step(ts(v_e, v_e, col(NMU), MIN_EXP, ALU.mult, ALU.max))
            step(ts(v_e, v_e, 0.0, None, ALU.min))
            dve.wait_ge(p_act, 4)
            step(tt(v_v, v_e, v_e, ALU.mult))
            step(ts(v_v, v_v, -1.0, 1.0, ALU.mult, ALU.add))
            step(ts(v_v, v_v, col(C1), col(C2), ALU.mult, ALU.add))
            step(ts(v_vn, v_v, col(SP + 4), None, ALU.mult))
            step(tt(col(22), col(21), col(TAU), ALU.mult))
            step(ts(col(21), col(22), 0.0, 1e-20, ALU.is_equal, ALU.mult))
            step(tt(col(22), col(22), col(21), ALU.add))
            step(rec(col(25), col(22)))
            step(ts(col(NCO), col(22), -1.0, None, ALU.mult))
            step(ts(col(RL), col(25), -0.5 * DH, None, ALU.mult))
            step(ts(col(RB), col(25), -BIG, None, ALU.mult))
            dve.wait_ge(p_act, 6)
            step(stt(v_t3, v_lnv, col(RL), v_t3, ALU.mult, ALU.subtract))
            step(ts(v_t3[:, N:VEC], v_t3[:, N:VEC], col(RB), None, ALU.add))
            assert done[0] == V_TABLES, done
            TWO_PI = (6.28125, 1.9350051879882812e-3, 3.0199159819567529e-7)
            for k in range(4):
                step(ts(ang, tokens, om[:, k:k + 1], None, ALU.mult))
                step(ts(turns, ang, 1.0 / (2 * math.pi), MAGIC, ALU.mult, ALU.add))
                step(ts(turns, turns, MAGIC, None, ALU.subtract))
                for c in TWO_PI:
                    step(stt(ang, turns, -c, ang, ALU.mult, ALU.add))
                step(ts(ang, ang, 3.1415925, -3.1415925, ALU.min, ALU.max))
                dve.wait_ge(p_act, 8 + 2 * k)
                step(ts(rope_sn[k], rope_sp[k], -1.0, None, ALU.mult))
                step(tt(half_sin, half_sin, half_sin, ALU.mult))
                step(ts(rope_cs[k], half_sin, -2.0, 1.0, ALU.mult, ALU.add))
                assert done[0] == V_ROPE[k]
            dve.wait_ge(ffn_in, 48)
            for z in (qkb[:, 0:3, :], qkb[:, 3:6, :], swt[:, 0:3, :]):
                dve.tensor_copy(z, z.bitcast(I32)).then_inc(ffn_cast, 1)
            for m in range(4):
                for s in range(4):
                    dve.wait_ge(split_hi, 4 * m + s + 1)
                    for hi, lo, raw in split_views(m, s):
                        last = tt(lo, raw, hi.bitcast(F32), ALU.subtract)
                    last.then_inc(split_lo, 1)

            def norm(src, dst, chain, c, k, made, v, mark):
                for j in range(NT):
                    last = dve.bn_stats(stats[:, j, :], src(j))
                last.then_inc(chain, 1)
                dve.wait_ge(chain, c + k + 1)
                settle(c)
                for j in range(NT):
                    last = dve.bn_aggr(mv[:, j, :], stats[:, j, :])
                last.then_inc(chain, 1)
                dve.wait_ge(chain, c + k + 2)
                ts(rstd[:, :], mv[:, :, 1], EPS_LN, None, ALU.add).then_inc(chain, 1)
                dve.wait_ge(made, v)
                for j in range(NT):
                    last = ts(dst(j), src(j), mv[:, j, 0:1], rstd[:, j:j + 1], ALU.subtract, ALU.mult)
                last.then_inc(mark, 1)

            with dve.Fori(0, B // 2) as i:
                i16 = dve.snap(i * 16 + 16)
                for s in range(2):
                    c3 = dve.snap(i * 6 + 3 * s + 3)
                    c1 = dve.snap(i * 2 + s + 2)
                    c2 = dve.snap(i * 4 + 2 * s + 2)
                    dve.wait_ge(x_in[s], i16)
                    dve.wait_ge(x_tr, c2)
                    norm(lambda j: xraw[s][:, j, :], lambda j: xnorm[s][:, j, :], x_ln, c3, 0, x_root, c1, x_norm)
                    for kt in range(KT):
                        dve.wait_ge(x_hi, c2 + kt + 1)
                        tt(xt[s][:, kt, 1, :], pp[kt][:, :], xt[s][:, kt, 0, :].bitcast(F32), ALU.subtract).then_inc(x_lo, 1)

            def rotate(c, hh, par, m):
                dve.wait_ge(pa_act, c[6] + 3 * hh + 1 + m)
                dst = qkb[:, 3 * hh + m, :]
                if m == 0:
                    stt(dst, pa[0][:, :], -2.0, ropet(par, hh, 0), ALU.mult, ALU.mult).then_inc(pa_dve, 1)
                else:
                    tt(dst, pa[1][:, :], ropet(par, hh, 0), ALU.mult).then_inc(pa_dve, 1)

            def rotated(c, hh, m):
                dst = qkb[:, 3 * hh + m, :]
                dve.wait_ge(pa_dve, c[6] + 3 * hh + m + 1)
                dve.wait_ge(t2_pool, c[4] + 2 * hh + m + 1)
                tt(dst, dst, swt[:, 2 + m, :], ALU.add).then_inc(rope, 1)

            def keep_norm_q(c, hh):
                dve.wait_ge(proj, c[8] + 4 * hh + 4)
                dve.tensor_copy(qn[:, hh, 0, :], pa[1][:, 0:NT])
                ts(qn[:, hh, 1, :], pa[1][:, 0:NT], -1.0, None, ALU.mult).then_inc(pa_dve, 1)

            def distance_a(c, hh, n):
                i, m, w = n % 2, 4 * hh + n, width(n)
                dve.wait_ge(s_rdy, c[8] + m + 1)
                dve.wait_ge(ek_pool, c[8] + m + 1)
                dve.wait_ge(ex_act, c[8] + m + 1 - 8)
                tt(lg[:, hh, at(n)], ps[i][:, 0:w], ek[:, i, 0:w], ALU.add).then_inc(a_dve, 1)

            def distance_b(c, hh, n, par):
                if n in POOL_SCALES:
                    return
                m, w = 4 * hh + n, width(n)
                dve.wait_ge(a_dve, c[8] + m + 1)
                tt(lg[:, hh, at(n)], lg[:, hh, at(n)], tab(par, hh, E_T, N - w), ALU.mult).then_inc(b_dve, 1)

            def distance_c(c, hh, n, par):
                w = width(n)
                before = sum(1 for q in POOL_SCALES if q <= n)
                if n in POOL_SCALES:
                    dve.wait_ge(b_pool, c[2] * NPB + NPB * hh + before)
                else:
                    dve.wait_ge(b_dve, c[2] * (4 - NPB) + (4 - NPB) * hh + n + 1 - before)
                stt(lg[:, hh, at(n)], lg[:, hh, at(n)], qn[:, hh, 1, TILES[n]:TILES[n] + 1], tab(par, hh, VN_T, N - w),
                    ALU.max, ALU.add).then_inc(cd_dve, 1)

            def logits(c, hh, n, par):
                m, w, q = 4 * hh + n, width(n), NT * hh + TILES[n]
                dve.wait_ge(ln_act, c[8] + m + 1)
                settle(c[8])
                dve.tensor_tensor_reduce(lg[:, hh, at(n)], lg[:, hh, at(n)], tab(par, hh, T3_T, N - w), ncog[:, par, hh:hh + 1],
                                         3e38, ALU.add, ALU.min, nmax[:, q:q + 1]).then_inc(f_dve, 1)

            def keep_y(c, hh):
                dve.wait_ge(ex_act, c[8] + 4 * hh + 4)
                rec(rden[:, NT * hh:NT * hh + NT], den[:, NT * hh:NT * hh + NT]).then_inc(rd_dve, 1)
                dve.wait_ge(rd_dve, c[2] + hh + 1)
                dve.wait_ge(av_rdy, c[8] + 4 * hh + 4)
                dve.wait_ge(yt_rdy, c[2] + hh + 1 - 1)
                tt(ysb[:, :, :], py[:, :].rearrange("p (j n) -> p j n", j=NT),
                   rden[:, NT * hh:NT * hh + NT].unsqueeze(2).broadcast_to([P, NT, P]), ALU.mult).then_inc(y_dve, 1)

            def y_low(c, hh):
                dve.wait_ge(yh_act, c[2] + hh + 1)
                tt(yhl[:, hh, 1, :], po[:, :], yhl[:, hh, 0, :].bitcast(F32), ALU.subtract).then_inc(yl_dve, 1)

            def add_output(c, b, half):
                dve.wait_ge(o_rdy, c[2] + half + 1)
                if isinstance(b, int):
                    dst = accf[:, b * NT * D + half * N:b * NT * D + half * N + N]
                else:
                    dst = accf[:, bass.ds(b * (NT * D) + half * N, N)]
                tt(dst, dst, (po, py)[half][:, :], ALU.add).then_inc(acc_dve, 1)

            PERS = (8, 6, 4, 2)

            def body(it):
                c = counts(dve, it.t, PERS)
                cp, cn = previous(c), following(c)
                old = it.before is not None
                if it.new is not None:
                    start(it.new, it.par)
                nxt = it.behind is not None
                distance_a(c, 0, 0)
                distance_a(c, 0, 1)
                rotate(c, 1, it.par, 0)
                rotate(c, 1, it.par, 1)
                distance_b(c, 0, 1, it.par)
                rotated(c, 1, 0)
                distance_a(c, 0, 2)
                if old:
                    keep_y(cp, 0)
                distance_c(c, 0, 0, it.par)
                distance_c(c, 0, 1, it.par)
                distance_b(c, 0, 2, it.par)
                distance_c(c, 0, 2, it.par)
                distance_a(c, 0, 3)
                logits(c, 0, 0, it.par)
                rotated(c, 1, 1)
                distance_b(c, 0, 3, it.par)
                keep_norm_q(c, 1)
                distance_c(c, 0, 3, it.par)
                logits(c, 0, 1, it.par)
                distance_a(c, 1, 0)
                if it.opens is not None:
                    dve.wait_ge(grp[it.behind], it.opens)
                if nxt:
                    rotate(cn, 0, it.behind, 0)
                if old:
                    keep_y(cp, 1)
                    y_low(cp, 0)
                logits(c, 0, 2, it.par)
                distance_c(c, 1, 0, it.par)
                distance_a(c, 1, 1)
                distance_a(c, 1, 2)
                if old:
                    y_low(cp, 1)
                distance_b(c, 1, 1, it.par)
                distance_b(c, 1, 2, it.par)
                logits(c, 0, 3, it.par)
                distance_a(c, 1, 3)
                distance_c(c, 1, 1, it.par)
                distance_c(c, 1, 2, it.par)
                if nxt:
                    rotate(cn, 0, it.behind, 1)
                distance_b(c, 1, 3, it.par)
                if old:
                    add_output(cp, it.b_before, 0)
                distance_c(c, 1, 3, it.par)
                if nxt:
                    rotated(cn, 0, 0)
                logits(c, 1, 0, it.par)
                if nxt:
                    keep_norm_q(cn, 0)
                    rotated(cn, 0, 1)
                logits(c, 1, 1, it.par)
                if old:
                    add_output(cp, it.b_before, 1)
                logits(c, 1, 2, it.par)
                logits(c, 1, 3, it.par)

            def start(g, par):
                if isinstance(g, int):
                    src, v = nco[:, g * HH:(g + 1) * HH], g + 1
                else:
                    src, v = nco[:, bass.ds(g * HH, HH)], dve.snap(g + 1)
                dve.tensor_copy(ncog[:, par, :], src).then_inc(ncog_dve, 1)
                dve.wait_ge(ncog_dve, v)
                settle(v)

            dve.wait_ge(nco_in, 16)
            dve.wait_ge(consts, 7)
            dve.wait_ge(grp[0], 64)
            c0 = counts(dve, 0, PERS)
            rotate(c0, 0, 0, 0)
            rotated(c0, 0, 0)
            rotate(c0, 0, 0, 1)
            rotated(c0, 0, 1)
            keep_norm_q(c0, 0)
            run_iterations(dve, body)
            c = counts(dve, G * B - 1, PERS)
            for hh in range(HH):
                keep_y(c, hh)
                y_low(c, hh)
            add_output(c, B - 1, 0)
            add_output(c, B - 1, 1)

            credit(dve, (f_norm, 2), (f_lo, 2), (f_h, FT), (f_res, 2), (f_ln, 8), (f_l3, 4))

            def acc_of(b, j0=0, n=NT):
                if isinstance(b, int):
                    return accf[:, (b * NT + j0) * D:(b * NT + j0 + n) * D]
                return accf[:, bass.ds(b * (NT * D) + j0 * D, n * D)]

            def front(b, c, s, xv):
                def part0():
                    dve.wait_ge(f_x[s], xv)
                    settle(c[2])
                    norm(lambda j: acc_of(b, j, 1), lambda j: f_tmp[:, j, :], f_ln, c[8], 0, f_root, c[2] + 1, f_ln)

                def part1():
                    dve.wait_ge(f_ln, c[8] + 4)
                    tt(acc_of(b), f_tmp.rearrange("p j n -> p (j n)"), f_xin[s].rearrange("p j n -> p (j n)"),
                       ALU.add).then_inc(f_ln, 1)
                    dve.wait_ge(f_ln, c[8] + 5)

                def part2():
                    dve.wait_ge(f_tr, c[2])
                    settle(xv)
                    norm(lambda j: acc_of(b, j, 1), lambda j: f_nrm[:, j, :], f_ln, c[8], 5, f_root, c[2] + 2, f_norm)
                return [part0, part1, part2]

            def split_low(c, s):
                for kt in range(KT):
                    dve.wait_ge(f_hi, c[2] + kt + 1)
                    tt(xt[s][:, kt, 1, :], pp[kt][:, :], xt[s][:, kt, 0, :].bitcast(F32), ALU.subtract).then_inc(f_lo, 1)

            def hidden(c, r):
                dve.wait_ge(f_silu, c[FT] + r + 1)
                dve.wait_ge(f_u, c[FT] + r + 1)
                dve.wait_ge(f_hl, c[FT] + r + 1 - 2)
                dve.wait_ge(f_hh, c[FT] + r + 1 - 2)
                stt(f_hid(r), ps[r % 2][:, :], SCALE, f_gate(r), ALU.mult, ALU.mult).then_inc(f_h, 1)

            def back(b, c, s, ov):
                dve.wait_ge(f_ev, c[2] + 2)
                norm(lambda j: f_y[:, j, :], lambda j: f_tmp[:, j, :], f_l3, c[4], 0, f_rootb, c[1] + 1, f_l3)
                dve.wait_ge(f_l3, c[4] + 4)
                dve.wait_ge(f_out[s], ov)
                tt(f_outs[s].rearrange("p j n -> p (j n)"), f_tmp.rearrange("p j n -> p (j n)"), acc_of(b),
                   ALU.add).then_inc(f_res, 1)

            FP = (FT, 8, 4, 2, 1)

            def f_body(b, s, i, nxt):
                c = counts(dve, b, FP)
                parts = [None] * 3
                if nxt:
                    cn = {p: v + p for p, v in c.items()}
                    xv = (i + (2 if s else 1)) * 16
                    parts = front(b + 1 if isinstance(b, int) else dve.snap(b + 1), cn, 1 - s,
                                  xv if isinstance(xv, int) else dve.snap(xv))
                for r in range(FT):
                    hidden(c, r)
                    if nxt and r < 3:
                        parts[r]()
                if nxt:
                    split_low(cn, 1 - s)
                ov = (i + 1) * 16
                back(b, c, s, ov if isinstance(ov, int) else dve.snap(ov))

            c0 = counts(dve, 0, FP)
            for part in front(0, c0, 0, 16):
                part()
            split_low(c0, 0)
            with dve.Fori(0, B // 2 - 1) as i:
                f_body(dve.snap(i * 2), 0, i, True)
                f_body(dve.snap(i * 2 + 1), 1, i, True)
            f_body(B - 2, 0, B // 2 - 1, True)
            f_body(B - 1, 1, B // 2 - 1, False)


_INS = ['L0_attn_x', 'L0_attn_Wq', 'L0_attn_Wk', 'L0_attn_Wv', 'L0_attn_Wo', 'L0_attn_omega', 'L0_attn_mu_raw',
        'L0_attn_sigma_raw', 'L0_attn_eta_raw', 'L0_attn_gamma_raw', 'L0_attn_nu_raw', 'L0_attn_tau',
        'L0_ffn_w_gate', 'L0_ffn_w_up', 'L0_ffn_w_down']


def kernel(**inputs):
    import concourse.bacc as _bacc
    from concourse.bass_utils import run_bass_kernel_spmd as _run

    nc = _bacc.Bacc("TRN2", target_bir_lowering=False, num_devices=1)
    arrays, args = {}, []
    for name in _INS:
        a = np.ascontiguousarray(inputs[name])
        arrays[f"in_{name}"] = a
        args.append(nc.dram_tensor(f"in_{name}", a.shape, mybir.dt.from_np(a.dtype), kind="ExternalInput").ap())
    out = nc.dram_tensor("out", (B, N, D), F32, kind="ExternalOutput").ap()
    build(nc, *args[0:6], args[6:11], *args[11:15], out)
    r = _run(nc, [arrays], core_ids=[0])
    return r.results[0]["out"]
```
